# Optimizing a Trainium2 kernel written in Bass

```python
import numpy as np
import jax
import jax.numpy as jnp

def _softmax(x, axis=-1):
    return jax.nn.softmax(x, axis=axis)

def _gelu(x):
    return jax.nn.gelu(x, approximate=True)

def _silu(x):
    return jax.nn.silu(x)

def _sigmoid(x):
    return jax.nn.sigmoid(x)

def _layernorm(x, axis=-1, eps=1e-05):
    m = jnp.mean(x, axis=axis, keepdims=True)
    v = jnp.var(x, axis=axis, keepdims=True)
    return (x - m) / jnp.sqrt(v + eps)

def _scatter_add(tgt, idx, src, axis=0):
    return tgt.at[idx].add(src)

def _segment_sum(src, seg, n):
    return jax.ops.segment_sum(src, seg, n)
kernel_name = 'mk_gnn_resnorm_d2_gnn_r8_9d0e0e'

def setup_inputs(seed: int=0):
    np.random.seed(seed)
    _w = jnp.asarray

    def _rec_inputs():
        import jax
        import jax.numpy as jnp
        _gk = jax.random.key(seed)
        x = -0.000202 + 1 * jax.random.normal(jax.random.fold_in(_gk, 1), (12500, 128), jnp.float32)
        src = jax.random.randint(jax.random.fold_in(_gk, 2), (200000,), 0, 12500, jnp.int32)
        dst = jax.random.randint(jax.random.fold_in(_gk, 3), (200000,), 0, 12500, jnp.int32)
        _o = jnp.argsort(dst, stable=True)
        src = src[_o]
        dst = dst[_o]
        edge_weight = jax.random.uniform(jax.random.fold_in(_gk, 12), (200000,), jnp.float32, 0.0, 0.999998)
        return (x, src, dst, edge_weight)
    x, src, dst, edge_weight = _rec_inputs()

    def _L0_gnn_setup():
        import jax, jax.numpy as jnp
        import numpy as np
        N = 6250
        E = 80000
        F_DIM = 128
        H = 128
        OUT = 128
        NUM_OBS = 4
        V_MAX = 0.9
        BN_EPS = 1e-05
        LN_EPS = 1e-05
        key = jax.random.key(seed)
        ks = jax.random.split(key, 12)
        x = jax.random.normal(ks[0], (N, F_DIM), dtype=jnp.float32)
        edge_index = jax.random.randint(ks[1], (2, E), 0, N, dtype=jnp.int64)

        def xavier(k, fan_in, fan_out):
            lim = np.sqrt(6.0 / (fan_in + fan_out)).astype(np.float32)
            return jax.random.uniform(k, (fan_in, fan_out), jnp.float32, -lim, lim)
        return {'x': x, 'edge_index': edge_index, 'W_ft': xavier(ks[2], F_DIM, H), 'b_ft': jnp.zeros((H,), jnp.float32), 'W_conv': xavier(ks[3], H, H), 'b_conv': jnp.zeros((H,), jnp.float32), 'velocity_factor': jnp.float32(0.5), 'velocity_params': jnp.linspace(V_MAX / NUM_OBS, V_MAX, NUM_OBS, dtype=jnp.float32), 'attention': jnp.ones((NUM_OBS, H), jnp.float32) / NUM_OBS, 'bn_scale': jnp.ones((NUM_OBS, H), jnp.float32), 'bn_bias': jnp.zeros((NUM_OBS, H), jnp.float32), 'W1': xavier(ks[4], NUM_OBS * H, 2 * H), 'b1': jnp.zeros((2 * H,), jnp.float32), 'ln_scale': jnp.ones((2 * H,), jnp.float32), 'ln_bias': jnp.zeros((2 * H,), jnp.float32), 'W2': xavier(ks[5], 2 * H, OUT), 'b2': jnp.zeros((OUT,), jnp.float32)}
    _L0_gnn_all = _L0_gnn_setup()
    _L0_gnn_in = {k: v for k, v in _L0_gnn_all.items() if k in ('W_ft', 'b_ft', 'W_conv', 'b_conv', 'velocity_factor', 'velocity_params', 'attention', 'bn_scale', 'bn_bias', 'W1', 'b1', 'ln_scale', 'ln_bias', 'W2', 'b2')}
    del _L0_gnn_all

    def _L1_gnn_setup():
        import jax, jax.numpy as jnp
        import numpy as np
        N_NODE = 12500
        N_EDGE = 200000
        D_IN = 128
        D_OUT = 128
        key = jax.random.key(seed)
        k1, k2, k3, k4, k5 = jax.random.split(key, 5)
        x = jax.random.normal(k1, (N_NODE, D_IN), dtype=jnp.float32)
        lim = 1.0 / np.sqrt(D_IN)
        W = jax.random.uniform(k2, (D_OUT, D_IN), dtype=jnp.float32, minval=-lim, maxval=lim)
        b = jax.random.uniform(k3, (D_OUT,), dtype=jnp.float32, minval=-lim, maxval=lim)
        edge_index = jax.random.randint(k4, (2, N_EDGE), 0, N_NODE, dtype=jnp.int64)
        edge_weight = jax.random.uniform(k5, (N_EDGE,), dtype=jnp.float32)
        return {'x': x, 'W': W, 'b': b, 'edge_index': edge_index, 'edge_weight': edge_weight}
    _L1_gnn_all = _L1_gnn_setup()
    _L1_gnn_in = {k: v for k, v in _L1_gnn_all.items() if k in ('W', 'b')}
    del _L1_gnn_all
    return {'x': x, 'src': src, 'dst': dst, 'edge_weight': edge_weight, 'L0_gnn_W_ft': _L0_gnn_in['W_ft'], 'L0_gnn_b_ft': _L0_gnn_in['b_ft'], 'L0_gnn_W_conv': _L0_gnn_in['W_conv'], 'L0_gnn_b_conv': _L0_gnn_in['b_conv'], 'L0_gnn_velocity_factor': _L0_gnn_in['velocity_factor'], 'L0_gnn_velocity_params': _L0_gnn_in['velocity_params'], 'L0_gnn_attention': _L0_gnn_in['attention'], 'L0_gnn_bn_scale': _L0_gnn_in['bn_scale'], 'L0_gnn_bn_bias': _L0_gnn_in['bn_bias'], 'L0_gnn_W1': _L0_gnn_in['W1'], 'L0_gnn_b1': _L0_gnn_in['b1'], 'L0_gnn_ln_scale': _L0_gnn_in['ln_scale'], 'L0_gnn_ln_bias': _L0_gnn_in['ln_bias'], 'L0_gnn_W2': _L0_gnn_in['W2'], 'L0_gnn_b2': _L0_gnn_in['b2'], 'L1_gnn_W': _L1_gnn_in['W'], 'L1_gnn_b': _L1_gnn_in['b']}

def reference(x, src, dst, edge_weight, L0_gnn_W_ft, L0_gnn_b_ft, L0_gnn_W_conv, L0_gnn_b_conv, L0_gnn_velocity_factor, L0_gnn_velocity_params, L0_gnn_attention, L0_gnn_bn_scale, L0_gnn_bn_bias, L0_gnn_W1, L0_gnn_b1, L0_gnn_ln_scale, L0_gnn_ln_bias, L0_gnn_W2, L0_gnn_b2, L1_gnn_W, L1_gnn_b):
    import jax
    import jax.numpy as jnp

    def _L0_gnn_ref(x, edge_index, W_ft, b_ft, W_conv, b_conv, velocity_factor, velocity_params, attention, bn_scale, bn_bias, W1, b1, ln_scale, ln_bias, W2, b2):
        import jax, jax.numpy as jnp
        import numpy as np
        N = 6250
        E = 80000
        F_DIM = 128
        H = 128
        OUT = 128
        NUM_OBS = 4
        V_MAX = 0.9
        BN_EPS = 1e-05
        LN_EPS = 1e-05
        n_nodes = x.shape[0]
        h = jax.nn.relu(x @ W_ft + b_ft)
        pos = h[:, :3]
        src = edge_index[0]
        dst = edge_index[1]
        dpos = pos[src] - pos[dst]
        dist = jnp.linalg.norm(dpos, axis=1, keepdims=True)
        dist_norm = dist / jnp.max(dist)
        direction = dpos / (dist + 1e-08)
        dir_sum = jnp.sum(direction, axis=1, keepdims=True)
        transformed = h[src] @ W_conv + b_conv
        v_obs = jax.lax.stop_gradient(velocity_params)
        views = []
        for i in range(NUM_OBS):
            v_rel = velocity_factor * jnp.minimum(dist_norm, v_obs[i])
            gamma = 1.0 / jnp.sqrt(1.0 - v_rel * v_rel)
            aberr = 1.0 / (gamma * (1.0 + v_rel * dir_sum))
            msgs = transformed * aberr
            agg = jax.ops.segment_sum(msgs, dst, num_segments=n_nodes)
            mean = jnp.mean(agg, axis=0)
            var = jnp.var(agg, axis=0)
            bn = (agg - mean) / jnp.sqrt(var + BN_EPS) * bn_scale[i] + bn_bias[i]
            view = jax.nn.relu(bn) * jax.nn.softmax(attention[i])[None, :]
            views.append(view)
        combined = jnp.concatenate(views, axis=1)
        z = combined @ W1 + b1
        mu = jnp.mean(z, axis=-1, keepdims=True)
        sig = jnp.var(z, axis=-1, keepdims=True)
        z = (z - mu) / jnp.sqrt(sig + LN_EPS) * ln_scale + ln_bias
        z = jax.nn.relu(z)
        return z @ W2 + b2

    def _L1_gnn_ref(x, W, b, edge_index, edge_weight):
        import jax, jax.numpy as jnp
        import numpy as np
        N_NODE = 12500
        N_EDGE = 200000
        D_IN = 128
        D_OUT = 128
        n_node = x.shape[0]
        row, col = (edge_index[0], edge_index[1])
        deg = jax.ops.segment_sum(edge_weight, row, num_segments=n_node)
        deg = jnp.where(deg < 0.5, deg + 1.0, deg)
        w = edge_weight / deg[row]
        h = jax.nn.relu(x @ W.T + b)
        out = jax.ops.segment_sum(w[:, None] * h[col], row, num_segments=n_node)
        return out
    edge_index = jnp.stack([src, dst])
    x = _layernorm(x + _L0_gnn_ref(x, edge_index, L0_gnn_W_ft, L0_gnn_b_ft, L0_gnn_W_conv, L0_gnn_b_conv, L0_gnn_velocity_factor, L0_gnn_velocity_params, L0_gnn_attention, L0_gnn_bn_scale, L0_gnn_bn_bias, L0_gnn_W1, L0_gnn_b1, L0_gnn_ln_scale, L0_gnn_ln_bias, L0_gnn_W2, L0_gnn_b2), axis=-1)
    x = _layernorm(x + _L1_gnn_ref(x, L1_gnn_W, L1_gnn_b, edge_index, edge_weight), axis=-1)
    return x

_drawn_inputs = setup_inputs


def setup_inputs(seed=0):
    import zlib

    import numpy as np

    out = dict(_drawn_inputs(seed))
    spreads = {'L0_gnn_b_ft': (0.0, 0.8),
     'L0_gnn_b_conv': (0.0, 0.8),
     'L0_gnn_attention': (0.25, 0.6),
     'L0_gnn_bn_scale': (1.0, 0.6),
     'L0_gnn_bn_bias': (0.0, 0.8),
     'L0_gnn_b1': (0.0, 0.1),
     'L0_gnn_ln_scale': (1.0, 0.2),
     'L0_gnn_ln_bias': (0.0, 0.1),
     'L0_gnn_b2': (0.0, 0.1)}
    factors = {'L0_gnn_velocity_params': 8.0}
    for name, (base, spread) in spreads.items():
        noise = np.random.default_rng([zlib.crc32(name.encode()), seed]).standard_normal(out[name].shape)
        drawn = base * np.exp(spread * noise) if base else spread * noise
        out[name] = jnp.asarray(drawn.astype(out[name].dtype))
    for name, factor in factors.items():
        out[name] = (out[name] * factor).astype(out[name].dtype)
    return out
```

```python
import concourse.bass as bass
from concourse import mybir
from contextlib import ExitStack

P = 128
F = 128
VIEWS = 4
ROW = 132
TPU = 5
SPLITS = TPU
FP32 = mybir.dt.float32
I32 = mybir.dt.int32
ALU = mybir.AluOpType
ACT = mybir.ActivationFunctionType
AX = mybir.AxisListType
FULL = (P, P)


def after(eng, sem, value):
    if isinstance(value, int) and value <= 0:
        return
    eng.wait_ge(sem, value)


def rounds(eng, n, body, last=None):
    extra = () if last is None else (FULL,)
    body(0, *extra)
    with eng.Fori(1, n - 1) as i:
        body(i, *extra)
    body(n - 1, *(() if last is None else (last,)))


def gate(eng, sem, value, passed):
    if isinstance(value, int) and value <= 0:
        return
    eng.wait_ge(sem, value)
    eng.sem_inc(passed, 1)


class Chain:

    def __init__(self, eng, sem, base=0):
        self.eng, self.sem, self.base, self.n = eng, sem, base, 0

    def link(self, instruction):
        instruction.then_inc(self.sem, 1)
        self.n += 1
        self.eng.wait_ge(self.sem, self.base + self.n)


def resnorm_gnn(nc, x, src, dst, edge_weight, W_ft, b_ft, W_conv, b_conv, velocity_factor,
                velocity_params, attention, bn_scale, bn_bias, W1, b1, ln_scale, ln_bias, W2, b2,
                L1_W, L1_b, out):
    N, E = x.shape[0], src.shape[0]
    NT = -(-N // P)
    assert NT % 2 == 0
    LAST = (P, N - (NT - 1) * P)
    UE = TPU * P
    NU = 2 * -(-E // (2 * UE))
    NG = NU // 2
    FU = E // UE
    TAIL = (E - FU * UE) // TPU
    assert TAIL * TPU == E - FU * UE and TAIL % 32 == 0 and NU - FU <= 2
    Z = W1.shape[1]
    ZB = Z // P
    EPS = 1e-5
    SUM_ROWS = NT * P + P

    node_table = nc.dram_tensor("node_table", [N, ROW], FP32).ap()
    pos_table = nc.dram_tensor("pos_table", [N, 4], FP32).ap()
    gathered = nc.dram_tensor("gathered", [NU, P, TPU * ROW], FP32).ap()
    agg = nc.dram_tensor("agg", [SUM_ROWS, VIEWS * F], FP32).ap()
    h1_table = nc.dram_tensor("h1_table", [N, F], FP32).ap()
    sums = [nc.dram_tensor(f"sums{k}", [SUM_ROWS, F + 1], FP32).ap() for k in range(SPLITS)]
    x1_rows = nc.dram_tensor("x1_rows", [N, F], FP32).ap()

    top = ExitStack()
    with top:
        def tensor(ctx, name, shape, dt=FP32):
            return ctx.enter_context(nc.sbuf_tensor(name, shape, dt))

        def bank(ctx, name, shape):
            return ctx.enter_context(nc.psum_tensor(name, shape, FP32))

        def sem(ctx, name):
            return ctx.enter_context(nc.semaphore(name))

        pool_passed = sem(top, "pool_passed")
        vector_passed = sem(top, "vector_passed")
        ident = tensor(top, "ident", [P, P])
        earlier = tensor(top, "earlier", [P, P])
        ones = tensor(top, "ones", [1, P])
        trash = tensor(top, "trash", [P, 1])
        trash_i = tensor(top, "trash_i", [P, 1], I32)
        w_ft = tensor(top, "w_ft", [P, F])
        w_conv = tensor(top, "w_conv", [P, ROW])
        bias_conv = tensor(top, "bias_conv", [1, ROW])
        b_ft_c = tensor(top, "b_ft_c", [P, 1])
        w1 = tensor(top, "w1", [P, VIEWS, Z])
        b1_r = tensor(top, "b1_r", [1, Z])
        w2 = tensor(top, "w2", [P, ZB, F])
        b2_r = tensor(top, "b2_r", [1, F])
        ln_s = tensor(top, "ln_s", [P, ZB])
        ln_b = tensor(top, "ln_b", [P, ZB])
        bn_s = tensor(top, "bn_s", [P, VIEWS])
        bn_b = tensor(top, "bn_b", [P, VIEWS])
        att = tensor(top, "att", [VIEWS, F])
        l1_w = tensor(top, "l1_w", [P, F])
        l1_b = tensor(top, "l1_b", [1, F])
        v_obs = tensor(top, "v_obs", [P, VIEWS])
        v_fac = tensor(top, "v_fac", [P, 1])
        src_i = tensor(top, "src_i", [P, NU * TPU], I32)
        dst_i = tensor(top, "dst_i", [P, NU * TPU], I32)
        ew = tensor(top, "ew", [P, NU * TPU])
        dist = tensor(top, "dist", [P, NU * TPU])
        dirs = tensor(top, "dirs", [P, NU * TPU])
        aberr = tensor(top, "aberr", [P, VIEWS, NU * TPU])

        def rows(table, t, r):
            return table[bass.ds(t * P, r), :]

        with ExitStack() as ctx:
            x_in = [tensor(ctx, f"x_in{s}", [P, F]) for s in range(2)]
            xT = [tensor(ctx, f"xT{s}", [P, P]) for s in range(2)]
            hT = [tensor(ctx, f"hT{s}", [P, P]) for s in range(2)]
            row_out = [tensor(ctx, f"row_out{s}", [P, ROW]) for s in range(2)]
            pt = [bank(ctx, f"pt{s}", [P, P]) for s in range(2)]
            ph = [bank(ctx, f"ph{s}", [P, P]) for s in range(2)]
            pr = [bank(ctx, f"pr{s}", [P, ROW]) for s in range(2)]
            cleared = sem(ctx, "cleared")
            pads_cleared = sem(ctx, "pads_cleared")
            masks_cleared = sem(ctx, "masks_cleared")
            ones_written = sem(ctx, "ones_written")
            constants = sem(ctx, "constants")
            weights_in = sem(ctx, "weights_in")
            edges_in = sem(ctx, "edges_in")
            trash_written = sem(ctx, "trash_written")
            x_loaded = [sem(ctx, f"x_loaded{s}") for s in range(2)]
            x_transposed = sem(ctx, "x_transposed")
            xT_ready = sem(ctx, "xT_ready")
            h_summed = sem(ctx, "h_summed")
            hT_ready = sem(ctx, "hT_ready")
            row_summed = sem(ctx, "row_summed")
            row_ready = sem(ctx, "row_ready")
            row_stored = [sem(ctx, f"row_stored{s}") for s in range(2)]
            block = ctx.enter_context(nc.Block())
            EARLY = 4

            @block.sync
            def _(sp):
                sp.wait_ge(cleared, 2)
                sp.dma_start(w_ft[:, :], W_ft).then_inc(weights_in, 16)
                sp.dma_start(w_conv[:, 0:F], W_conv).then_inc(weights_in, 16)
                sp.dma_start(bias_conv[:, 0:F], b_conv.unsqueeze(0)).then_inc(weights_in, 16)
                sp.dma_start(b_ft_c[:, :], b_ft.unsqueeze(1)).then_inc(weights_in, 16)

                def load(i, r=FULL):
                    for s in range(2):
                        t = 2 * i + s
                        after(sp, x_transposed, t - 1)
                        sp.dma_start(x_in[s][0:r[s], :], rows(x, t, r[s])).then_inc(x_loaded[s], 16)

                rounds(sp, NT // 2, load, LAST)

            @block.gpsimd
            def _(pool):
                nc.gpsimd.memset(w_conv[:, F:ROW], 0.0).then_inc(cleared, 1)
                nc.gpsimd.memset(bias_conv[:, F:ROW], 0.0).then_inc(cleared, 1)
                nc.gpsimd.memset(ident[:, :], 0.0).then_inc(masks_cleared, 1)
                nc.gpsimd.memset(earlier[:, :], 1.0).then_inc(masks_cleared, 1)
                pool.wait_ge(masks_cleared, 2)
                pool.wait_ge(cleared, 2)
                nc.gpsimd.affine_select(out=ident[:, :], in_=ident[:, :], compare_op=ALU.not_equal,
                                        fill=1.0, base=0, pattern=[[-1, P]],
                                        channel_multiplier=1).then_inc(constants, 1)
                nc.gpsimd.affine_select(out=w_conv[:, F:F + 3], in_=w_conv[:, F:F + 3],
                                        compare_op=ALU.not_equal, fill=1.0, base=0,
                                        pattern=[[-1, 3]], channel_multiplier=1).then_inc(constants, 1)
                nc.gpsimd.affine_select(out=earlier[:, :], in_=earlier[:, :], compare_op=ALU.is_gt,
                                        fill=0.0, base=0, pattern=[[-1, P]],
                                        channel_multiplier=1).then_inc(constants, 1)
                nc.gpsimd.iota(trash_i[:, :], [[0, 1]], base=NT * P, channel_multiplier=1)\
                    .then_inc(trash_written, 1)
                pool.wait_ge(trash_written, 1)
                nc.gpsimd.tensor_copy(trash[:, :], trash_i[:, :])

                def store(i, r=FULL):
                    for s in range(2):
                        t = 2 * i + s
                        gate(pool, row_ready, t + 1, pool_passed)
                        pool.dma_start(rows(node_table, t, r[s]), row_out[s][0:r[s], :])\
                            .then_inc(row_stored[s], 16)
                        pool.dma_start(rows(pos_table, t, r[s]), row_out[s][0:r[s], F:ROW])\
                            .then_inc(row_stored[s], 16)

                rounds(pool, NT // 2, store, LAST)
                for s in range(2):
                    pool.wait_ge(row_stored[s], 32 * (NT // 2))

            @block.tensor
            def _(pe):
                pe.wait_ge(constants, 3)
                pe.wait_ge(ones_written, 1)
                pe.wait_ge(weights_in, 16 * EARLY)

                def tile(i, r=FULL):
                    for s in range(2):
                        t = 2 * i + s
                        pe.wait_ge(x_loaded[s], 16 * (i + 1))
                        after(pe, xT_ready, t - 1)
                        nc.tensor.transpose(pt[s][:, 0:r[s]], x_in[s][0:r[s], :],
                                            ident[0:r[s], 0:r[s]]).then_inc(x_transposed, 1)
                    for s in range(2):
                        t = 2 * i + s
                        pe.wait_ge(xT_ready, t + 1)
                        after(pe, hT_ready, t - 1)
                        nc.tensor.matmul(ph[s][:, 0:r[s]], w_ft[:, :], xT[s][:, 0:r[s]], start=True,
                                         stop=True).then_inc(h_summed, 1)
                    for s in range(2):
                        t = 2 * i + s
                        pe.wait_ge(hT_ready, t + 1)
                        after(pe, row_ready, t - 1)
                        nc.tensor.matmul(pr[s][0:r[s], :], hT[s][:, 0:r[s]], w_conv[:, :],
                                         start=True, stop=False)
                        nc.tensor.matmul(pr[s][0:r[s], :], ones[:, 0:r[s]], bias_conv[:, :],
                                         start=False, stop=True).then_inc(row_summed, 1)

                rounds(pe, NT // 2, tile, LAST)

            @block.scalar
            def _(act):
                act.dma_start(w1[:, :, :], W1.rearrange("(v p) z -> p v z", p=P)).then_inc(edges_in, 16)
                act.dma_start(w2[:, :, :], W2.rearrange("(v p) z -> p v z", p=P)).then_inc(edges_in, 16)
                act.dma_start(b1_r[:, :], b1.unsqueeze(0)).then_inc(edges_in, 16)
                act.dma_start(b2_r[:, :], b2.unsqueeze(0)).then_inc(edges_in, 16)
                act.dma_start(l1_b[:, :], L1_b.unsqueeze(0)).then_inc(edges_in, 16)
                act.dma_start(l1_w[:, :], L1_W).then_inc(edges_in, 16)
                act.dma_start(att[:, :], attention).then_inc(edges_in, 16)
                for v in range(VIEWS):
                    act.dma_start(bn_s[:, v:v + 1], bn_scale[v].unsqueeze(1)).then_inc(edges_in, 16)
                    act.dma_start(bn_b[:, v:v + 1], bn_bias[v].unsqueeze(1)).then_inc(edges_in, 16)
                for b in range(ZB):
                    act.dma_start(ln_s[:, b:b + 1], ln_scale[b * P:(b + 1) * P].unsqueeze(1))\
                        .then_inc(edges_in, 16)
                    act.dma_start(ln_b[:, b:b + 1], ln_bias[b * P:(b + 1) * P].unsqueeze(1))\
                        .then_inc(edges_in, 16)
                act.dma_start(v_obs[:, :], velocity_params.unsqueeze(0).broadcast_to([P, VIEWS]))\
                    .then_inc(edges_in, 16)
                act.dma_start(v_fac[:, :], velocity_factor.unsqueeze(0).broadcast_to([P, 1]))\
                    .then_inc(edges_in, 16)
                act.wait_ge(pads_cleared, 3)
                for held, given in ((src_i, src), (dst_i, dst), (ew, edge_weight)):
                    act.dma_start(held[:, 0:FU * TPU].rearrange("p (u k) -> p u k", k=TPU),
                                  given[0:FU * UE].rearrange("(u p k) -> p u k", p=P, k=TPU))\
                        .then_inc(edges_in, 16)
                    if TAIL:
                        act.dma_start(held[0:TAIL, FU * TPU:(FU + 1) * TPU],
                                      given[FU * UE:E].rearrange("(p k) -> p k", k=TPU))\
                            .then_inc(edges_in, 16)
                act.wait_ge(weights_in, 16 * EARLY)

                def tile(i, r=FULL):
                    for s in range(2):
                        t = 2 * i + s
                        act.wait_ge(x_transposed, t + 1)
                        after(act, h_summed, t - 1)
                        nc.scalar.copy(xT[s][:, 0:r[s]], pt[s][:, 0:r[s]]).then_inc(xT_ready, 1)
                    for s in range(2):
                        t = 2 * i + s
                        act.wait_ge(h_summed, t + 1)
                        after(act, row_summed, t - 1)
                        nc.scalar.activation(hT[s][:, 0:r[s]], ph[s][:, 0:r[s]], ACT.Relu,
                                             bias=b_ft_c[:, 0:1]).then_inc(hT_ready, 1)

                rounds(act, NT // 2, tile, LAST)
                act.wait_ge(edges_in, 16 * (9 + 2 * VIEWS + 2 * ZB + 3 * (1 + (TAIL > 0))))

            @block.vector
            def _(dve):
                nc.vector.memset(ones[:, :], 1.0).then_inc(ones_written, 1)
                for held in (src_i, dst_i, ew):
                    nc.vector.memset(held[:, FU * TPU:NU * TPU], 0).then_inc(pads_cleared, 1)

                def tile(i, r=FULL):
                    for s in range(2):
                        t = 2 * i + s
                        dve.wait_ge(row_summed, t + 1)
                        after(dve, row_stored[s], 32 * i)
                        nc.vector.tensor_copy(row_out[s][0:r[s], :], pr[s][0:r[s], :])\
                            .then_inc(row_ready, 1)

                rounds(dve, NT // 2, tile, LAST)

        with ExitStack() as ctx:
            zeros = tensor(ctx, "zeros", [P, 11 * VIEWS * F])
            at_src = [tensor(ctx, f"at_src{a}", [P, TPU], I32) for a in range(2)]
            at_dst = [tensor(ctx, f"at_dst{a}", [P, TPU], I32) for a in range(2)]
            src_row = [tensor(ctx, f"src_row{a}", [P, TPU, ROW]) for a in range(2)]
            dst_pos = [tensor(ctx, f"dst_pos{a}", [P, TPU, 4]) for a in range(2)]
            dpos = tensor(ctx, "dpos", [P, TPU, 3])
            square = tensor(ctx, "square", [P, TPU, 3])
            zeros_ready = sem(ctx, "zeros_ready")
            tables_zeroed = sem(ctx, "tables_zeroed")
            index_ready = sem(ctx, "index_ready")
            rows_in = [sem(ctx, f"rows_in{a}") for a in range(2)]
            rows_out = [sem(ctx, f"rows_out{a}") for a in range(2)]
            measured = sem(ctx, "measured")
            vector_step = sem(ctx, "vector_step")
            block = ctx.enter_context(nc.Block())
            def clears():
                for table in [agg, *sums]:
                    per = SUM_ROWS * table.shape[1] // P
                    every = table.rearrange("n f -> (n f)").rearrange("(p m) -> p m", p=P)
                    at = 0
                    while at < per:
                        m = min(per - at, zeros.shape[1])
                        yield every[:, at:at + m], zeros[:, 0:m]
                        at += m

            @block.sync
            def _(sp):
                sp.wait_ge(zeros_ready, 1)
                n = 0
                for to, of in clears():
                    sp.dma_start(to, of).then_inc(tables_zeroed, 16)
                    n += 1

                def store(g):
                    for a in range(2):
                        sp.wait_ge(rows_in[a], 16 * 2 * TPU * (g + 1))
                        sp.dma_start(gathered[2 * g + a, :, :].squeeze() if isinstance(g, int) else
                                     gathered[bass.ds(2 * g + a, 1), :, :].rearrange("a p m -> (a p) m"),
                                     src_row[a][:, :, :].rearrange("p k f -> p (k f)"))\
                            .then_inc(rows_out[a], 16)

                rounds(sp, NG, store)
                for a in range(2):
                    sp.wait_ge(rows_out[a], 16 * NG)
                sp.wait_ge(tables_zeroed, 16 * n)

            @block.gpsimd
            def _(pool):
                def gather(g):
                    for a in range(2):
                        u = 2 * g + a
                        gate(pool, index_ready, 2 * (u + 1), pool_passed)
                        gate(pool, rows_out[a], 16 * g, pool_passed)
                        gate(pool, measured, u - 1, pool_passed)
                        for k in range(TPU):
                            pool.indirect_dma_start(
                                src_row[a][:, k, :], None, node_table,
                                bass.IndirectOffsetOnAxis(ap=at_src[a][:, k:k + 1], axis=0),
                            ).then_inc(rows_in[a], 16)
                            pool.indirect_dma_start(
                                dst_pos[a][:, k, :], None, pos_table,
                                bass.IndirectOffsetOnAxis(ap=at_dst[a][:, k:k + 1], axis=0),
                            ).then_inc(rows_in[a], 16)

                rounds(pool, NG, gather)

            @block.scalar
            def _(act):
                def indices(g):
                    for a in range(2):
                        u = 2 * g + a
                        after(act, rows_in[a], 16 * 2 * TPU * g)
                        nc.scalar.copy(at_src[a][:, :], src_i[:, bass.ds(u * TPU, TPU)])\
                            .then_inc(index_ready, 1)
                        nc.scalar.copy(at_dst[a][:, :], dst_i[:, bass.ds(u * TPU, TPU)])\
                            .then_inc(index_ready, 1)

                rounds(act, NG, indices)

            @block.vector
            def _(dve):
                nc.vector.memset(zeros[:, :], 0.0).then_inc(zeros_ready, 1)

                def measure(g):
                    for a in range(2):
                        u = 2 * g + a
                        chain = Chain(dve, vector_step, 3 * u)
                        dve.wait_ge(rows_in[a], 16 * 2 * TPU * (g + 1))
                        chain.link(nc.vector.tensor_tensor(dpos[:, :, :], src_row[a][:, :, F:F + 3],
                                                           dst_pos[a][:, :, 0:3], ALU.subtract))
                        chain.link(nc.vector.tensor_tensor(square[:, :, :], dpos[:, :, :],
                                                           dpos[:, :, :], ALU.mult))
                        nc.vector.tensor_reduce(dist[:, bass.ds(u * TPU, TPU)], square[:, :, :],
                                                axis=AX.X, op=ALU.add)
                        chain.link(nc.vector.tensor_reduce(dirs[:, bass.ds(u * TPU, TPU)],
                                                           dpos[:, :, :], axis=AX.X, op=ALU.add))
                        dve.nop().then_inc(measured, 1)

                rounds(dve, NG, measure)

        with ExitStack() as ctx:
            far = tensor(ctx, "far", [P, 1])
            far_all = tensor(ctx, "far_all", [P, 1])
            near = tensor(ctx, "near", [P, 1])
            work = tensor(ctx, "work", [P, NU * TPU])
            speed = tensor(ctx, "speed", [P, NU * TPU])
            root = tensor(ctx, "root", [P, NU * TPU])
            vector_step = sem(ctx, "vector_step2")
            squares_ready = sem(ctx, "squares_ready")
            dist_ready = sem(ctx, "dist_ready")
            far_ready = sem(ctx, "far_ready")
            far_shared = sem(ctx, "far_shared")
            rest_ready = sem(ctx, "rest_ready")
            root_ready = sem(ctx, "root_ready")
            block = ctx.enter_context(nc.Block())

            @block.scalar
            def _(act):
                act.wait_ge(squares_ready, 1)
                nc.scalar.activation(dist[:, :], dist[:, :], ACT.Sqrt).then_inc(dist_ready, 1)
                for v in range(VIEWS):
                    act.wait_ge(rest_ready, v + 1)
                    nc.scalar.activation(root[:, :], root[:, :], ACT.Sqrt).then_inc(root_ready, 1)

            @block.gpsimd
            def _(pool):
                pool.wait_ge(far_ready, 1)
                nc.gpsimd.partition_all_reduce(far_all[:, :], far[:, :], P,
                                               bass.bass_isa.ReduceOp.max).then_inc(far_shared, 1)

            @block.vector
            def _(dve):
                chain = Chain(dve, vector_step)
                chain.link(nc.vector.tensor_scalar(dist[:, :], dist[:, :], 1e-32, None, ALU.max))
                dve.nop().then_inc(squares_ready, 1)
                dve.wait_ge(dist_ready, 1)
                nc.vector.tensor_reduce(far[:, :], dist[:, :], axis=AX.X, op=ALU.max)\
                    .then_inc(far_ready, 1)
                chain.link(nc.vector.tensor_scalar(work[:, :], dist[:, :], 1e-8, None, ALU.add))
                chain.link(nc.vector.reciprocal(work[:, :], work[:, :]))
                chain.link(nc.vector.tensor_tensor(dirs[:, :], dirs[:, :], work[:, :], ALU.mult))
                dve.wait_ge(far_shared, 1)
                chain.link(nc.vector.reciprocal(near[:, :], far_all[:, :]))
                chain.link(nc.vector.tensor_scalar(dist[:, :], dist[:, :], near[:, 0:1], None, ALU.mult))
                for v in range(VIEWS):
                    chain.link(nc.vector.tensor_scalar(speed[:, :], dist[:, :], v_obs[:, v:v + 1],
                                                       v_fac[:, 0:1], ALU.min, ALU.mult))
                    chain.link(nc.vector.tensor_tensor(root[:, :], speed[:, :], speed[:, :], ALU.mult))
                    chain.link(nc.vector.tensor_scalar(root[:, :], root[:, :], -1.0, 1.0, ALU.mult,
                                                       ALU.add))
                    dve.nop().then_inc(rest_ready, 1)
                    chain.link(nc.vector.tensor_tensor(work[:, :], speed[:, :], dirs[:, :], ALU.mult))
                    chain.link(nc.vector.tensor_scalar(work[:, :], work[:, :], 1.0, None, ALU.add))
                    chain.link(nc.vector.reciprocal(work[:, :], work[:, :]))
                    dve.wait_ge(root_ready, v + 1)
                    chain.link(nc.vector.tensor_tensor(aberr[:, v, :], root[:, :], work[:, :], ALU.mult))
                if TAIL:
                    nc.vector.memset(aberr[TAIL:P, :, FU * TPU:(FU + 1) * TPU], 0.0)
                if NU > FU + (TAIL > 0):
                    nc.vector.memset(aberr[:, :, (FU + (TAIL > 0)) * TPU:NU * TPU], 0.0)

        with ExitStack() as ctx:
            row_in = [tensor(ctx, f"row_in{a}", [P, TPU, ROW]) for a in range(2)]
            node = [tensor(ctx, f"node{a}", [P, TPU]) for a in range(2)]
            share = [tensor(ctx, f"share{a}", [P, VIEWS, TPU]) for a in range(2)]
            same = [tensor(ctx, f"same{j}", [P, VIEWS, P]) for j in range(2)]
            scrap = tensor(ctx, "scrap", [P, P])
            before = [tensor(ctx, f"before{a}", [P, TPU]) for a in range(2)]
            to_trash = tensor(ctx, "to_trash", [P, TPU])
            moved = tensor(ctx, "moved", [P, TPU])
            at_node = [tensor(ctx, f"at_node{a}", [P, TPU], I32) for a in range(2)]
            total = [tensor(ctx, f"total{j}", [P, VIEWS * F]) for j in range(2)]
            pn = [bank(ctx, f"pn{j}", [P, P]) for j in range(2)]
            ps = [bank(ctx, f"ps{j}", [P, VIEWS * F]) for j in range(2)]
            rows_in = [sem(ctx, f"rows_in_b{a}") for a in range(2)]
            staged = sem(ctx, "staged")
            nodes_spread = sem(ctx, "nodes_spread")
            same_ready = sem(ctx, "same_ready")
            summed = sem(ctx, "summed")
            total_ready = sem(ctx, "total_ready")
            at_ready = sem(ctx, "at_ready")
            added = sem(ctx, "added")
            vector_step = sem(ctx, "vector_step3")
            block = ctx.enter_context(nc.Block())

            @block.sync
            def _(sp):
                def load(g):
                    for a in range(2):
                        u = 2 * g + a
                        after(sp, summed, TPU * (u - 1))
                        sp.dma_start(row_in[a][:, :, :].rearrange("p k f -> p (k f)"),
                                     gathered[bass.ds(u, 1), :, :].rearrange("a p m -> (a p) m"))\
                            .then_inc(rows_in[a], 16)

                rounds(sp, NG, load)

            @block.scalar
            def _(act):
                def stage(g):
                    for a in range(2):
                        u = 2 * g + a
                        after(act, at_ready, u - 1)
                        after(act, same_ready, TPU * (u - 1))
                        nc.scalar.copy(node[a][:, :], dst_i[:, bass.ds(u * TPU, TPU)])
                        nc.scalar.copy(share[a][:, :, :], aberr[:, :, bass.ds(u * TPU, TPU)])\
                            .then_inc(staged, 1)
                    for a in range(2):
                        u = 2 * g + a
                        for k in range(TPU):
                            q = TPU * u + k
                            act.wait_ge(summed, q + 1)
                            after(act, added, 16 * (q - 1))
                            j = (TPU * a + k) % 2
                            nc.scalar.copy(total[j][:, :], ps[j][:, :]).then_inc(total_ready, 1)

                rounds(act, NG, stage)

            @block.tensor
            def _(pe):
                def unit(g):
                    for a in range(2):
                        u = 2 * g + a
                        pe.wait_ge(staged, u + 1)
                        pe.wait_ge(rows_in[a], 16 * (g + 1))
                        for k in range(TPU):
                            q, j = TPU * u + k, (TPU * a + k) % 2
                            after(pe, same_ready, q - 1)
                            nc.tensor.matmul(pn[j][:, :], node[a][:, k:k + 1].to_broadcast([P, P]),
                                             ident[:, :], start=True, stop=True)\
                                .then_inc(nodes_spread, 1)
                            pe.wait_ge(same_ready, q + 1)
                            after(pe, total_ready, q - 1)
                            for v in range(VIEWS):
                                last = nc.tensor.matmul(ps[j][:, v * F:(v + 1) * F], same[j][:, v, :],
                                                        row_in[a][:, k, 0:F], start=True, stop=True)
                            last.then_inc(summed, 1)

                rounds(pe, NG, unit)

            @block.vector
            def _(dve):
                def unit(g):
                    for a in range(2):
                        u = 2 * g + a
                        chain = Chain(dve, vector_step, 3 * u)
                        dve.wait_ge(staged, u + 1)
                        for k in range(TPU):
                            q, j = TPU * u + k, (TPU * a + k) % 2
                            dve.wait_ge(nodes_spread, q + 1)
                            after(dve, summed, q - 1)
                            nc.vector.scalar_tensor_tensor(
                                out=scrap[:, :], in0=pn[j][:, :], scalar=node[a][:, k:k + 1],
                                in1=earlier[:, :], op0=ALU.is_equal, op1=ALU.mult,
                                accum_out=before[a][:, k:k + 1])
                            for v in range(VIEWS):
                                last = nc.vector.tensor_scalar(
                                    same[j][:, v, :], pn[j][:, :], node[a][:, k:k + 1],
                                    share[a][:, v, k:k + 1], ALU.is_equal, ALU.mult)
                            last.then_inc(same_ready, 1)
                        dve.wait_ge(same_ready, TPU * (u + 1))
                        after(dve, added, 16 * TPU * (u - 1))
                        chain.link(nc.vector.tensor_scalar(to_trash[:, :], node[a][:, :], -1.0,
                                                           trash[:, 0:1], ALU.mult, ALU.add))
                        chain.link(nc.vector.scalar_tensor_tensor(
                            out=moved[:, :], in0=before[a][:, :], scalar=0.5, in1=to_trash[:, :],
                            op0=ALU.is_gt, op1=ALU.mult))
                        chain.link(nc.vector.tensor_tensor(at_node[a][:, :], moved[:, :],
                                                           node[a][:, :], ALU.add))
                        dve.nop().then_inc(at_ready, 1)

                rounds(dve, NG, unit)

            @block.gpsimd
            def _(pool):
                def scatter(g):
                    for a in range(2):
                        u = 2 * g + a
                        gate(pool, at_ready, u + 1, pool_passed)
                        for k in range(TPU):
                            q, j = TPU * u + k, (TPU * a + k) % 2
                            pool.wait_ge(total_ready, q + 1)
                            gate(pool, added, 16 * q, pool_passed)
                            pool.indirect_dma_start(
                                agg, bass.IndirectOffsetOnAxis(ap=at_node[a][:, k:k + 1], axis=0),
                                total[j][:, :], None, compute_op=ALU.add).then_inc(added, 16)

                rounds(pool, NG, scatter)
                pool.wait_ge(added, 16 * TPU * NU)

        with ExitStack() as both:
            bn_scale_c = tensor(both, "bn_scale_c", [P, VIEWS])
            bn_bias_c = tensor(both, "bn_bias_c", [P, VIEWS])
            l1_wT = tensor(both, "l1_wT", [P, F])
            with ExitStack() as ctx:
                a_in = [tensor(ctx, f"a_in{s}", [P, VIEWS * F]) for s in range(2)]
                stats = tensor(ctx, "stats", [P, VIEWS, NT * 6])
                moments = tensor(ctx, "moments", [P, VIEWS, 2])
                small = tensor(ctx, "small", [P, VIEWS])
                soft = tensor(ctx, "soft", [VIEWS, F])
                peak = tensor(ctx, "peak", [VIEWS, 1])
                mass = tensor(ctx, "mass", [VIEWS, 1])
                softT = tensor(ctx, "softT", [P, VIEWS])
                pa = [bank(ctx, f"pa{s}", [P, VIEWS, P]) for s in range(2)]
                pw = bank(ctx, "pw", [P, P])
                px = bank(ctx, "px", [P, P])
                a_loaded = [sem(ctx, f"a_loaded{s}") for s in range(2)]
                a_transposed = sem(ctx, "a_transposed")
                a_measured = sem(ctx, "a_measured")
                peak_ready = sem(ctx, "peak_ready")
                soft_ready = sem(ctx, "soft_ready")
                soft_scaled = sem(ctx, "soft_scaled")
                turned = sem(ctx, "turned")
                variance_ready = sem(ctx, "variance_ready")
                deviation_ready = sem(ctx, "deviation_ready")
                vector_step = sem(ctx, "vector_step4")
                block = ctx.enter_context(nc.Block())

                @block.sync
                def _(sp):
                    def load(i, r=FULL):
                        for s in range(2):
                            t = 2 * i + s
                            after(sp, a_transposed, t - 1)
                            sp.dma_start(a_in[s][0:r[s], :], rows(agg, t, r[s]))\
                                .then_inc(a_loaded[s], 16)

                    rounds(sp, NT // 2, load, LAST)

                @block.tensor
                def _(pe):
                    def tile(i, r=FULL):
                        for s in range(2):
                            t = 2 * i + s
                            pe.wait_ge(a_loaded[s], 16 * (i + 1))
                            after(pe, a_measured, t - 1)
                            for v in range(VIEWS):
                                last = nc.tensor.transpose(pa[s][:, v, 0:r[s]],
                                                           a_in[s][0:r[s], v * F:(v + 1) * F],
                                                           ident[0:r[s], 0:r[s]])
                            last.then_inc(a_transposed, 1)

                    rounds(pe, NT // 2, tile, LAST)
                    nc.tensor.transpose(pw[:, :], l1_w[:, :], ident[:, :]).then_inc(turned, 1)
                    pe.wait_ge(soft_scaled, 1)
                    nc.tensor.transpose(px[:, 0:VIEWS], soft[:, :], ident[0:VIEWS, 0:VIEWS])\
                        .then_inc(turned, 1)

                @block.scalar
                def _(act):
                    act.wait_ge(peak_ready, 1)
                    nc.scalar.activation(soft[:, :], att[:, :], ACT.Exp, bias=peak[:, 0:1],
                                         accum_out=mass[:, 0:1]).then_inc(soft_ready, 1)
                    act.wait_ge(variance_ready, 1)
                    nc.scalar.activation(small[:, :], small[:, :], ACT.Sqrt)\
                        .then_inc(deviation_ready, 1)

                @block.vector
                def _(dve):
                    def tile(i, r=FULL):
                        for s in range(2):
                            t = 2 * i + s
                            dve.wait_ge(a_transposed, t + 1)
                            for v in range(VIEWS):
                                last = nc.vector.bn_stats(stats[:, v, bass.ds(t * 6, 6)],
                                                          pa[s][:, v, 0:r[s]])
                            last.then_inc(a_measured, 1)

                    rounds(dve, NT // 2, tile, LAST)
                    chain = Chain(dve, vector_step)
                    chain.link(nc.vector.tensor_reduce(peak[:, :], att[:, :], axis=AX.X, op=ALU.max))
                    chain.link(nc.vector.tensor_scalar(peak[:, :], peak[:, :], -1.0, None, ALU.mult))
                    dve.nop().then_inc(peak_ready, 1)
                    dve.wait_ge(a_measured, NT)
                    for v in range(VIEWS):
                        chain.link(nc.vector.bn_aggr(moments[:, v, :], stats[:, v, :]))
                    chain.link(nc.vector.tensor_scalar(small[:, :], moments[:, :, 1], EPS, None,
                                                       ALU.add))
                    dve.nop().then_inc(variance_ready, 1)
                    dve.wait_ge(soft_ready, 1)
                    chain.link(nc.vector.reciprocal(mass[:, :], mass[:, :]))
                    chain.link(nc.vector.tensor_scalar(soft[:, :], soft[:, :], mass[:, 0:1], None,
                                                       ALU.mult))
                    dve.nop().then_inc(soft_scaled, 1)
                    dve.wait_ge(deviation_ready, 1)
                    chain.link(nc.vector.reciprocal(small[:, :], small[:, :]))
                    chain.link(nc.vector.tensor_tensor(bn_scale_c[:, :], small[:, :], bn_s[:, :],
                                                       ALU.mult))
                    chain.link(nc.vector.tensor_tensor(small[:, :], bn_scale_c[:, :],
                                                       moments[:, :, 0], ALU.mult))
                    chain.link(nc.vector.tensor_tensor(bn_bias_c[:, :], bn_b[:, :], small[:, :],
                                                       ALU.subtract))
                    dve.wait_ge(turned, 2)
                    chain.link(nc.vector.tensor_copy(l1_wT[:, :], pw[:, :]))
                    chain.link(nc.vector.tensor_copy(softT[:, :], px[:, 0:VIEWS]))
                    chain.link(nc.vector.tensor_tensor(bn_scale_c[:, :], bn_scale_c[:, :],
                                                       softT[:, :], ALU.mult))
                    chain.link(nc.vector.tensor_tensor(bn_bias_c[:, :], bn_bias_c[:, :],
                                                       softT[:, :], ALU.mult))

            with ExitStack() as ctx:
                def pair(name, shape):
                    return [tensor(ctx, f"{name}{s}", shape) for s in range(2)]

                a_in, x_in = pair("a_again", [P, VIEWS * F]), pair("x_again", [P, F])
                view = pair("view", [P, VIEWS, P])
                zstat, zmom, zdev = pair("zstat", [P, 6]), pair("zmom", [P, 2]), pair("zdev", [P, 1])
                z_n, z_r = pair("z_n", [P, Z]), pair("z_r", [P, ZB, P])
                y = pair("y", [P, F])
                ystat, ymom, ydev = pair("ystat", [P, 6]), pair("ymom", [P, 2]), pair("ydev", [P, 1])
                x1, x1T, h1 = pair("x1", [P, F]), pair("x1T", [P, P]), pair("h1", [P, F])
                pa = [bank(ctx, f"pb{s}", [P, VIEWS, P]) for s in range(2)]
                pz = [bank(ctx, f"pz{s}", [P, 512]) for s in range(2)]
                pt = [bank(ctx, f"pt2{s}", [P, ZB, P]) for s in range(2)]
                names = ("a_turned", "view_ready", "z_summed", "z_dev", "z_root", "z_ready",
                         "z_turned", "z_relu", "y_summed", "y_dev", "y_root", "x1_ready",
                         "x1_turned", "x1T_ready", "h1_summed", "h1_ready")
                (a_turned, view_ready, z_summed, z_dev, z_root, z_ready, z_turned, z_relu, y_summed,
                 y_dev, y_root, x1_ready, x1_turned, x1T_ready, h1_summed, h1_ready) = (
                    sem(ctx, n) for n in names)
                loaded = [sem(ctx, f"loaded{s}") for s in range(2)]
                stored = [sem(ctx, f"stored{s}") for s in range(2)]
                vector_step = sem(ctx, "vector_step5")
                block = ctx.enter_context(nc.Block())

                @block.sync
                def _(sp):
                    def load(i, r=FULL):
                        for s in range(2):
                            t = 2 * i + s
                            after(sp, a_turned, t - 1)
                            sp.dma_start(a_in[s][0:r[s], :], rows(agg, t, r[s]))\
                                .then_inc(loaded[s], 16)
                            after(sp, y_dev, t - 1)
                            sp.dma_start(x_in[s][0:r[s], :], rows(x, t, r[s]))\
                                .then_inc(loaded[s], 16)

                    rounds(sp, NT // 2, load, LAST)

                @block.gpsimd
                def _(pool):
                    def store(i, r=FULL):
                        for s in range(2):
                            t = 2 * i + s
                            gate(pool, x1_ready, t + 1, pool_passed)
                            pool.dma_start(rows(x1_rows, t, r[s]), x1[s][0:r[s], :])\
                                .then_inc(stored[s], 16)
                            gate(pool, h1_ready, t + 1, pool_passed)
                            pool.dma_start(rows(h1_table, t, r[s]), h1[s][0:r[s], :])\
                                .then_inc(stored[s], 16)

                    rounds(pool, NT // 2, store, LAST)
                    for s in range(2):
                        pool.wait_ge(stored[s], 16 * NT)

                @block.tensor
                def _(pe):
                    def tile(i, r=FULL):
                        for s in range(2):
                            t, n = 2 * i + s, r[s]
                            pe.wait_ge(loaded[s], 32 * (i + 1))
                            after(pe, view_ready, t - 1)
                            for v in range(VIEWS):
                                last = nc.tensor.transpose(pa[s][:, v, 0:n],
                                                           a_in[s][0:n, v * F:(v + 1) * F],
                                                           ident[0:n, 0:n])
                            last.then_inc(a_turned, 1)
                        for s in range(2):
                            t, n = 2 * i + s, r[s]
                            pe.wait_ge(view_ready, t + 1)
                            after(pe, h1_ready, t - 1)
                            for v in range(VIEWS):
                                nc.tensor.matmul(pz[s][0:n, 0:Z], view[s][:, v, 0:n], w1[:, v, :],
                                                 start=(v == 0), stop=False)
                            nc.tensor.matmul(pz[s][0:n, 0:Z], ones[:, 0:n], b1_r[:, :],
                                             start=False, stop=True).then_inc(z_summed, 1)
                        for s in range(2):
                            t, n = 2 * i + s, r[s]
                            pe.wait_ge(z_ready, t + 1)
                            after(pe, x1T_ready, t - 1)
                            for b in range(ZB):
                                last = nc.tensor.transpose(pt[s][:, b, 0:n],
                                                           z_n[s][0:n, b * P:(b + 1) * P],
                                                           ident[0:n, 0:n])
                            last.then_inc(z_turned, 1)
                        for s in range(2):
                            t, n = 2 * i + s, r[s]
                            pe.wait_ge(z_relu, t + 1)
                            for b in range(ZB):
                                nc.tensor.matmul(pz[s][0:n, 0:F], z_r[s][:, b, 0:n], w2[:, b, :],
                                                 start=(b == 0), stop=False)
                            nc.tensor.matmul(pz[s][0:n, 0:F], ones[:, 0:n], b2_r[:, :],
                                             start=False, stop=True).then_inc(y_summed, 1)
                        for s in range(2):
                            t, n = 2 * i + s, r[s]
                            pe.wait_ge(x1_ready, t + 1)
                            nc.tensor.transpose(pt[s][:, 0, 0:n], x1[s][0:n, :], ident[0:n, 0:n])\
                                .then_inc(x1_turned, 1)
                        for s in range(2):
                            t, n = 2 * i + s, r[s]
                            pe.wait_ge(x1T_ready, t + 1)
                            nc.tensor.matmul(pz[s][0:n, 0:F], x1T[s][:, 0:n], l1_wT[:, :],
                                             start=True, stop=False)
                            nc.tensor.matmul(pz[s][0:n, 0:F], ones[:, 0:n], l1_b[:, :],
                                             start=False, stop=True).then_inc(h1_summed, 1)

                    rounds(pe, NT // 2, tile, LAST)

                @block.scalar
                def _(act):
                    def tile(i, r=FULL):
                        for s in range(2):
                            t, n = 2 * i + s, r[s]
                            act.wait_ge(a_turned, t + 1)
                            after(act, z_summed, t - 1)
                            for v in range(VIEWS):
                                last = nc.scalar.activation(view[s][:, v, 0:n], pa[s][:, v, 0:n],
                                                            ACT.Relu, bias=bn_bias_c[:, v:v + 1],
                                                            scale=bn_scale_c[:, v:v + 1])
                            last.then_inc(view_ready, 1)
                        for s in range(2):
                            t, n = 2 * i + s, r[s]
                            act.wait_ge(z_dev, t + 1)
                            nc.scalar.activation(zdev[s][0:n, :], zdev[s][0:n, :], ACT.Sqrt)\
                                .then_inc(z_root, 1)
                        for s in range(2):
                            t, n = 2 * i + s, r[s]
                            act.wait_ge(z_turned, t + 1)
                            after(act, y_summed, t - 1)
                            for b in range(ZB):
                                last = nc.scalar.activation(z_r[s][:, b, 0:n], pt[s][:, b, 0:n],
                                                            ACT.Relu, bias=ln_b[:, b:b + 1],
                                                            scale=ln_s[:, b:b + 1])
                            last.then_inc(z_relu, 1)
                        for s in range(2):
                            t, n = 2 * i + s, r[s]
                            act.wait_ge(y_dev, t + 1)
                            nc.scalar.activation(ydev[s][0:n, :], ydev[s][0:n, :], ACT.Sqrt)\
                                .then_inc(y_root, 1)
                        for s in range(2):
                            t, n = 2 * i + s, r[s]
                            act.wait_ge(x1_turned, t + 1)
                            after(act, h1_summed, t - 1)
                            nc.scalar.copy(x1T[s][:, 0:n], pt[s][:, 0, 0:n]).then_inc(x1T_ready, 1)
                        for s in range(2):
                            t, n = 2 * i + s, r[s]
                            act.wait_ge(h1_summed, t + 1)
                            after(act, stored[s], 32 * i)
                            nc.scalar.activation(h1[s][0:n, :], pz[s][0:n, 0:F], ACT.Relu)\
                                .then_inc(h1_ready, 1)

                    rounds(act, NT // 2, tile, LAST)

                @block.vector
                def _(dve):
                    STEPS = 4 + 5

                    def tile(i, r=FULL):
                        chain = Chain(dve, vector_step, 2 * STEPS * i)
                        for s in range(2):
                            t, n = 2 * i + s, r[s]
                            dve.wait_ge(z_summed, t + 1)
                            chain.link(nc.vector.bn_stats(zstat[s][0:n, :], pz[s][0:n, 0:Z]))
                            dve.sem_inc(vector_passed, 1)
                            chain.link(nc.vector.bn_aggr(zmom[s][0:n, :], zstat[s][0:n, :]))
                            nc.vector.tensor_scalar(zdev[s][0:n, :], zmom[s][0:n, 1:2], EPS, None,
                                                    ALU.add).then_inc(z_dev, 1)
                        for s in range(2):
                            t, n = 2 * i + s, r[s]
                            dve.wait_ge(z_root, t + 1)
                            after(dve, z_turned, t - 1)
                            chain.link(nc.vector.reciprocal(zdev[s][0:n, :], zdev[s][0:n, :]))
                            chain.link(nc.vector.tensor_scalar(
                                z_n[s][0:n, :], pz[s][0:n, 0:Z], zmom[s][0:n, 0:1],
                                zdev[s][0:n, 0:1], ALU.subtract, ALU.mult))
                            dve.nop().then_inc(z_ready, 1)
                        for s in range(2):
                            t, n = 2 * i + s, r[s]
                            dve.wait_ge(y_summed, t + 1)
                            chain.link(nc.vector.tensor_tensor(y[s][0:n, :], pz[s][0:n, 0:F],
                                                               x_in[s][0:n, :], ALU.add))
                            chain.link(nc.vector.bn_stats(ystat[s][0:n, :], y[s][0:n, :]))
                            dve.sem_inc(vector_passed, 1)
                            chain.link(nc.vector.bn_aggr(ymom[s][0:n, :], ystat[s][0:n, :]))
                            nc.vector.tensor_scalar(ydev[s][0:n, :], ymom[s][0:n, 1:2], EPS, None,
                                                    ALU.add).then_inc(y_dev, 1)
                        for s in range(2):
                            t, n = 2 * i + s, r[s]
                            dve.wait_ge(y_root, t + 1)
                            after(dve, stored[s], 32 * i)
                            after(dve, x1_turned, t - 1)
                            chain.link(nc.vector.reciprocal(ydev[s][0:n, :], ydev[s][0:n, :]))
                            chain.link(nc.vector.tensor_scalar(
                                x1[s][0:n, :], y[s][0:n, :], ymom[s][0:n, 0:1],
                                ydev[s][0:n, 0:1], ALU.subtract, ALU.mult))
                            dve.nop().then_inc(x1_ready, 1)
                        assert chain.n == 2 * STEPS

                    rounds(dve, NT // 2, tile, LAST)

        with ExitStack() as ctx:
            at_dst = [tensor(ctx, f"l1_at_dst{a}", [P, TPU], I32) for a in range(2)]
            at_src = [tensor(ctx, f"l1_at_src{a}", [P, TPU], I32) for a in range(2)]
            node = [tensor(ctx, f"l1_node{a}", [P, TPU]) for a in range(2)]
            share = [tensor(ctx, f"l1_share{a}", [P, TPU]) for a in range(2)]
            h_row = [tensor(ctx, f"h_row{a}", [P, TPU, F + 1]) for a in range(2)]
            same = [tensor(ctx, f"l1_same{j}", [P, P]) for j in range(2)]
            scrap = tensor(ctx, "l1_scrap", [P, P])
            before = [tensor(ctx, f"l1_before{a}", [P, TPU]) for a in range(2)]
            to_trash = tensor(ctx, "l1_to_trash", [P, TPU])
            moved = tensor(ctx, "l1_moved", [P, TPU])
            total = [tensor(ctx, f"l1_total{k}", [P, F + 1]) for k in range(TPU)]
            pn = [bank(ctx, f"l1_pn{j}", [P, P]) for j in range(2)]
            ps = [bank(ctx, f"l1_ps{j}", [P, F + 1]) for j in range(2)]
            ones_ready = sem(ctx, "ones_ready")
            staged = sem(ctx, "l1_staged")
            index_ready = sem(ctx, "l1_index_ready")
            rows_in = [sem(ctx, f"l1_rows_in{a}") for a in range(2)]
            nodes_spread = sem(ctx, "l1_nodes_spread")
            same_ready = sem(ctx, "l1_same_ready")
            summed = sem(ctx, "l1_summed")
            total_ready = sem(ctx, "l1_total_ready")
            at_ready = sem(ctx, "l1_at_ready")
            added = [sem(ctx, f"l1_added{k}") for k in range(TPU)]
            vector_step = sem(ctx, "vector_step6")
            block = ctx.enter_context(nc.Block())

            @block.scalar
            def _(act):
                def stage(g):
                    for a in range(2):
                        u = 2 * g + a
                        after(act, rows_in[a], 16 * TPU * g)
                        nc.scalar.copy(at_dst[a][:, :], dst_i[:, bass.ds(u * TPU, TPU)])\
                            .then_inc(index_ready, 1)
                        after(act, at_ready, u - 1)
                        nc.scalar.copy(node[a][:, :], src_i[:, bass.ds(u * TPU, TPU)])
                        nc.scalar.copy(share[a][:, :], ew[:, bass.ds(u * TPU, TPU)])\
                            .then_inc(staged, 1)
                    for a in range(2):
                        u = 2 * g + a
                        for k in range(TPU):
                            q, j = TPU * u + k, (TPU * a + k) % 2
                            act.wait_ge(summed, q + 1)
                            after(act, added[k], 16 * u)
                            nc.scalar.copy(total[k][:, :], ps[j][:, :]).then_inc(total_ready, 1)

                rounds(act, NG, stage)

            @block.tensor
            def _(pe):
                def unit(g):
                    for a in range(2):
                        u = 2 * g + a
                        pe.wait_ge(staged, u + 1)
                        for k in range(TPU):
                            q, j = TPU * u + k, (TPU * a + k) % 2
                            after(pe, same_ready, q - 1)
                            nc.tensor.matmul(pn[j][:, :], node[a][:, k:k + 1].to_broadcast([P, P]),
                                             ident[:, :], start=True, stop=True)\
                                .then_inc(nodes_spread, 1)
                            if k == 0:
                                pe.wait_ge(rows_in[a], 16 * TPU * (g + 1))
                            pe.wait_ge(same_ready, q + 1)
                            after(pe, total_ready, q - 1)
                            nc.tensor.matmul(ps[j][:, :], same[j][:, :], h_row[a][:, k, :],
                                             start=True, stop=True).then_inc(summed, 1)

                rounds(pe, NG, unit)

            @block.vector
            def _(dve):
                for a in range(2):
                    nc.vector.memset(h_row[a][:, :, F:F + 1], 1.0).then_inc(ones_ready, 1)

                def unit(g):
                    for a in range(2):
                        u = 2 * g + a
                        chain = Chain(dve, vector_step, 3 * u)
                        dve.wait_ge(staged, u + 1)
                        for k in range(TPU):
                            q, j = TPU * u + k, (TPU * a + k) % 2
                            dve.wait_ge(nodes_spread, q + 1)
                            after(dve, summed, q - 1)
                            nc.vector.scalar_tensor_tensor(
                                out=scrap[:, :], in0=pn[j][:, :], scalar=node[a][:, k:k + 1],
                                in1=earlier[:, :], op0=ALU.is_equal, op1=ALU.mult,
                                accum_out=before[a][:, k:k + 1])
                            nc.vector.tensor_scalar(
                                same[j][:, :], pn[j][:, :], node[a][:, k:k + 1],
                                share[a][:, k:k + 1], ALU.is_equal, ALU.mult)\
                                .then_inc(same_ready, 1)
                        dve.wait_ge(same_ready, TPU * (u + 1))
                        chain.link(nc.vector.tensor_scalar(to_trash[:, :], node[a][:, :], -1.0,
                                                           trash[:, 0:1], ALU.mult, ALU.add))
                        chain.link(nc.vector.scalar_tensor_tensor(
                            out=moved[:, :], in0=before[a][:, :], scalar=0.5, in1=to_trash[:, :],
                            op0=ALU.is_gt, op1=ALU.mult))
                        for k in range(TPU):
                            after(dve, added[k], 16 * (u - 1))
                        chain.link(nc.vector.tensor_tensor(at_src[a][:, :], moved[:, :],
                                                           node[a][:, :], ALU.add))
                        dve.nop().then_inc(at_ready, 1)

                rounds(dve, NG, unit)

            @block.gpsimd
            def _(pool):
                pool.wait_ge(ones_ready, 2)

                def gather(g, a):
                    u = 2 * g + a
                    gate(pool, index_ready, u + 1, pool_passed)
                    gate(pool, summed, TPU * (u - 1), pool_passed)
                    for k in range(TPU):
                        pool.indirect_dma_start(
                            h_row[a][:, k, 0:F], None, h1_table,
                            bass.IndirectOffsetOnAxis(ap=at_dst[a][:, k:k + 1], axis=0),
                        ).then_inc(rows_in[a], 16)

                def scatter(g):
                    for a in range(2):
                        gather(g, a)
                    for a in range(2):
                        u = 2 * g + a
                        gate(pool, at_ready, u + 1, pool_passed)
                        for k in range(TPU):
                            gate(pool, total_ready, TPU * u + k + 1, pool_passed)
                            gate(pool, added[k], 16 * u, pool_passed)
                            pool.indirect_dma_start(
                                sums[k], bass.IndirectOffsetOnAxis(ap=at_src[a][:, k:k + 1], axis=0),
                                total[k][:, :], None, compute_op=ALU.add).then_inc(added[k], 16)

                rounds(pool, NG, scatter)
                for k in range(TPU):
                    pool.wait_ge(added[k], 16 * NU)

        with ExitStack() as ctx:
            def pair(name, shape):
                return [tensor(ctx, f"{name}{s}", shape) for s in range(2)]

            part = pair("part", [P, SPLITS, F + 1])
            x1 = pair("x1_in", [P, F])
            whole = pair("whole", [P, F + 1])
            degree, low = pair("degree", [P, 1]), pair("low", [P, 1])
            y, ystat, ymom = pair("y_out", [P, F]), pair("ystat_out", [P, 6]), pair("ymom_out", [P, 2])
            ydev, result = pair("ydev_out", [P, 1]), pair("result", [P, F])
            loaded = [sem(ctx, f"f_loaded{s}") for s in range(2)]
            stored = [sem(ctx, f"f_stored{s}") for s in range(2)]
            used = sem(ctx, "f_used")
            dev, rooted, ready = sem(ctx, "f_dev"), sem(ctx, "f_root"), sem(ctx, "f_ready")
            vector_step = sem(ctx, "vector_step7")
            block = ctx.enter_context(nc.Block())

            @block.sync
            def _(sp):
                def load(i, r=FULL):
                    for s in range(2):
                        t, n = 2 * i + s, r[s]
                        after(sp, used, t - 1)
                        for k in range(SPLITS):
                            sp.dma_start(part[s][0:n, k, :], rows(sums[k], t, n))\
                                .then_inc(loaded[s], 16)
                        sp.dma_start(x1[s][0:n, :], rows(x1_rows, t, n)).then_inc(loaded[s], 16)

                rounds(sp, NT // 2, load, LAST)

            @block.scalar
            def _(act):
                def tile(i, r=FULL):
                    for s in range(2):
                        t, n = 2 * i + s, r[s]
                        act.wait_ge(dev, t + 1)
                        nc.scalar.activation(ydev[s][0:n, :], ydev[s][0:n, :], ACT.Sqrt)\
                            .then_inc(rooted, 1)

                rounds(act, NT // 2, tile, LAST)

            @block.vector
            def _(dve):
                STEPS = 9

                def tile(i, r=FULL):
                    chain = Chain(dve, vector_step, 2 * STEPS * i)
                    for s in range(2):
                        t, n = 2 * i + s, r[s]
                        dve.wait_ge(loaded[s], 16 * (SPLITS + 1) * (i + 1))
                        chain.link(nc.vector.tensor_reduce(
                            whole[s][0:n, :], part[s][0:n, :, :].rearrange("p k f -> p f k"),
                            axis=AX.X, op=ALU.add))
                        chain.link(nc.vector.tensor_scalar(low[s][0:n, :], whole[s][0:n, F:F + 1], 0.5,
                                                           None, ALU.is_lt))
                        chain.link(nc.vector.tensor_tensor(degree[s][0:n, :], whole[s][0:n, F:F + 1],
                                                           low[s][0:n, :], ALU.add))
                        chain.link(nc.vector.reciprocal(degree[s][0:n, :], degree[s][0:n, :]))
                        chain.link(nc.vector.scalar_tensor_tensor(
                            out=y[s][0:n, :], in0=whole[s][0:n, 0:F], scalar=degree[s][0:n, 0:1],
                            in1=x1[s][0:n, :], op0=ALU.mult, op1=ALU.add))
                        chain.link(nc.vector.bn_stats(ystat[s][0:n, :], y[s][0:n, :]))
                        dve.sem_inc(vector_passed, 1)
                        dve.nop().then_inc(used, 1)
                        chain.link(nc.vector.bn_aggr(ymom[s][0:n, :], ystat[s][0:n, :]))
                        nc.vector.tensor_scalar(ydev[s][0:n, :], ymom[s][0:n, 1:2], EPS, None,
                                                ALU.add).then_inc(dev, 1)
                    for s in range(2):
                        t, n = 2 * i + s, r[s]
                        dve.wait_ge(rooted, t + 1)
                        after(dve, stored[s], 16 * i)
                        chain.link(nc.vector.reciprocal(ydev[s][0:n, :], ydev[s][0:n, :]))
                        chain.link(nc.vector.tensor_scalar(
                            result[s][0:n, :], y[s][0:n, :], ymom[s][0:n, 0:1], ydev[s][0:n, 0:1],
                            ALU.subtract, ALU.mult))
                        dve.nop().then_inc(ready, 1)
                    assert chain.n == 2 * STEPS

                rounds(dve, NT // 2, tile, LAST)

            @block.gpsimd
            def _(pool):
                def store(i, r=FULL):
                    for s in range(2):
                        t, n = 2 * i + s, r[s]
                        gate(pool, ready, t + 1, pool_passed)
                        pool.dma_start(rows(out, t, n), result[s][0:n, :]).then_inc(stored[s], 16)

                rounds(pool, NT // 2, store, LAST)
                for s in range(2):
                    pool.wait_ge(stored[s], 16 * (NT // 2))


_INS = ["x", "src", "dst", "edge_weight", "L0_gnn_W_ft", "L0_gnn_b_ft", "L0_gnn_W_conv",
        "L0_gnn_b_conv", "L0_gnn_velocity_factor", "L0_gnn_velocity_params", "L0_gnn_attention",
        "L0_gnn_bn_scale", "L0_gnn_bn_bias", "L0_gnn_W1", "L0_gnn_b1", "L0_gnn_ln_scale",
        "L0_gnn_ln_bias", "L0_gnn_W2", "L0_gnn_b2", "L1_gnn_W", "L1_gnn_b"]


def kernel(**inputs):
    import numpy as _np
    import concourse.bacc as _bacc
    from concourse import mybir as _mybir
    from concourse.bass_utils import run_bass_kernel_spmd as _run

    nc = _bacc.Bacc("TRN2", target_bir_lowering=False, num_devices=1)
    arrays, args = {}, []
    for name in _INS:
        a = _np.ascontiguousarray(inputs[name])
        if a.ndim == 0:
            a = a.reshape(1)
        arrays[f"in_{name}"] = a
        args.append(nc.dram_tensor(f"in_{name}", a.shape, _mybir.dt.from_np(a.dtype),
                                   kind="ExternalInput").ap())
    shape = arrays["in_x"].shape
    args.append(nc.dram_tensor("out_x", shape, _mybir.dt.float32, kind="ExternalOutput").ap())
    resnorm_gnn(nc, *args)
    r = _run(nc, [arrays], core_ids=[0])
    return r.results[0]["out_x"]
```

```python
import concourse.bass as bass
from concourse import mybir
from contextlib import ExitStack

P = 128
F = 128
VIEWS = 4
ROW = 132
TPU = 5
WIN = 64
SPAN = 128
CHUNK = 250
SPLITS = TPU
FP32 = mybir.dt.float32
BF16 = mybir.dt.bfloat16
I32 = mybir.dt.int32
ALU = mybir.AluOpType
ACT = mybir.ActivationFunctionType
AX = mybir.AxisListType
FULL = (P, P)


def after(eng, sem, value):
    if isinstance(value, int) and value <= 0:
        return
    eng.wait_ge(sem, value)


def rounds(eng, n, body, last=None, full=FULL):
    extra = () if last is None else (full,)
    body(0, *extra)
    if n > 2:
        with eng.Fori(1, n - 1) as i:
            body(i, *extra)
    body(n - 1, *(() if last is None else (last,)))


def gate(eng, sem, value, passed):
    if isinstance(value, int) and value <= 0:
        return
    eng.wait_ge(sem, value)
    eng.sem_inc(passed, 1)


class Chain:

    def __init__(self, eng, sem, base=0):
        self.eng, self.sem, self.base, self.n = eng, sem, base, 0

    def link(self, instruction):
        instruction.then_inc(self.sem, 1)
        self.n += 1
        self.eng.wait_ge(self.sem, self.base + self.n)


def resnorm_gnn(nc, x, src, dst, edge_weight, W_ft, b_ft, W_conv, b_conv, velocity_factor,
                velocity_params, attention, bn_scale, bn_bias, W1, b1, ln_scale, ln_bias, W2, b2,
                L1_W, L1_b, out):
    N, E = x.shape[0], src.shape[0]
    NT = -(-N // P)
    assert NT % 2 == 0
    LAST = (P, N - (NT - 1) * P)
    UE = TPU * P
    NU = 2 * -(-E // (2 * UE))
    NG = NU // 2
    FU = E // UE
    TAIL = (E - FU * UE) // TPU
    assert TAIL * TPU == E - FU * UE and TAIL % 32 == 0 and NU - FU <= 2
    assert N % CHUNK == 0 and N // CHUNK % 2 == 0 and N <= 2 ** 15 and NU <= 512
    Z = W1.shape[1]
    ZB = Z // P
    EPS = 1e-5
    SUM_ROWS = NT * P + P

    node_table = nc.dram_tensor("node_table", [N, ROW], FP32).ap()
    pos_table = nc.dram_tensor("pos_table", [N, 4], FP32).ap()
    gathered = nc.dram_tensor("gathered", [NU, P, TPU * ROW], FP32).ap()
    agg = nc.dram_tensor("agg", [SUM_ROWS, VIEWS * F], FP32).ap()
    aggT = nc.dram_tensor("aggT", [F, VIEWS, N], FP32).ap()
    h1_table = nc.dram_tensor("h1_table", [N, F], FP32).ap()
    sums = [nc.dram_tensor(f"sums{k}", [SUM_ROWS, F + 1], FP32).ap() for k in range(SPLITS)]
    x1_rows = nc.dram_tensor("x1_rows", [N, F], FP32).ap()

    top = ExitStack()
    with top:
        def tensor(ctx, name, shape, dt=FP32):
            return ctx.enter_context(nc.sbuf_tensor(name, shape, dt))

        def bank(ctx, name, shape):
            return ctx.enter_context(nc.psum_tensor(name, shape, FP32))

        of_stage = {}

        def end_stage(sems):
            nc.clear_and_free_semaphores(sems)
            nc.all_engine_barrier()

        def sem(ctx, name):
            if ctx not in of_stage:
                of_stage[ctx] = []
                ctx.callback(end_stage, of_stage[ctx])
            of_stage[ctx].append(nc.alloc_semaphore(name))
            return of_stage[ctx][-1]

        pool_passed = sem(top, "pool_passed")
        vector_passed = sem(top, "vector_passed")
        ident = tensor(top, "ident", [P, P])
        earlier = tensor(top, "earlier", [P, P])
        ones = tensor(top, "ones", [1, P])
        trash = tensor(top, "trash", [P, 1])
        trash_i = tensor(top, "trash_i", [P, 1], I32)
        w_ft = tensor(top, "w_ft", [P, F])
        w_conv = tensor(top, "w_conv", [P, ROW])
        bias_conv = tensor(top, "bias_conv", [1, ROW])
        b_ft_c = tensor(top, "b_ft_c", [P, 1])
        w1 = tensor(top, "w1", [P, VIEWS, Z])
        b1_r = tensor(top, "b1_r", [1, Z])
        w2 = tensor(top, "w2", [P, ZB, F])
        b2_r = tensor(top, "b2_r", [1, F])
        ln_s = tensor(top, "ln_s", [P, ZB])
        ln_b = tensor(top, "ln_b", [P, ZB])
        bn_s = tensor(top, "bn_s", [P, VIEWS])
        bn_b = tensor(top, "bn_b", [P, VIEWS])
        att = tensor(top, "att", [VIEWS, F])
        l1_w = tensor(top, "l1_w", [P, F])
        l1_b = tensor(top, "l1_b", [1, F])
        v_obs = tensor(top, "v_obs", [P, VIEWS])
        v_fac = tensor(top, "v_fac", [P, 1])
        src_i = tensor(top, "src_i", [P, NU * TPU], I32)
        dst_i = tensor(top, "dst_i", [P, NU * TPU], I32)
        ew = tensor(top, "ew", [P, NU * TPU])
        dist = tensor(top, "dist", [P, NU * TPU])
        dirs = tensor(top, "dirs", [P, NU * TPU])
        aberr = tensor(top, "aberr", [P, VIEWS, NU * TPU])

        slot = tensor(top, "slot", [P, NU * TPU])
        slot_b = tensor(top, "slot_b", [P, NU * TPU], BF16)
        src_lo = tensor(top, "src_lo", [P, NU * TPU], BF16)
        src_hi = tensor(top, "src_hi", [P, NU * TPU], BF16)
        ident_b = tensor(top, "ident_b", [P, P], BF16)
        count_p = tensor(top, "count_p", [P, 1])
        count_f = tensor(top, "count_f", [P, WIN])
        unit_base = tensor(top, "unit_base", [1, NU], I32)
        span_base = tensor(top, "span_base", [1, NG], I32)
        unit_off = tensor(top, "unit_off", [1, NU], I32)
        sorted_flag = tensor(top, "sorted_flag", [1, 1], I32)

        def rows(table, t, r):
            return table[bass.ds(t * P, r), :]

        def pads(dve, chain, held):
            if TAIL:
                chain.link(nc.vector.memset(held[TAIL:P, FU * TPU:(FU + 1) * TPU]
                                            if len(held.shape) == 2 else
                                            held[TAIL:P, :, FU * TPU:(FU + 1) * TPU], 0.0))
            if NU > FU + (TAIL > 0):
                at = (FU + (TAIL > 0)) * TPU
                chain.link(nc.vector.memset(held[:, at:NU * TPU] if len(held.shape) == 2 else
                                            held[:, :, at:NU * TPU], 0.0))

        ZEROS = 5000
        SR, SLAST = -(-NG // 2), 2 - NG % 2
        VECTOR_VIEWS, SCALAR_VIEWS, POOL_VIEWS = (0, 1), (2,), (3,)

        def is_sorted():
            return nc.values_load(sorted_flag[0:1, 0:1], min_val=0, max_val=1) == 1

        def by_partition(table):
            return table.rearrange("n f -> (n f)").rearrange("(p m) -> p m", p=P)

        def clears(tables, zeros):
            for table in tables:
                for at in range(0, table.shape[1], ZEROS):
                    m = min(table.shape[1] - at, ZEROS)
                    yield table[:, at:at + m], zeros[:, 0:m]

        with ExitStack() as ctx:
            x_in = [tensor(ctx, f"x_in{s}", [P, F]) for s in range(2)]
            xT = [tensor(ctx, f"xT{s}", [P, P]) for s in range(2)]
            hT = [tensor(ctx, f"hT{s}", [P, P]) for s in range(2)]
            row_out = [tensor(ctx, f"row_out{s}", [P, ROW]) for s in range(2)]
            pt = [bank(ctx, f"pt{s}", [P, P]) for s in range(2)]
            ph = [bank(ctx, f"ph{s}", [P, P]) for s in range(2)]
            pr = [bank(ctx, f"pr{s}", [P, ROW]) for s in range(2)]
            cleared = sem(ctx, "cleared")
            pads_cleared = sem(ctx, "pads_cleared")
            masks_cleared = sem(ctx, "masks_cleared")
            ones_written = sem(ctx, "ones_written")
            constants = sem(ctx, "constants")
            weights_in = sem(ctx, "weights_in")
            edges_in = sem(ctx, "edges_in")
            trash_written = sem(ctx, "trash_written")
            x_loaded = [sem(ctx, f"x_loaded{s}") for s in range(2)]
            x_transposed = sem(ctx, "x_transposed")
            xT_ready = sem(ctx, "xT_ready")
            h_summed = sem(ctx, "h_summed")
            hT_ready = sem(ctx, "hT_ready")
            row_summed = sem(ctx, "row_summed")
            row_ready = sem(ctx, "row_ready")
            row_stored = [sem(ctx, f"row_stored{s}") for s in range(2)]
            block = ctx.enter_context(nc.Block())
            EARLY = 4

            @block.sync
            def _(sp):
                sp.wait_ge(cleared, 2)
                sp.dma_start(w_ft[:, :], W_ft).then_inc(weights_in, 16)
                sp.dma_start(w_conv[:, 0:F], W_conv).then_inc(weights_in, 16)
                sp.dma_start(bias_conv[:, 0:F], b_conv.unsqueeze(0)).then_inc(weights_in, 16)
                sp.dma_start(b_ft_c[:, :], b_ft.unsqueeze(1)).then_inc(weights_in, 16)

                def load(i, r=FULL):
                    for s in range(2):
                        t = 2 * i + s
                        after(sp, x_transposed, t - 1)
                        sp.dma_start(x_in[s][0:r[s], :], rows(x, t, r[s])).then_inc(x_loaded[s], 16)

                rounds(sp, NT // 2, load, LAST)

            @block.gpsimd
            def _(pool):
                nc.gpsimd.memset(w_conv[:, F:ROW], 0.0).then_inc(cleared, 1)
                nc.gpsimd.memset(bias_conv[:, F:ROW], 0.0).then_inc(cleared, 1)
                nc.gpsimd.memset(ident[:, :], 0.0).then_inc(masks_cleared, 1)
                nc.gpsimd.memset(earlier[:, :], 1.0).then_inc(masks_cleared, 1)
                pool.wait_ge(masks_cleared, 2)
                pool.wait_ge(cleared, 2)
                nc.gpsimd.affine_select(out=ident[:, :], in_=ident[:, :], compare_op=ALU.not_equal,
                                        fill=1.0, base=0, pattern=[[-1, P]],
                                        channel_multiplier=1).then_inc(constants, 1)
                nc.gpsimd.affine_select(out=w_conv[:, F:F + 3], in_=w_conv[:, F:F + 3],
                                        compare_op=ALU.not_equal, fill=1.0, base=0,
                                        pattern=[[-1, 3]], channel_multiplier=1).then_inc(constants, 1)
                nc.gpsimd.affine_select(out=earlier[:, :], in_=earlier[:, :], compare_op=ALU.is_gt,
                                        fill=0.0, base=0, pattern=[[-1, P]],
                                        channel_multiplier=1).then_inc(constants, 1)
                nc.gpsimd.iota(trash_i[:, :], [[0, 1]], base=NT * P, channel_multiplier=1)\
                    .then_inc(trash_written, 1)
                pool.wait_ge(trash_written, 1)
                nc.gpsimd.tensor_copy(trash[:, :], trash_i[:, :])

                def store(i, r=FULL):
                    for s in range(2):
                        t = 2 * i + s
                        gate(pool, row_ready, t + 1, pool_passed)
                        pool.dma_start(rows(node_table, t, r[s]), row_out[s][0:r[s], :])\
                            .then_inc(row_stored[s], 16)
                        pool.dma_start(rows(pos_table, t, r[s]), row_out[s][0:r[s], F:ROW])\
                            .then_inc(row_stored[s], 16)

                rounds(pool, NT // 2, store, LAST)
                for s in range(2):
                    pool.wait_ge(row_stored[s], 32 * (NT // 2))

            @block.tensor
            def _(pe):
                pe.wait_ge(constants, 3)
                pe.wait_ge(ones_written, 1)
                pe.wait_ge(weights_in, 16 * EARLY)

                def tile(i, r=FULL):
                    for s in range(2):
                        t = 2 * i + s
                        pe.wait_ge(x_loaded[s], 16 * (i + 1))
                        after(pe, xT_ready, t - 1)
                        nc.tensor.transpose(pt[s][:, 0:r[s]], x_in[s][0:r[s], :],
                                            ident[0:r[s], 0:r[s]]).then_inc(x_transposed, 1)
                    for s in range(2):
                        t = 2 * i + s
                        pe.wait_ge(xT_ready, t + 1)
                        after(pe, hT_ready, t - 1)
                        nc.tensor.matmul(ph[s][:, 0:r[s]], w_ft[:, :], xT[s][:, 0:r[s]], start=True,
                                         stop=True).then_inc(h_summed, 1)
                    for s in range(2):
                        t = 2 * i + s
                        pe.wait_ge(hT_ready, t + 1)
                        after(pe, row_ready, t - 1)
                        nc.tensor.matmul(pr[s][0:r[s], :], hT[s][:, 0:r[s]], w_conv[:, :],
                                         start=True, stop=False)
                        nc.tensor.matmul(pr[s][0:r[s], :], ones[:, 0:r[s]], bias_conv[:, :],
                                         start=False, stop=True).then_inc(row_summed, 1)

                rounds(pe, NT // 2, tile, LAST)

            @block.scalar
            def _(act):
                act.dma_start(w1[:, :, :], W1.rearrange("(v p) z -> p v z", p=P)).then_inc(edges_in, 16)
                act.dma_start(w2[:, :, :], W2.rearrange("(v p) z -> p v z", p=P)).then_inc(edges_in, 16)
                act.dma_start(b1_r[:, :], b1.unsqueeze(0)).then_inc(edges_in, 16)
                act.dma_start(b2_r[:, :], b2.unsqueeze(0)).then_inc(edges_in, 16)
                act.dma_start(l1_b[:, :], L1_b.unsqueeze(0)).then_inc(edges_in, 16)
                act.dma_start(l1_w[:, :], L1_W).then_inc(edges_in, 16)
                act.dma_start(att[:, :], attention).then_inc(edges_in, 16)
                for v in range(VIEWS):
                    act.dma_start(bn_s[:, v:v + 1], bn_scale[v].unsqueeze(1)).then_inc(edges_in, 16)
                    act.dma_start(bn_b[:, v:v + 1], bn_bias[v].unsqueeze(1)).then_inc(edges_in, 16)
                for b in range(ZB):
                    act.dma_start(ln_s[:, b:b + 1], ln_scale[b * P:(b + 1) * P].unsqueeze(1))\
                        .then_inc(edges_in, 16)
                    act.dma_start(ln_b[:, b:b + 1], ln_bias[b * P:(b + 1) * P].unsqueeze(1))\
                        .then_inc(edges_in, 16)
                act.dma_start(v_obs[:, :], velocity_params.unsqueeze(0).broadcast_to([P, VIEWS]))\
                    .then_inc(edges_in, 16)
                act.dma_start(v_fac[:, :], velocity_factor.unsqueeze(0).broadcast_to([P, 1]))\
                    .then_inc(edges_in, 16)
                act.wait_ge(pads_cleared, 3)
                for held, given in ((src_i, src), (dst_i, dst), (ew, edge_weight)):
                    act.dma_start(held[:, 0:FU * TPU].rearrange("p (u k) -> p u k", k=TPU),
                                  given[0:FU * UE].rearrange("(u p k) -> p u k", p=P, k=TPU))\
                        .then_inc(edges_in, 16)
                    if TAIL:
                        act.dma_start(held[0:TAIL, FU * TPU:(FU + 1) * TPU],
                                      given[FU * UE:E].rearrange("(p k) -> p k", k=TPU))\
                            .then_inc(edges_in, 16)
                act.wait_ge(weights_in, 16 * EARLY)

                def tile(i, r=FULL):
                    for s in range(2):
                        t = 2 * i + s
                        act.wait_ge(x_transposed, t + 1)
                        after(act, h_summed, t - 1)
                        nc.scalar.copy(xT[s][:, 0:r[s]], pt[s][:, 0:r[s]]).then_inc(xT_ready, 1)
                    for s in range(2):
                        t = 2 * i + s
                        act.wait_ge(h_summed, t + 1)
                        after(act, row_summed, t - 1)
                        nc.scalar.activation(hT[s][:, 0:r[s]], ph[s][:, 0:r[s]], ACT.Relu,
                                             bias=b_ft_c[:, 0:1]).then_inc(hT_ready, 1)

                rounds(act, NT // 2, tile, LAST)
                act.wait_ge(edges_in, 16 * (9 + 2 * VIEWS + 2 * ZB + 3 * (1 + (TAIL > 0))))

            @block.vector
            def _(dve):
                nc.vector.memset(ones[:, :], 1.0).then_inc(ones_written, 1)
                for held in (src_i, dst_i, ew):
                    nc.vector.memset(held[:, FU * TPU:NU * TPU], 0).then_inc(pads_cleared, 1)

                def tile(i, r=FULL):
                    for s in range(2):
                        t = 2 * i + s
                        dve.wait_ge(row_summed, t + 1)
                        after(dve, row_stored[s], 32 * i)
                        nc.vector.tensor_copy(row_out[s][0:r[s], :], pr[s][0:r[s], :])\
                            .then_inc(row_ready, 1)

                rounds(dve, NT // 2, tile, LAST)

        with ExitStack() as ctx:
            first = tensor(ctx, "first", [1, NU])
            first2 = tensor(ctx, "first2", [1, NG])
            offset = tensor(ctx, "offset", [1, NU])
            half_i = tensor(ctx, "half_i", [P, NU * TPU], I32)
            count_i = tensor(ctx, "count_i", [P, 1 + WIN], I32)
            over = tensor(ctx, "over", [P, 4])
            worst = tensor(ctx, "worst", [P, 1])
            worst_all = tensor(ctx, "worst_all", [P, 1])
            pb = bank(ctx, "pb_base", [P, NU])
            vector_step = sem(ctx, "vector_step0")
            first_ready = sem(ctx, "first_ready")
            first_spread = sem(ctx, "first_spread")
            counts_ready = sem(ctx, "counts_ready")
            worst_ready = sem(ctx, "worst_ready")
            worst_shared = sem(ctx, "worst_shared")
            block = ctx.enter_context(nc.Block())

            @block.tensor
            def _(pe):
                pe.wait_ge(first_ready, 1)
                nc.tensor.matmul(pb[:, :], ones[:, :], first[:, :], start=True, stop=True)\
                    .then_inc(first_spread, 1)

            @block.gpsimd
            def _(pool):
                nc.gpsimd.iota(count_i[:, 0:1], [[0, 1]], base=0, channel_multiplier=1)\
                    .then_inc(counts_ready, 1)
                nc.gpsimd.iota(count_i[:, 1:1 + WIN], [[1, WIN]], base=0, channel_multiplier=0)\
                    .then_inc(counts_ready, 1)
                pool.wait_ge(worst_ready, 1)
                nc.gpsimd.partition_all_reduce(worst_all[:, :], worst[:, :], P,
                                               bass.bass_isa.ReduceOp.max).then_inc(worst_shared, 1)

            @block.vector
            def _(dve):
                chain = Chain(dve, vector_step)
                firsts = dst_i[0:1, :].rearrange("p (u k) -> p u k", k=TPU)[:, :, 0]
                chain.link(nc.vector.tensor_scalar(first[:, :], firsts, float(N - WIN), None, ALU.min))
                if NU > FU + (TAIL > 0):
                    chain.link(nc.vector.tensor_copy(first[:, NU - 1:NU], first[:, NU - 2:NU - 1]))
                dve.nop().then_inc(first_ready, 1)
                by_two = first[:, :].rearrange("p (g a) -> p g a", a=2)
                chain.link(nc.vector.tensor_scalar(first2[:, :], by_two[:, :, 0], float(N - SPAN),
                                                   None, ALU.min))
                chain.link(nc.vector.tensor_tensor(
                    offset[:, :].rearrange("p (g a) -> p g a", a=2), by_two,
                    first2[:, :].unsqueeze(2).to_broadcast([1, NG, 2]), ALU.subtract))
                nc.vector.tensor_copy(unit_base[:, :], first[:, :])
                nc.vector.tensor_copy(span_base[:, :], first2[:, :])
                nc.vector.tensor_copy(unit_off[:, :], offset[:, :])
                nc.vector.tensor_copy(ident_b[:, :], ident[:, :])
                for half, bits in ((src_lo, P - 1), (src_hi, 2 ** 15 - P)):
                    chain.link(nc.vector.tensor_scalar(half_i[:, :], src_i[:, :], bits, None,
                                                       ALU.bitwise_and))
                    chain.link(nc.vector.tensor_copy(half[:, :], half_i[:, :]))
                dve.wait_ge(counts_ready, 2)
                nc.vector.tensor_copy(count_p[:, :], count_i[:, 0:1])
                nc.vector.tensor_copy(count_f[:, :], count_i[:, 1:1 + WIN])
                dve.wait_ge(first_spread, 1)
                by_unit = slot[:, :].rearrange("p (u k) -> p u k", k=TPU)
                chain.link(nc.vector.tensor_tensor(
                    by_unit, dst_i[:, :].rearrange("p (u k) -> p u k", k=TPU),
                    pb[:, :].unsqueeze(2).to_broadcast([P, NU, TPU]), ALU.subtract))
                pads(dve, chain, slot[:, :])
                chain.link(nc.vector.tensor_copy(slot_b[:, :], slot[:, :]))
                chain.link(nc.vector.memset(over[:, :], -1.0))
                chain.link(nc.vector.tensor_reduce(over[:, 0:1], slot[:, :], axis=AX.X, op=ALU.max))
                chain.link(nc.vector.tensor_reduce(over[:, 1:2], slot[:, :], axis=AX.X, op=ALU.min))
                chain.link(nc.vector.tensor_reduce(over[0:1, 2:3], offset[:, :], axis=AX.X, op=ALU.max))
                chain.link(nc.vector.tensor_reduce(over[0:1, 3:4], offset[:, :], axis=AX.X, op=ALU.min))
                chain.link(nc.vector.tensor_scalar(over[:, 0:1], over[:, 0:1], -float(WIN - 1), None,
                                                   ALU.add))
                chain.link(nc.vector.tensor_scalar(over[:, 1:2], over[:, 1:2], -1.0, None, ALU.mult))
                chain.link(nc.vector.tensor_scalar(over[0:1, 2:3], over[0:1, 2:3],
                                                   -float(SPAN - WIN), None, ALU.add))
                chain.link(nc.vector.tensor_scalar(over[0:1, 3:4], over[0:1, 3:4], -1.0, None,
                                                   ALU.mult))
                chain.link(nc.vector.tensor_reduce(worst[:, :], over[:, :], axis=AX.X, op=ALU.max))
                dve.nop().then_inc(worst_ready, 1)
                dve.wait_ge(worst_shared, 1)
                chain.link(nc.vector.tensor_scalar(sorted_flag[:, :], worst_all[0:1, :], 0.0, None,
                                                   ALU.is_le))

        with nc.If(is_sorted()):
            with ExitStack() as ctx:
                zeros = tensor(ctx, "w_zeros", [P, ZEROS])
                at_src = [tensor(ctx, f"w_at_src{a}", [P, TPU], I32) for a in range(2)]
                slots = [tensor(ctx, f"w_slots{a}", [P, TPU], BF16) for a in range(2)]
                src_row = [tensor(ctx, f"w_src_row{a}", [P, TPU, ROW]) for a in range(2)]
                pos_win = [tensor(ctx, f"w_pos_win{a}", [WIN, 4]) for a in range(2)]
                pick = [tensor(ctx, f"w_pick{a}", [WIN, TPU * P]) for a in range(2)]
                dpos = [tensor(ctx, f"w_dpos{a}", [P, TPU, 3]) for a in range(2)]
                square = [tensor(ctx, f"w_square{a}", [P, TPU, 3]) for a in range(2)]
                pr = [bank(ctx, f"w_pr{a}", [P, 1024]) for a in range(2)]
                pd = [bank(ctx, f"w_pd{a}", [P, TPU, 4]) for a in range(2)]
                zeros_ready = sem(ctx, "w_zeros_ready")
                tables_zeroed = sem(ctx, "w_tables_zeroed")
                index_ready = sem(ctx, "w_index_ready")
                slots_ready = sem(ctx, "w_slots_ready")
                window_in = [sem(ctx, f"w_window_in{a}") for a in range(2)]
                slots_spread = sem(ctx, "w_slots_spread")
                pick_ready = sem(ctx, "w_pick_ready")
                picked = sem(ctx, "w_picked")
                rows_in = [sem(ctx, f"w_rows_in{a}") for a in range(2)]
                rows_out = [sem(ctx, f"w_rows_out{a}") for a in range(2)]
                measured = sem(ctx, "w_measured")
                vector_step = sem(ctx, "w_vector_step")
                block = ctx.enter_context(nc.Block())

                @block.sync
                def _(sp):
                    sp.wait_ge(zeros_ready, 1)
                    n = 0
                    for to, of in clears([aggT.rearrange("f v n -> f (v n)"), *map(by_partition, sums)], zeros):
                        sp.dma_start(to, of).then_inc(tables_zeroed, 16)
                        n += 1

                    def unit(g):
                        for a in range(2):
                            u = 2 * g + a
                            after(sp, picked, u - 1)
                            base = sp.value_load(unit_base[0:1, bass.ds(u, 1)], min_val=0,
                                                 max_val=N - WIN)
                            sp.dma_start(pos_win[a][:, :], pos_table[bass.ds(base, WIN), :])\
                                .then_inc(window_in[a], 16)
                        for a in range(2):
                            sp.wait_ge(rows_in[a], 16 * TPU * (g + 1))
                            sp.dma_start(gathered[bass.ds(2 * g + a, 1), :, :].rearrange("a p m -> (a p) m"),
                                         src_row[a][:, :, :].rearrange("p k f -> p (k f)"))\
                                .then_inc(rows_out[a], 16)

                    rounds(sp, NG, unit)
                    for a in range(2):
                        sp.wait_ge(rows_out[a], 16 * NG)
                    sp.wait_ge(tables_zeroed, 16 * n)

                @block.gpsimd
                def _(pool):
                    def gather(g):
                        for a in range(2):
                            u = 2 * g + a
                            gate(pool, index_ready, u + 1, pool_passed)
                            gate(pool, rows_out[a], 16 * g, pool_passed)
                            gate(pool, measured, u - 1, pool_passed)
                            for k in range(TPU):
                                pool.indirect_dma_start(
                                    src_row[a][:, k, :], None, node_table,
                                    bass.IndirectOffsetOnAxis(ap=at_src[a][:, k:k + 1], axis=0),
                                ).then_inc(rows_in[a], 16)

                    rounds(pool, NG, gather)

                @block.scalar
                def _(act):
                    def indices(g):
                        for a in range(2):
                            u = 2 * g + a
                            after(act, slots_spread, u - 1)
                            nc.scalar.copy(slots[a][:, :], slot_b[:, bass.ds(u * TPU, TPU)])\
                                .then_inc(slots_ready, 1)
                            after(act, rows_in[a], 16 * TPU * g)
                            nc.scalar.copy(at_src[a][:, :], src_i[:, bass.ds(u * TPU, TPU)])\
                                .then_inc(index_ready, 1)

                    rounds(act, NG, indices)

                @block.tensor
                def _(pe):
                    def unit(g):
                        for a in range(2):
                            u = 2 * g + a
                            pe.wait_ge(slots_ready, u + 1)
                            after(pe, pick_ready, u - 1)
                            for k in range(TPU):
                                last = nc.tensor.matmul(pr[a][0:WIN, k * P:(k + 1) * P],
                                                        slots[a][:, k:k + 1].to_broadcast([P, WIN]),
                                                        ident_b[:, :], start=True, stop=True)
                            last.then_inc(slots_spread, 1)
                            pe.wait_ge(pick_ready, u + 1)
                            pe.wait_ge(window_in[a], 16 * (g + 1))
                            after(pe, measured, u - 1)
                            for k in range(TPU):
                                last = nc.tensor.matmul(pd[a][:, k, 0:3], pick[a][:, k * P:(k + 1) * P],
                                                        pos_win[a][:, 0:3], start=True, stop=True)
                            last.then_inc(picked, 1)

                    rounds(pe, NG, unit)

                @block.vector
                def _(dve):
                    nc.vector.memset(zeros[:, :], 0.0).then_inc(zeros_ready, 1)

                    def measure(g):
                        for a in range(2):
                            u = 2 * g + a
                            dve.wait_ge(slots_spread, u + 1)
                            after(dve, picked, u - 1)
                            nc.vector.tensor_scalar(pick[a][:, :], pr[a][0:WIN, 0:TPU * P],
                                                    count_p[0:WIN, 0:1], None, ALU.is_equal)\
                                .then_inc(pick_ready, 1)
                        for a in range(2):
                            u = 2 * g + a
                            chain = Chain(dve, vector_step, 3 * u)
                            dve.wait_ge(picked, u + 1)
                            dve.wait_ge(rows_in[a], 16 * TPU * (g + 1))
                            chain.link(nc.vector.tensor_tensor(dpos[a][:, :, :], src_row[a][:, :, F:F + 3],
                                                               pd[a][:, :, 0:3], ALU.subtract))
                            chain.link(nc.vector.tensor_tensor(square[a][:, :, :], dpos[a][:, :, :],
                                                               dpos[a][:, :, :], ALU.mult))
                            nc.vector.tensor_reduce(dist[:, bass.ds(u * TPU, TPU)], square[a][:, :, :],
                                                    axis=AX.X, op=ALU.add)
                            chain.link(nc.vector.tensor_reduce(dirs[:, bass.ds(u * TPU, TPU)],
                                                               dpos[a][:, :, :], axis=AX.X, op=ALU.add))
                            dve.nop().then_inc(measured, 1)

                    rounds(dve, NG, measure)

        with nc.Else():
            with ExitStack() as ctx:
                zeros = tensor(ctx, "zeros", [P, ZEROS])
                at_src = [tensor(ctx, f"at_src{a}", [P, TPU], I32) for a in range(2)]
                at_dst = [tensor(ctx, f"at_dst{a}", [P, TPU], I32) for a in range(2)]
                src_row = [tensor(ctx, f"src_row{a}", [P, TPU, ROW]) for a in range(2)]
                dst_pos = [tensor(ctx, f"dst_pos{a}", [P, TPU, 4]) for a in range(2)]
                dpos = tensor(ctx, "dpos", [P, TPU, 3])
                square = tensor(ctx, "square", [P, TPU, 3])
                zeros_ready = sem(ctx, "zeros_ready")
                tables_zeroed = sem(ctx, "tables_zeroed")
                index_ready = sem(ctx, "index_ready")
                rows_in = [sem(ctx, f"rows_in{a}") for a in range(2)]
                rows_out = [sem(ctx, f"rows_out{a}") for a in range(2)]
                measured = sem(ctx, "measured")
                vector_step = sem(ctx, "vector_step")
                block = ctx.enter_context(nc.Block())
                @block.sync
                def _(sp):
                    sp.wait_ge(zeros_ready, 1)
                    n = 0
                    for to, of in clears([by_partition(t) for t in (agg, *sums)], zeros):
                        sp.dma_start(to, of).then_inc(tables_zeroed, 16)
                        n += 1

                    def store(g):
                        for a in range(2):
                            sp.wait_ge(rows_in[a], 16 * 2 * TPU * (g + 1))
                            sp.dma_start(gathered[2 * g + a, :, :].squeeze() if isinstance(g, int) else
                                         gathered[bass.ds(2 * g + a, 1), :, :].rearrange("a p m -> (a p) m"),
                                         src_row[a][:, :, :].rearrange("p k f -> p (k f)"))\
                                .then_inc(rows_out[a], 16)

                    rounds(sp, NG, store)
                    for a in range(2):
                        sp.wait_ge(rows_out[a], 16 * NG)
                    sp.wait_ge(tables_zeroed, 16 * n)

                @block.gpsimd
                def _(pool):
                    def gather(g):
                        for a in range(2):
                            u = 2 * g + a
                            gate(pool, index_ready, 2 * (u + 1), pool_passed)
                            gate(pool, rows_out[a], 16 * g, pool_passed)
                            gate(pool, measured, u - 1, pool_passed)
                            for k in range(TPU):
                                pool.indirect_dma_start(
                                    src_row[a][:, k, :], None, node_table,
                                    bass.IndirectOffsetOnAxis(ap=at_src[a][:, k:k + 1], axis=0),
                                ).then_inc(rows_in[a], 16)
                                pool.indirect_dma_start(
                                    dst_pos[a][:, k, :], None, pos_table,
                                    bass.IndirectOffsetOnAxis(ap=at_dst[a][:, k:k + 1], axis=0),
                                ).then_inc(rows_in[a], 16)

                    rounds(pool, NG, gather)

                @block.scalar
                def _(act):
                    def indices(g):
                        for a in range(2):
                            u = 2 * g + a
                            after(act, rows_in[a], 16 * 2 * TPU * g)
                            nc.scalar.copy(at_src[a][:, :], src_i[:, bass.ds(u * TPU, TPU)])\
                                .then_inc(index_ready, 1)
                            nc.scalar.copy(at_dst[a][:, :], dst_i[:, bass.ds(u * TPU, TPU)])\
                                .then_inc(index_ready, 1)

                    rounds(act, NG, indices)

                @block.vector
                def _(dve):
                    nc.vector.memset(zeros[:, :], 0.0).then_inc(zeros_ready, 1)

                    def measure(g):
                        for a in range(2):
                            u = 2 * g + a
                            chain = Chain(dve, vector_step, 3 * u)
                            dve.wait_ge(rows_in[a], 16 * 2 * TPU * (g + 1))
                            chain.link(nc.vector.tensor_tensor(dpos[:, :, :], src_row[a][:, :, F:F + 3],
                                                               dst_pos[a][:, :, 0:3], ALU.subtract))
                            chain.link(nc.vector.tensor_tensor(square[:, :, :], dpos[:, :, :],
                                                               dpos[:, :, :], ALU.mult))
                            nc.vector.tensor_reduce(dist[:, bass.ds(u * TPU, TPU)], square[:, :, :],
                                                    axis=AX.X, op=ALU.add)
                            chain.link(nc.vector.tensor_reduce(dirs[:, bass.ds(u * TPU, TPU)],
                                                               dpos[:, :, :], axis=AX.X, op=ALU.add))
                            dve.nop().then_inc(measured, 1)

                    rounds(dve, NG, measure)

        with ExitStack() as ctx:
            far = tensor(ctx, "far", [P, 1])
            far_all = tensor(ctx, "far_all", [P, 1])
            near = tensor(ctx, "near", [P, 1])
            work = tensor(ctx, "work", [P, NU * TPU])
            speed = tensor(ctx, "speed", [P, NU * TPU])
            root = tensor(ctx, "root", [P, NU * TPU])
            vector_step = sem(ctx, "vector_step2")
            squares_ready = sem(ctx, "squares_ready")
            dist_ready = sem(ctx, "dist_ready")
            far_ready = sem(ctx, "far_ready")
            far_shared = sem(ctx, "far_shared")
            rest_ready = sem(ctx, "rest_ready")
            root_ready = sem(ctx, "root_ready")
            block = ctx.enter_context(nc.Block())

            @block.scalar
            def _(act):
                act.wait_ge(squares_ready, 1)
                nc.scalar.activation(dist[:, :], dist[:, :], ACT.Sqrt).then_inc(dist_ready, 1)
                for v in range(VIEWS):
                    act.wait_ge(rest_ready, v + 1)
                    nc.scalar.activation(root[:, :], root[:, :], ACT.Sqrt).then_inc(root_ready, 1)

            @block.gpsimd
            def _(pool):
                pool.wait_ge(far_ready, 1)
                nc.gpsimd.partition_all_reduce(far_all[:, :], far[:, :], P,
                                               bass.bass_isa.ReduceOp.max).then_inc(far_shared, 1)

            @block.vector
            def _(dve):
                chain = Chain(dve, vector_step)
                pads(dve, chain, dist[:, :])
                chain.link(nc.vector.tensor_scalar(dist[:, :], dist[:, :], 1e-32, None, ALU.max))
                dve.nop().then_inc(squares_ready, 1)
                dve.wait_ge(dist_ready, 1)
                nc.vector.tensor_reduce(far[:, :], dist[:, :], axis=AX.X, op=ALU.max)\
                    .then_inc(far_ready, 1)
                chain.link(nc.vector.tensor_scalar(work[:, :], dist[:, :], 1e-8, None, ALU.add))
                chain.link(nc.vector.reciprocal(work[:, :], work[:, :]))
                chain.link(nc.vector.tensor_tensor(dirs[:, :], dirs[:, :], work[:, :], ALU.mult))
                dve.wait_ge(far_shared, 1)
                chain.link(nc.vector.reciprocal(near[:, :], far_all[:, :]))
                chain.link(nc.vector.tensor_scalar(dist[:, :], dist[:, :], near[:, 0:1], None, ALU.mult))
                for v in range(VIEWS):
                    chain.link(nc.vector.tensor_scalar(speed[:, :], dist[:, :], v_obs[:, v:v + 1],
                                                       v_fac[:, 0:1], ALU.min, ALU.mult))
                    chain.link(nc.vector.tensor_tensor(root[:, :], speed[:, :], speed[:, :], ALU.mult))
                    chain.link(nc.vector.tensor_scalar(root[:, :], root[:, :], -1.0, 1.0, ALU.mult,
                                                       ALU.add))
                    dve.nop().then_inc(rest_ready, 1)
                    chain.link(nc.vector.tensor_tensor(work[:, :], speed[:, :], dirs[:, :], ALU.mult))
                    chain.link(nc.vector.tensor_scalar(work[:, :], work[:, :], 1.0, None, ALU.add))
                    chain.link(nc.vector.reciprocal(work[:, :], work[:, :]))
                    dve.wait_ge(root_ready, v + 1)
                    chain.link(nc.vector.tensor_tensor(aberr[:, v, :], root[:, :], work[:, :], ALU.mult))
                pads(dve, chain, aberr[:, :, :])

        with nc.If(is_sorted()):
            with ExitStack() as ctx:
                row_in = [tensor(ctx, f"w_row_in{a}", [P, TPU, ROW]) for a in range(2)]
                put = [tensor(ctx, f"w_put{a}", [P, TPU, WIN]) for a in range(2)]
                weighed = [tensor(ctx, f"w_weighed{a}", [P, TPU, VIEWS, WIN]) for a in range(2)]
                total = [tensor(ctx, f"w_total{h}", [P, VIEWS, SPAN]) for h in range(2)]
                nothing = tensor(ctx, "w_nothing", [P, VIEWS * SPAN], BF16)
                pw = [bank(ctx, f"w_pw{h}", [P, VIEWS, SPAN]) for h in range(2)]
                nothing_ready = sem(ctx, "w_nothing_ready")
                rows_in = [sem(ctx, f"w_rows_in_b{a}") for a in range(2)]
                put_ready = sem(ctx, "w_put_ready")
                by_vector, by_scalar, by_pool = (sem(ctx, f"w_by_{n}") for n in ("vector", "scalar", "pool"))
                unit_summed = sem(ctx, "w_unit_summed")
                total_ready = sem(ctx, "w_total_ready")
                added = sem(ctx, "w_added")
                block = ctx.enter_context(nc.Block())
                BOTH, ONE = 2, 1

                @block.sync
                def _(sp):
                    def load(i, spans):
                        for h in range(spans):
                            for a in range(2):
                                g = 2 * i + h
                                u = 2 * g + a
                                after(sp, unit_summed, u - 1)
                                sp.dma_start(row_in[a][:, :, :].rearrange("p k f -> p (k f)"),
                                             gathered[bass.ds(u, 1), :, :].rearrange("a p m -> (a p) m"))\
                                    .then_inc(rows_in[a], 16)

                    rounds(sp, SR, load, SLAST, BOTH)

                @block.vector
                def _(dve):
                    nc.vector.memset(nothing[:, :], 0.0).then_inc(nothing_ready, 1)

                    def weigh(i, spans):
                        for h in range(spans):
                            for a in range(2):
                                u = 2 * (2 * i + h) + a
                                here = bass.ds(u * TPU, TPU)
                                after(dve, unit_summed, u - 1)
                                nc.vector.tensor_tensor(
                                    put[a][:, :, :],
                                    count_f[:, :].unsqueeze(1).to_broadcast([P, TPU, WIN]),
                                    slot[:, here].unsqueeze(2).to_broadcast([P, TPU, WIN]),
                                    ALU.is_equal).then_inc(put_ready, 1)
                                dve.wait_ge(put_ready, u + 1)
                                for v in VECTOR_VIEWS:
                                    last = nc.vector.tensor_tensor(
                                        weighed[a][:, :, v, :], put[a][:, :, :],
                                        aberr[:, v, here].unsqueeze(2).to_broadcast([P, TPU, WIN]),
                                        ALU.mult)
                                last.then_inc(by_vector, 1)

                    rounds(dve, SR, weigh, SLAST, BOTH)

                @block.scalar
                def _(act):
                    def weigh(i, spans):
                        for h in range(spans):
                            for a in range(2):
                                u = 2 * (2 * i + h) + a
                                act.wait_ge(put_ready, u + 1)
                                for v in SCALAR_VIEWS:
                                    for k in range(TPU):
                                        last = nc.scalar.activation(
                                            weighed[a][:, k, v, :], put[a][:, k, :], ACT.Copy,
                                            scale=aberr[:, v, bass.ds(u * TPU + k, 1)])
                                last.then_inc(by_scalar, 1)
                        for h in range(spans):
                            g = 2 * i + h
                            act.wait_ge(unit_summed, 2 * (g + 1))
                            after(act, added, 16 * (g - 1))
                            nc.scalar.copy(total[h][:, :, :], pw[h][:, :, :]).then_inc(total_ready, 1)

                    rounds(act, SR, weigh, SLAST, BOTH)

                @block.tensor
                def _(pe):
                    pe.wait_ge(nothing_ready, 1)

                    def unit(i, spans):
                        for h in range(spans):
                            g = 2 * i + h
                            after(pe, total_ready, g - 1)
                            nc.tensor.matmul(pw[h][:, :, :].rearrange("p v n -> p (v n)"),
                                             nothing[:, 0:P], nothing[:, :], start=True, stop=True)
                            for a in range(2):
                                u = 2 * g + a
                                off = pe.value_load(unit_off[0:1, bass.ds(u, 1)], min_val=0,
                                                    max_val=SPAN - WIN)
                                pe.wait_ge(rows_in[a], 16 * (g + 1))
                                pe.wait_ge(by_vector, u + 1)
                                pe.wait_ge(by_scalar, u + 1)
                                if POOL_VIEWS:
                                    pe.wait_ge(by_pool, u + 1)
                                for k in range(TPU):
                                    last = nc.tensor.matmul(
                                        pw[h][:, :, bass.ds(off, WIN)], row_in[a][:, k, 0:F],
                                        weighed[a][:, k, :, :], start=False, stop=True,
                                        skip_group_check=True)
                                last.then_inc(unit_summed, 1)

                    rounds(pe, SR, unit, SLAST, BOTH)

                @block.gpsimd
                def _(pool):
                    def weigh(i, spans):
                        for h in range(spans):
                            g = 2 * i + h
                            if POOL_VIEWS:
                                for a in range(2):
                                    u = 2 * g + a
                                    gate(pool, put_ready, u + 1, pool_passed)
                                    for v in POOL_VIEWS:
                                        last = nc.gpsimd.tensor_tensor(
                                            weighed[a][:, :, v, :], put[a][:, :, :],
                                            aberr[:, v, bass.ds(u * TPU, TPU)].unsqueeze(2)
                                            .to_broadcast([P, TPU, WIN]), ALU.mult)
                                    last.then_inc(by_pool, 1)
                            if h == 0:
                                if not (isinstance(i, int) and i == 0):
                                    add(2 * i - 1, 1)
                            else:
                                add(2 * i, 0)

                    def add(g, h):
                        base = pool.value_load(span_base[0:1, bass.ds(g, 1)], min_val=0, max_val=N - SPAN)
                        gate(pool, total_ready, g + 1, pool_passed)
                        gate(pool, added, 16 * g, pool_passed)
                        pool.dma_start(aggT[:, :, bass.ds(base, SPAN)], total[h][:, :, :],
                                       accum_op=ALU.add).then_inc(added, 16)

                    rounds(pool, SR, weigh, SLAST, BOTH)
                    add(NG - 1, (NG - 1) % 2)
                    pool.wait_ge(added, 16 * NG)

        with nc.Else():
            with ExitStack() as ctx:
                row_in = [tensor(ctx, f"row_in{a}", [P, TPU, ROW]) for a in range(2)]
                node = [tensor(ctx, f"node{a}", [P, TPU]) for a in range(2)]
                share = [tensor(ctx, f"share{a}", [P, VIEWS, TPU]) for a in range(2)]
                same = [tensor(ctx, f"same{j}", [P, VIEWS, P]) for j in range(2)]
                scrap = [tensor(ctx, f"scrap{j}", [P, P]) for j in range(2)]
                before = [tensor(ctx, f"before{a}", [P, TPU]) for a in range(2)]
                to_trash = tensor(ctx, "to_trash", [P, TPU])
                moved = tensor(ctx, "moved", [P, TPU])
                at_node = [tensor(ctx, f"at_node{a}", [P, TPU], I32) for a in range(2)]
                total = [tensor(ctx, f"total{j}", [P, VIEWS * F]) for j in range(2)]
                pn = [bank(ctx, f"pn{j}", [P, P]) for j in range(2)]
                ps = [bank(ctx, f"ps{j}", [P, VIEWS * F]) for j in range(2)]
                rows_in = [sem(ctx, f"rows_in_b{a}") for a in range(2)]
                staged = sem(ctx, "staged")
                nodes_spread = sem(ctx, "nodes_spread")
                same_ready = sem(ctx, "same_ready")
                summed = sem(ctx, "summed")
                total_ready = sem(ctx, "total_ready")
                at_ready = sem(ctx, "at_ready")
                added = sem(ctx, "added")
                vector_step = sem(ctx, "vector_step3")
                block = ctx.enter_context(nc.Block())

                @block.sync
                def _(sp):
                    def load(g):
                        for a in range(2):
                            u = 2 * g + a
                            after(sp, summed, TPU * (u - 1))
                            sp.dma_start(row_in[a][:, :, :].rearrange("p k f -> p (k f)"),
                                         gathered[bass.ds(u, 1), :, :].rearrange("a p m -> (a p) m"))\
                                .then_inc(rows_in[a], 16)

                    rounds(sp, NG, load)

                @block.scalar
                def _(act):
                    def stage(g):
                        for a in range(2):
                            u = 2 * g + a
                            after(act, at_ready, u - 1)
                            after(act, same_ready, TPU * (u - 1))
                            nc.scalar.copy(node[a][:, :], dst_i[:, bass.ds(u * TPU, TPU)])
                            nc.scalar.copy(share[a][:, :, :], aberr[:, :, bass.ds(u * TPU, TPU)])\
                                .then_inc(staged, 1)
                        for a in range(2):
                            u = 2 * g + a
                            for k in range(TPU):
                                q = TPU * u + k
                                act.wait_ge(summed, q + 1)
                                after(act, added, 16 * (q - 1))
                                j = (TPU * a + k) % 2
                                nc.scalar.copy(total[j][:, :], ps[j][:, :]).then_inc(total_ready, 1)

                    rounds(act, NG, stage)

                @block.tensor
                def _(pe):
                    def unit(g):
                        for a in range(2):
                            u = 2 * g + a
                            pe.wait_ge(staged, u + 1)
                            pe.wait_ge(rows_in[a], 16 * (g + 1))
                            for k in range(TPU):
                                q, j = TPU * u + k, (TPU * a + k) % 2
                                after(pe, same_ready, q - 1)
                                nc.tensor.matmul(pn[j][:, :], node[a][:, k:k + 1].to_broadcast([P, P]),
                                                 ident[:, :], start=True, stop=True)\
                                    .then_inc(nodes_spread, 1)
                                pe.wait_ge(same_ready, q + 1)
                                after(pe, total_ready, q - 1)
                                for v in range(VIEWS):
                                    last = nc.tensor.matmul(ps[j][:, v * F:(v + 1) * F], same[j][:, v, :],
                                                            row_in[a][:, k, 0:F], start=True, stop=True)
                                last.then_inc(summed, 1)

                    rounds(pe, NG, unit)

                @block.vector
                def _(dve):
                    def unit(g):
                        for a in range(2):
                            u = 2 * g + a
                            chain = Chain(dve, vector_step, 3 * u)
                            dve.wait_ge(staged, u + 1)
                            for k in range(TPU):
                                q, j = TPU * u + k, (TPU * a + k) % 2
                                dve.wait_ge(nodes_spread, q + 1)
                                after(dve, summed, q - 1)
                                nc.vector.scalar_tensor_tensor(
                                    out=scrap[j][:, :], in0=pn[j][:, :], scalar=node[a][:, k:k + 1],
                                    in1=earlier[:, :], op0=ALU.is_equal, op1=ALU.mult,
                                    accum_out=before[a][:, k:k + 1])
                                for v in range(VIEWS):
                                    last = nc.vector.tensor_scalar(
                                        same[j][:, v, :], pn[j][:, :], node[a][:, k:k + 1],
                                        share[a][:, v, k:k + 1], ALU.is_equal, ALU.mult)
                                last.then_inc(same_ready, 1)
                            dve.wait_ge(same_ready, TPU * (u + 1))
                            after(dve, added, 16 * TPU * (u - 1))
                            chain.link(nc.vector.tensor_scalar(to_trash[:, :], node[a][:, :], -1.0,
                                                               trash[:, 0:1], ALU.mult, ALU.add))
                            chain.link(nc.vector.scalar_tensor_tensor(
                                out=moved[:, :], in0=before[a][:, :], scalar=0.5, in1=to_trash[:, :],
                                op0=ALU.is_gt, op1=ALU.mult))
                            chain.link(nc.vector.tensor_tensor(at_node[a][:, :], moved[:, :],
                                                               node[a][:, :], ALU.add))
                            dve.nop().then_inc(at_ready, 1)

                    rounds(dve, NG, unit)

                @block.gpsimd
                def _(pool):
                    def scatter(g):
                        for a in range(2):
                            u = 2 * g + a
                            gate(pool, at_ready, u + 1, pool_passed)
                            for k in range(TPU):
                                q, j = TPU * u + k, (TPU * a + k) % 2
                                pool.wait_ge(total_ready, q + 1)
                                gate(pool, added, 16 * q, pool_passed)
                                pool.indirect_dma_start(
                                    agg, bass.IndirectOffsetOnAxis(ap=at_node[a][:, k:k + 1], axis=0),
                                    total[j][:, :], None, compute_op=ALU.add).then_inc(added, 16)

                    rounds(pool, NG, scatter)
                    pool.wait_ge(added, 16 * TPU * NU)

            with ExitStack() as ctx:
                a_in = [tensor(ctx, f"t_in{s}", [P, VIEWS * F]) for s in range(2)]
                a_out = [tensor(ctx, f"t_out{s}", [P, VIEWS, P]) for s in range(2)]
                pa = [bank(ctx, f"t_pa{s}", [P, VIEWS, P]) for s in range(2)]
                a_loaded = [sem(ctx, f"t_loaded{s}") for s in range(2)]
                a_stored = [sem(ctx, f"t_stored{s}") for s in range(2)]
                a_transposed = sem(ctx, "t_transposed")
                a_copied = sem(ctx, "t_copied")
                block = ctx.enter_context(nc.Block())

                @block.sync
                def _(sp):
                    def load(i, r=FULL):
                        for s in range(2):
                            t = 2 * i + s
                            after(sp, a_transposed, t - 1)
                            sp.dma_start(a_in[s][0:r[s], :], rows(agg, t, r[s])).then_inc(a_loaded[s], 16)

                    rounds(sp, NT // 2, load, LAST)

                @block.tensor
                def _(pe):
                    def tile(i, r=FULL):
                        for s in range(2):
                            t = 2 * i + s
                            pe.wait_ge(a_loaded[s], 16 * (i + 1))
                            after(pe, a_copied, t - 1)
                            for v in range(VIEWS):
                                last = nc.tensor.transpose(pa[s][:, v, 0:r[s]],
                                                           a_in[s][0:r[s], v * F:(v + 1) * F],
                                                           ident[0:r[s], 0:r[s]])
                            last.then_inc(a_transposed, 1)

                    rounds(pe, NT // 2, tile, LAST)

                @block.scalar
                def _(act):
                    def tile(i, r=FULL):
                        for s in range(2):
                            t = 2 * i + s
                            act.wait_ge(a_transposed, t + 1)
                            after(act, a_stored[s], 16 * i)
                            nc.scalar.copy(a_out[s][:, :, 0:r[s]], pa[s][:, :, 0:r[s]])\
                                .then_inc(a_copied, 1)

                    rounds(act, NT // 2, tile, LAST)

                @block.gpsimd
                def _(pool):
                    def store(i, r=FULL):
                        for s in range(2):
                            t = 2 * i + s
                            gate(pool, a_copied, t + 1, pool_passed)
                            pool.dma_start(aggT[:, :, bass.ds(t * P, r[s])], a_out[s][:, :, 0:r[s]])\
                                .then_inc(a_stored[s], 16)

                    rounds(pool, NT // 2, store, LAST)
                    for s in range(2):
                        pool.wait_ge(a_stored[s], 16 * (NT // 2))

        with ExitStack() as both:
            bn_scale_c = tensor(both, "bn_scale_c", [P, VIEWS])
            bn_bias_c = tensor(both, "bn_bias_c", [P, VIEWS])
            l1_wT = tensor(both, "l1_wT", [P, F])
            with ExitStack() as ctx:
                NC = N // CHUNK
                a_in = [tensor(ctx, f"a_in{s}", [P, VIEWS, CHUNK]) for s in range(2)]
                stats = tensor(ctx, "stats", [P, VIEWS, NC * 6])
                moments = tensor(ctx, "moments", [P, VIEWS, 2])
                small = tensor(ctx, "small", [P, VIEWS])
                soft = tensor(ctx, "soft", [VIEWS, F])
                peak = tensor(ctx, "peak", [VIEWS, 1])
                mass = tensor(ctx, "mass", [VIEWS, 1])
                softT = tensor(ctx, "softT", [P, VIEWS])
                pw = bank(ctx, "pw", [P, P])
                px = bank(ctx, "px", [P, P])
                a_loaded = [sem(ctx, f"a_loaded{s}") for s in range(2)]
                a_measured = sem(ctx, "a_measured")
                peak_ready = sem(ctx, "peak_ready")
                soft_ready = sem(ctx, "soft_ready")
                soft_scaled = sem(ctx, "soft_scaled")
                turned = sem(ctx, "turned")
                variance_ready = sem(ctx, "variance_ready")
                deviation_ready = sem(ctx, "deviation_ready")
                vector_step = sem(ctx, "vector_step4")
                block = ctx.enter_context(nc.Block())

                @block.sync
                def _(sp):
                    def load(i):
                        for s in range(2):
                            c = 2 * i + s
                            after(sp, a_measured, c - 1)
                            sp.dma_start(a_in[s][:, :, :], aggT[:, :, bass.ds(c * CHUNK, CHUNK)])\
                                .then_inc(a_loaded[s], 16)

                    rounds(sp, NC // 2, load)

                @block.tensor
                def _(pe):
                    nc.tensor.transpose(pw[:, :], l1_w[:, :], ident[:, :]).then_inc(turned, 1)
                    pe.wait_ge(soft_scaled, 1)
                    nc.tensor.transpose(px[:, 0:VIEWS], soft[:, :], ident[0:VIEWS, 0:VIEWS])\
                        .then_inc(turned, 1)

                @block.scalar
                def _(act):
                    act.wait_ge(peak_ready, 1)
                    nc.scalar.activation(soft[:, :], att[:, :], ACT.Exp, bias=peak[:, 0:1],
                                         accum_out=mass[:, 0:1]).then_inc(soft_ready, 1)
                    act.wait_ge(variance_ready, 1)
                    nc.scalar.activation(small[:, :], small[:, :], ACT.Sqrt)\
                        .then_inc(deviation_ready, 1)

                @block.vector
                def _(dve):
                    def chunk(i):
                        for s in range(2):
                            c = 2 * i + s
                            dve.wait_ge(a_loaded[s], 16 * (i + 1))
                            for v in range(VIEWS):
                                last = nc.vector.bn_stats(stats[:, v, bass.ds(c * 6, 6)],
                                                          a_in[s][:, v, :])
                            last.then_inc(a_measured, 1)

                    rounds(dve, NC // 2, chunk)
                    chain = Chain(dve, vector_step)
                    chain.link(nc.vector.tensor_reduce(peak[:, :], att[:, :], axis=AX.X, op=ALU.max))
                    chain.link(nc.vector.tensor_scalar(peak[:, :], peak[:, :], -1.0, None, ALU.mult))
                    dve.nop().then_inc(peak_ready, 1)
                    dve.wait_ge(a_measured, NC)
                    for v in range(VIEWS):
                        chain.link(nc.vector.bn_aggr(moments[:, v, :], stats[:, v, :]))
                    chain.link(nc.vector.tensor_scalar(small[:, :], moments[:, :, 1], EPS, None,
                                                       ALU.add))
                    dve.nop().then_inc(variance_ready, 1)
                    dve.wait_ge(soft_ready, 1)
                    chain.link(nc.vector.reciprocal(mass[:, :], mass[:, :]))
                    chain.link(nc.vector.tensor_scalar(soft[:, :], soft[:, :], mass[:, 0:1], None,
                                                       ALU.mult))
                    dve.nop().then_inc(soft_scaled, 1)
                    dve.wait_ge(deviation_ready, 1)
                    chain.link(nc.vector.reciprocal(small[:, :], small[:, :]))
                    chain.link(nc.vector.tensor_tensor(bn_scale_c[:, :], small[:, :], bn_s[:, :],
                                                       ALU.mult))
                    chain.link(nc.vector.tensor_tensor(small[:, :], bn_scale_c[:, :],
                                                       moments[:, :, 0], ALU.mult))
                    chain.link(nc.vector.tensor_tensor(bn_bias_c[:, :], bn_b[:, :], small[:, :],
                                                       ALU.subtract))
                    dve.wait_ge(turned, 2)
                    chain.link(nc.vector.tensor_copy(l1_wT[:, :], pw[:, :]))
                    chain.link(nc.vector.tensor_copy(softT[:, :], px[:, 0:VIEWS]))
                    chain.link(nc.vector.tensor_tensor(bn_scale_c[:, :], bn_scale_c[:, :],
                                                       softT[:, :], ALU.mult))
                    chain.link(nc.vector.tensor_tensor(bn_bias_c[:, :], bn_bias_c[:, :],
                                                       softT[:, :], ALU.mult))

            with ExitStack() as ctx:
                def pair(name, shape):
                    return [tensor(ctx, f"{name}{s}", shape) for s in range(2)]

                a_in, x_in = pair("a_again", [P, VIEWS, P]), pair("x_again", [P, F])
                view = pair("view", [P, VIEWS, P])
                zstat, zmom, zdev = pair("zstat", [P, 6]), pair("zmom", [P, 2]), pair("zdev", [P, 1])
                z_n, z_r = pair("z_n", [P, Z]), pair("z_r", [P, ZB, P])
                y = pair("y", [P, F])
                ystat, ymom, ydev = pair("ystat", [P, 6]), pair("ymom", [P, 2]), pair("ydev", [P, 1])
                x1, x1T, h1 = pair("x1", [P, F]), pair("x1T", [P, P]), pair("h1", [P, F])
                pz = [bank(ctx, f"pz{s}", [P, 512]) for s in range(2)]
                pt = [bank(ctx, f"pt2{s}", [P, ZB, P]) for s in range(2)]
                names = ("view_ready", "z_summed", "z_dev", "z_root", "z_ready",
                         "z_turned", "z_relu", "y_summed", "y_dev", "y_root", "x1_ready",
                         "x1_turned", "x1T_ready", "h1_summed", "h1_ready")
                (view_ready, z_summed, z_dev, z_root, z_ready, z_turned, z_relu, y_summed,
                 y_dev, y_root, x1_ready, x1_turned, x1T_ready, h1_summed, h1_ready) = (
                    sem(ctx, n) for n in names)
                loaded = [sem(ctx, f"loaded{s}") for s in range(2)]
                x_loaded = [sem(ctx, f"x_again_loaded{s}") for s in range(2)]
                stored = [sem(ctx, f"stored{s}") for s in range(2)]
                vector_step = sem(ctx, "vector_step5")
                block = ctx.enter_context(nc.Block())

                @block.sync
                def _(sp):
                    def load(i, r=FULL):
                        for s in range(2):
                            t = 2 * i + s
                            after(sp, view_ready, t - 1)
                            sp.dma_start(a_in[s][:, :, 0:r[s]], aggT[:, :, bass.ds(t * P, r[s])])\
                                .then_inc(loaded[s], 16)
                            after(sp, y_dev, t - 1)
                            sp.dma_start(x_in[s][0:r[s], :], rows(x, t, r[s]))\
                                .then_inc(x_loaded[s], 16)

                    rounds(sp, NT // 2, load, LAST)

                @block.gpsimd
                def _(pool):
                    def store(i, r=FULL):
                        for s in range(2):
                            t = 2 * i + s
                            gate(pool, x1_ready, t + 1, pool_passed)
                            pool.dma_start(rows(x1_rows, t, r[s]), x1[s][0:r[s], :])\
                                .then_inc(stored[s], 16)
                            gate(pool, h1_ready, t + 1, pool_passed)
                            pool.dma_start(rows(h1_table, t, r[s]), h1[s][0:r[s], :])\
                                .then_inc(stored[s], 16)

                    rounds(pool, NT // 2, store, LAST)
                    for s in range(2):
                        pool.wait_ge(stored[s], 16 * NT)

                @block.tensor
                def _(pe):
                    def tile(i, r=FULL):
                        for s in range(2):
                            t, n = 2 * i + s, r[s]
                            pe.wait_ge(view_ready, t + 1)
                            after(pe, h1_ready, t - 1)
                            for v in range(VIEWS):
                                nc.tensor.matmul(pz[s][0:n, 0:Z], view[s][:, v, 0:n], w1[:, v, :],
                                                 start=(v == 0), stop=False)
                            nc.tensor.matmul(pz[s][0:n, 0:Z], ones[:, 0:n], b1_r[:, :],
                                             start=False, stop=True).then_inc(z_summed, 1)
                        for s in range(2):
                            t, n = 2 * i + s, r[s]
                            pe.wait_ge(z_ready, t + 1)
                            after(pe, x1T_ready, t - 1)
                            for b in range(ZB):
                                last = nc.tensor.transpose(pt[s][:, b, 0:n],
                                                           z_n[s][0:n, b * P:(b + 1) * P],
                                                           ident[0:n, 0:n])
                            last.then_inc(z_turned, 1)
                        for s in range(2):
                            t, n = 2 * i + s, r[s]
                            pe.wait_ge(z_relu, t + 1)
                            for b in range(ZB):
                                nc.tensor.matmul(pz[s][0:n, 0:F], z_r[s][:, b, 0:n], w2[:, b, :],
                                                 start=(b == 0), stop=False)
                            nc.tensor.matmul(pz[s][0:n, 0:F], ones[:, 0:n], b2_r[:, :],
                                             start=False, stop=True).then_inc(y_summed, 1)
                        for s in range(2):
                            t, n = 2 * i + s, r[s]
                            pe.wait_ge(x1_ready, t + 1)
                            nc.tensor.transpose(pt[s][:, 0, 0:n], x1[s][0:n, :], ident[0:n, 0:n])\
                                .then_inc(x1_turned, 1)
                        for s in range(2):
                            t, n = 2 * i + s, r[s]
                            pe.wait_ge(x1T_ready, t + 1)
                            nc.tensor.matmul(pz[s][0:n, 0:F], x1T[s][:, 0:n], l1_wT[:, :],
                                             start=True, stop=False)
                            nc.tensor.matmul(pz[s][0:n, 0:F], ones[:, 0:n], l1_b[:, :],
                                             start=False, stop=True).then_inc(h1_summed, 1)

                    rounds(pe, NT // 2, tile, LAST)

                @block.scalar
                def _(act):
                    def tile(i, r=FULL):
                        for s in range(2):
                            t, n = 2 * i + s, r[s]
                            act.wait_ge(loaded[s], 16 * (i + 1))
                            after(act, z_summed, t - 1)
                            for v in range(VIEWS):
                                last = nc.scalar.activation(view[s][:, v, 0:n], a_in[s][:, v, 0:n],
                                                            ACT.Relu, bias=bn_bias_c[:, v:v + 1],
                                                            scale=bn_scale_c[:, v:v + 1])
                            last.then_inc(view_ready, 1)
                        for s in range(2):
                            t, n = 2 * i + s, r[s]
                            act.wait_ge(z_dev, t + 1)
                            nc.scalar.activation(zdev[s][0:n, :], zdev[s][0:n, :], ACT.Sqrt)\
                                .then_inc(z_root, 1)
                        for s in range(2):
                            t, n = 2 * i + s, r[s]
                            act.wait_ge(z_turned, t + 1)
                            after(act, y_summed, t - 1)
                            for b in range(ZB):
                                last = nc.scalar.activation(z_r[s][:, b, 0:n], pt[s][:, b, 0:n],
                                                            ACT.Relu, bias=ln_b[:, b:b + 1],
                                                            scale=ln_s[:, b:b + 1])
                            last.then_inc(z_relu, 1)
                        for s in range(2):
                            t, n = 2 * i + s, r[s]
                            act.wait_ge(y_dev, t + 1)
                            nc.scalar.activation(ydev[s][0:n, :], ydev[s][0:n, :], ACT.Sqrt)\
                                .then_inc(y_root, 1)
                        for s in range(2):
                            t, n = 2 * i + s, r[s]
                            act.wait_ge(x1_turned, t + 1)
                            after(act, h1_summed, t - 1)
                            nc.scalar.copy(x1T[s][:, 0:n], pt[s][:, 0, 0:n]).then_inc(x1T_ready, 1)
                        for s in range(2):
                            t, n = 2 * i + s, r[s]
                            act.wait_ge(h1_summed, t + 1)
                            after(act, stored[s], 32 * i)
                            nc.scalar.activation(h1[s][0:n, :], pz[s][0:n, 0:F], ACT.Relu)\
                                .then_inc(h1_ready, 1)

                    rounds(act, NT // 2, tile, LAST)

                @block.vector
                def _(dve):
                    STEPS = 4 + 5

                    def tile(i, r=FULL):
                        chain = Chain(dve, vector_step, 2 * STEPS * i)
                        for s in range(2):
                            t, n = 2 * i + s, r[s]
                            dve.wait_ge(z_summed, t + 1)
                            chain.link(nc.vector.bn_stats(zstat[s][0:n, :], pz[s][0:n, 0:Z]))
                            dve.sem_inc(vector_passed, 1)
                            chain.link(nc.vector.bn_aggr(zmom[s][0:n, :], zstat[s][0:n, :]))
                            nc.vector.tensor_scalar(zdev[s][0:n, :], zmom[s][0:n, 1:2], EPS, None,
                                                    ALU.add).then_inc(z_dev, 1)
                        for s in range(2):
                            t, n = 2 * i + s, r[s]
                            dve.wait_ge(z_root, t + 1)
                            after(dve, z_turned, t - 1)
                            chain.link(nc.vector.reciprocal(zdev[s][0:n, :], zdev[s][0:n, :]))
                            chain.link(nc.vector.tensor_scalar(
                                z_n[s][0:n, :], pz[s][0:n, 0:Z], zmom[s][0:n, 0:1],
                                zdev[s][0:n, 0:1], ALU.subtract, ALU.mult))
                            dve.nop().then_inc(z_ready, 1)
                        for s in range(2):
                            t, n = 2 * i + s, r[s]
                            dve.wait_ge(y_summed, t + 1)
                            dve.wait_ge(x_loaded[s], 16 * (i + 1))
                            chain.link(nc.vector.tensor_tensor(y[s][0:n, :], pz[s][0:n, 0:F],
                                                               x_in[s][0:n, :], ALU.add))
                            chain.link(nc.vector.bn_stats(ystat[s][0:n, :], y[s][0:n, :]))
                            dve.sem_inc(vector_passed, 1)
                            chain.link(nc.vector.bn_aggr(ymom[s][0:n, :], ystat[s][0:n, :]))
                            nc.vector.tensor_scalar(ydev[s][0:n, :], ymom[s][0:n, 1:2], EPS, None,
                                                    ALU.add).then_inc(y_dev, 1)
                        for s in range(2):
                            t, n = 2 * i + s, r[s]
                            dve.wait_ge(y_root, t + 1)
                            after(dve, stored[s], 32 * i)
                            after(dve, x1_turned, t - 1)
                            chain.link(nc.vector.reciprocal(ydev[s][0:n, :], ydev[s][0:n, :]))
                            chain.link(nc.vector.tensor_scalar(
                                x1[s][0:n, :], y[s][0:n, :], ymom[s][0:n, 0:1],
                                ydev[s][0:n, 0:1], ALU.subtract, ALU.mult))
                            dve.nop().then_inc(x1_ready, 1)
                        assert chain.n == 2 * STEPS

                    rounds(dve, NT // 2, tile, LAST)

        with nc.If(is_sorted()):
            with ExitStack() as ctx:
                slots = [tensor(ctx, f"m_slots{a}", [P, TPU], BF16) for a in range(2)]
                lo = [tensor(ctx, f"m_lo{a}", [P, TPU], BF16) for a in range(2)]
                hi = [tensor(ctx, f"m_hi{a}", [P, TPU], BF16) for a in range(2)]
                at_src = [tensor(ctx, f"m_at_src{a}", [P, TPU], I32) for a in range(2)]
                node = [tensor(ctx, f"m_node{a}", [P, TPU]) for a in range(2)]
                share = [tensor(ctx, f"m_share{a}", [P, TPU]) for a in range(2)]
                h_win = [tensor(ctx, f"m_h_win{a}", [WIN, F + 1]) for a in range(2)]
                pick = [tensor(ctx, f"m_pick{a}", [WIN, TPU * P]) for a in range(2)]
                h_row = [tensor(ctx, f"m_h_row{j}", [P, F + 1]) for j in range(2)]
                same = [tensor(ctx, f"m_same{j}", [P, P]) for j in range(2)]
                scrap = [tensor(ctx, f"m_scrap{j}", [P, P]) for j in range(2)]
                before = [tensor(ctx, f"m_before{a}", [P, TPU]) for a in range(2)]
                to_trash = tensor(ctx, "m_to_trash", [P, TPU])
                moved = tensor(ctx, "m_moved", [P, TPU])
                total = [tensor(ctx, f"m_total{k}", [P, F + 1]) for k in range(TPU)]
                pr = bank(ctx, "m_pr", [P, 1024])
                pn = [bank(ctx, f"m_pn{j}", [P, P]) for j in range(2)]
                ph = [bank(ctx, f"m_ph{j}", [P, F + 1]) for j in range(2)]
                ps = [bank(ctx, f"m_ps{j}", [P, F + 1]) for j in range(2)]
                (ones_ready, slots_ready, staged, slots_spread, pick_ready, nodes_spread, h_picked,
                 h_ready, same_ready, summed, total_ready, at_ready, vector_step) = (
                    sem(ctx, f"m_{n}") for n in (
                        "ones_ready", "slots_ready", "staged", "slots_spread", "pick_ready",
                        "nodes_spread", "h_picked", "h_ready", "same_ready", "summed", "total_ready",
                        "at_ready", "vector_step"))
                window_in = [sem(ctx, f"m_window_in{a}") for a in range(2)]
                added = [sem(ctx, f"m_added{k}") for k in range(TPU)]
                block = ctx.enter_context(nc.Block())

                @block.sync
                def _(sp):
                    def load(g):
                        for a in range(2):
                            u = 2 * g + a
                            base = sp.value_load(unit_base[0:1, bass.ds(u, 1)], min_val=0,
                                                 max_val=N - WIN)
                            after(sp, h_picked, TPU * (u - 1))
                            sp.dma_start(h_win[a][:, 0:F], h1_table[bass.ds(base, WIN), :])\
                                .then_inc(window_in[a], 16)

                    rounds(sp, NG, load)

                @block.scalar
                def _(act):
                    def unit(g):
                        for a in range(2):
                            u = 2 * g + a
                            here = bass.ds(u * TPU, TPU)
                            after(act, slots_spread, u - 1)
                            nc.scalar.copy(slots[a][:, :], slot_b[:, here]).then_inc(slots_ready, 1)
                            after(act, at_ready, u - 1)
                            nc.scalar.copy(lo[a][:, :], src_lo[:, here])
                            nc.scalar.copy(hi[a][:, :], src_hi[:, here])
                            nc.scalar.copy(node[a][:, :], src_i[:, here])
                            nc.scalar.copy(share[a][:, :], ew[:, here]).then_inc(staged, 1)
                        for a in range(2):
                            u = 2 * g + a
                            for k in range(TPU + 1):
                                if k < TPU:
                                    q, j = TPU * u + k, (TPU * a + k) % 2
                                    act.wait_ge(h_picked, q + 1)
                                    after(act, summed, q - 1)
                                    nc.scalar.copy(h_row[j][:, :], ph[j][:, :]).then_inc(h_ready, 1)
                                if k > 0:
                                    q, j = TPU * u + k - 1, (TPU * a + k - 1) % 2
                                    act.wait_ge(summed, q + 1)
                                    after(act, added[k - 1], 16 * u)
                                    nc.scalar.copy(total[k - 1][:, :], ps[j][:, :])\
                                        .then_inc(total_ready, 1)

                    rounds(act, NG, unit)

                @block.tensor
                def _(pe):
                    pe.wait_ge(ones_ready, 2)

                    def unit(g):
                        for a in range(2):
                            u = 2 * g + a
                            pe.wait_ge(slots_ready, u + 1)
                            after(pe, pick_ready, u)
                            for k in range(TPU):
                                last = nc.tensor.matmul(pr[0:WIN, k * P:(k + 1) * P],
                                                        slots[a][:, k:k + 1].to_broadcast([P, WIN]),
                                                        ident_b[:, :], start=True, stop=True)
                            last.then_inc(slots_spread, 1)
                            pe.wait_ge(staged, u + 1)
                            for k in range(TPU + 1):
                                if k < TPU:
                                    q, j = TPU * u + k, (TPU * a + k) % 2
                                    after(pe, same_ready, q - 1)
                                    nc.tensor.matmul(pn[j][:, :], lo[a][:, k:k + 1].to_broadcast([P, P]),
                                                     ident_b[:, :], start=True, stop=False)
                                    nc.tensor.matmul(pn[j][:, :], hi[a][:, k:k + 1].to_broadcast([P, P]),
                                                     ident_b[:, :], start=False, stop=True)\
                                        .then_inc(nodes_spread, 1)
                                    if k == 0:
                                        pe.wait_ge(pick_ready, u + 1)
                                        pe.wait_ge(window_in[a], 16 * (g + 1))
                                    after(pe, h_ready, q - 1)
                                    nc.tensor.matmul(ph[j][:, :], pick[a][:, k * P:(k + 1) * P],
                                                     h_win[a][:, :], start=True, stop=True)\
                                        .then_inc(h_picked, 1)
                                if k > 0:
                                    q, j = TPU * u + k - 1, (TPU * a + k - 1) % 2
                                    pe.wait_ge(same_ready, q + 1)
                                    pe.wait_ge(h_ready, q + 1)
                                    after(pe, total_ready, q - 1)
                                    nc.tensor.matmul(ps[j][:, :], same[j][:, :], h_row[j][:, :],
                                                     start=True, stop=True).then_inc(summed, 1)

                    rounds(pe, NG, unit)

                @block.vector
                def _(dve):
                    for a in range(2):
                        nc.vector.memset(h_win[a][:, F:F + 1], 1.0).then_inc(ones_ready, 1)

                    def unit(g):
                        for a in range(2):
                            u = 2 * g + a
                            chain = Chain(dve, vector_step, 3 * u)
                            dve.wait_ge(slots_spread, u + 1)
                            after(dve, h_picked, TPU * (u - 1))
                            nc.vector.tensor_scalar(pick[a][:, :], pr[0:WIN, 0:TPU * P],
                                                    count_p[0:WIN, 0:1], None, ALU.is_equal)\
                                .then_inc(pick_ready, 1)
                            dve.wait_ge(staged, u + 1)
                            for k in range(TPU):
                                q, j = TPU * u + k, (TPU * a + k) % 2
                                dve.wait_ge(nodes_spread, q + 1)
                                after(dve, summed, q - 1)
                                nc.vector.scalar_tensor_tensor(
                                    out=scrap[j][:, :], in0=pn[j][:, :], scalar=node[a][:, k:k + 1],
                                    in1=earlier[:, :], op0=ALU.is_equal, op1=ALU.mult,
                                    accum_out=before[a][:, k:k + 1])
                                nc.vector.tensor_scalar(
                                    same[j][:, :], pn[j][:, :], node[a][:, k:k + 1],
                                    share[a][:, k:k + 1], ALU.is_equal, ALU.mult)\
                                    .then_inc(same_ready, 1)
                            dve.wait_ge(same_ready, TPU * (u + 1))
                            chain.link(nc.vector.tensor_scalar(to_trash[:, :], node[a][:, :], -1.0,
                                                               trash[:, 0:1], ALU.mult, ALU.add))
                            chain.link(nc.vector.scalar_tensor_tensor(
                                out=moved[:, :], in0=before[a][:, :], scalar=0.5, in1=to_trash[:, :],
                                op0=ALU.is_gt, op1=ALU.mult))
                            for k in range(TPU):
                                after(dve, added[k], 16 * (u - 1))
                            chain.link(nc.vector.tensor_tensor(at_src[a][:, :], moved[:, :],
                                                               node[a][:, :], ALU.add))
                            dve.nop().then_inc(at_ready, 1)

                    rounds(dve, NG, unit)

                @block.gpsimd
                def _(pool):
                    def scatter(g):
                        for a in range(2):
                            u = 2 * g + a
                            gate(pool, at_ready, u + 1, pool_passed)
                            for k in range(TPU):
                                gate(pool, total_ready, TPU * u + k + 1, pool_passed)
                                gate(pool, added[k], 16 * u, pool_passed)
                                pool.indirect_dma_start(
                                    sums[k], bass.IndirectOffsetOnAxis(ap=at_src[a][:, k:k + 1], axis=0),
                                    total[k][:, :], None, compute_op=ALU.add).then_inc(added[k], 16)

                    rounds(pool, NG, scatter)
                    for k in range(TPU):
                        pool.wait_ge(added[k], 16 * NU)

        with nc.Else():
            with ExitStack() as ctx:
                at_dst = [tensor(ctx, f"l1_at_dst{a}", [P, TPU], I32) for a in range(2)]
                at_src = [tensor(ctx, f"l1_at_src{a}", [P, TPU], I32) for a in range(2)]
                node = [tensor(ctx, f"l1_node{a}", [P, TPU]) for a in range(2)]
                share = [tensor(ctx, f"l1_share{a}", [P, TPU]) for a in range(2)]
                h_row = [tensor(ctx, f"h_row{a}", [P, TPU, F + 1]) for a in range(2)]
                same = [tensor(ctx, f"l1_same{j}", [P, P]) for j in range(2)]
                scrap = [tensor(ctx, f"l1_scrap{j}", [P, P]) for j in range(2)]
                before = [tensor(ctx, f"l1_before{a}", [P, TPU]) for a in range(2)]
                to_trash = tensor(ctx, "l1_to_trash", [P, TPU])
                moved = tensor(ctx, "l1_moved", [P, TPU])
                total = [tensor(ctx, f"l1_total{k}", [P, F + 1]) for k in range(TPU)]
                pn = [bank(ctx, f"l1_pn{j}", [P, P]) for j in range(2)]
                ps = [bank(ctx, f"l1_ps{j}", [P, F + 1]) for j in range(2)]
                ones_ready = sem(ctx, "ones_ready")
                staged = sem(ctx, "l1_staged")
                index_ready = sem(ctx, "l1_index_ready")
                rows_in = [sem(ctx, f"l1_rows_in{a}") for a in range(2)]
                nodes_spread = sem(ctx, "l1_nodes_spread")
                same_ready = sem(ctx, "l1_same_ready")
                summed = sem(ctx, "l1_summed")
                total_ready = sem(ctx, "l1_total_ready")
                at_ready = sem(ctx, "l1_at_ready")
                added = [sem(ctx, f"l1_added{k}") for k in range(TPU)]
                vector_step = sem(ctx, "vector_step6")
                block = ctx.enter_context(nc.Block())

                @block.scalar
                def _(act):
                    def stage(g):
                        for a in range(2):
                            u = 2 * g + a
                            after(act, rows_in[a], 16 * TPU * g)
                            nc.scalar.copy(at_dst[a][:, :], dst_i[:, bass.ds(u * TPU, TPU)])\
                                .then_inc(index_ready, 1)
                            after(act, at_ready, u - 1)
                            nc.scalar.copy(node[a][:, :], src_i[:, bass.ds(u * TPU, TPU)])
                            nc.scalar.copy(share[a][:, :], ew[:, bass.ds(u * TPU, TPU)])\
                                .then_inc(staged, 1)
                        for a in range(2):
                            u = 2 * g + a
                            for k in range(TPU):
                                q, j = TPU * u + k, (TPU * a + k) % 2
                                act.wait_ge(summed, q + 1)
                                after(act, added[k], 16 * u)
                                nc.scalar.copy(total[k][:, :], ps[j][:, :]).then_inc(total_ready, 1)

                    rounds(act, NG, stage)

                @block.tensor
                def _(pe):
                    def unit(g):
                        for a in range(2):
                            u = 2 * g + a
                            pe.wait_ge(staged, u + 1)
                            for k in range(TPU):
                                q, j = TPU * u + k, (TPU * a + k) % 2
                                after(pe, same_ready, q - 1)
                                nc.tensor.matmul(pn[j][:, :], node[a][:, k:k + 1].to_broadcast([P, P]),
                                                 ident[:, :], start=True, stop=True)\
                                    .then_inc(nodes_spread, 1)
                                if k == 0:
                                    pe.wait_ge(rows_in[a], 16 * TPU * (g + 1))
                                pe.wait_ge(same_ready, q + 1)
                                after(pe, total_ready, q - 1)
                                nc.tensor.matmul(ps[j][:, :], same[j][:, :], h_row[a][:, k, :],
                                                 start=True, stop=True).then_inc(summed, 1)

                    rounds(pe, NG, unit)

                @block.vector
                def _(dve):
                    for a in range(2):
                        nc.vector.memset(h_row[a][:, :, F:F + 1], 1.0).then_inc(ones_ready, 1)

                    def unit(g):
                        for a in range(2):
                            u = 2 * g + a
                            chain = Chain(dve, vector_step, 3 * u)
                            dve.wait_ge(staged, u + 1)
                            for k in range(TPU):
                                q, j = TPU * u + k, (TPU * a + k) % 2
                                dve.wait_ge(nodes_spread, q + 1)
                                after(dve, summed, q - 1)
                                nc.vector.scalar_tensor_tensor(
                                    out=scrap[j][:, :], in0=pn[j][:, :], scalar=node[a][:, k:k + 1],
                                    in1=earlier[:, :], op0=ALU.is_equal, op1=ALU.mult,
                                    accum_out=before[a][:, k:k + 1])
                                nc.vector.tensor_scalar(
                                    same[j][:, :], pn[j][:, :], node[a][:, k:k + 1],
                                    share[a][:, k:k + 1], ALU.is_equal, ALU.mult)\
                                    .then_inc(same_ready, 1)
                            dve.wait_ge(same_ready, TPU * (u + 1))
                            chain.link(nc.vector.tensor_scalar(to_trash[:, :], node[a][:, :], -1.0,
                                                               trash[:, 0:1], ALU.mult, ALU.add))
                            chain.link(nc.vector.scalar_tensor_tensor(
                                out=moved[:, :], in0=before[a][:, :], scalar=0.5, in1=to_trash[:, :],
                                op0=ALU.is_gt, op1=ALU.mult))
                            for k in range(TPU):
                                after(dve, added[k], 16 * (u - 1))
                            chain.link(nc.vector.tensor_tensor(at_src[a][:, :], moved[:, :],
                                                               node[a][:, :], ALU.add))
                            dve.nop().then_inc(at_ready, 1)

                    rounds(dve, NG, unit)

                @block.gpsimd
                def _(pool):
                    pool.wait_ge(ones_ready, 2)

                    def gather(g, a):
                        u = 2 * g + a
                        gate(pool, index_ready, u + 1, pool_passed)
                        gate(pool, summed, TPU * (u - 1), pool_passed)
                        for k in range(TPU):
                            pool.indirect_dma_start(
                                h_row[a][:, k, 0:F], None, h1_table,
                                bass.IndirectOffsetOnAxis(ap=at_dst[a][:, k:k + 1], axis=0),
                            ).then_inc(rows_in[a], 16)

                    def scatter(g):
                        for a in range(2):
                            gather(g, a)
                        for a in range(2):
                            u = 2 * g + a
                            gate(pool, at_ready, u + 1, pool_passed)
                            for k in range(TPU):
                                gate(pool, total_ready, TPU * u + k + 1, pool_passed)
                                gate(pool, added[k], 16 * u, pool_passed)
                                pool.indirect_dma_start(
                                    sums[k], bass.IndirectOffsetOnAxis(ap=at_src[a][:, k:k + 1], axis=0),
                                    total[k][:, :], None, compute_op=ALU.add).then_inc(added[k], 16)

                    rounds(pool, NG, scatter)
                    for k in range(TPU):
                        pool.wait_ge(added[k], 16 * NU)

        with ExitStack() as ctx:
            def pair(name, shape):
                return [tensor(ctx, f"{name}{s}", shape) for s in range(2)]

            part = pair("part", [P, SPLITS, F + 1])
            x1 = pair("x1_in", [P, F])
            whole = pair("whole", [P, F + 1])
            degree, low = pair("degree", [P, 1]), pair("low", [P, 1])
            y, ystat, ymom = pair("y_out", [P, F]), pair("ystat_out", [P, 6]), pair("ymom_out", [P, 2])
            ydev, result = pair("ydev_out", [P, 1]), pair("result", [P, F])
            loaded = [sem(ctx, f"f_loaded{s}") for s in range(2)]
            stored = [sem(ctx, f"f_stored{s}") for s in range(2)]
            used = sem(ctx, "f_used")
            dev, rooted, ready = sem(ctx, "f_dev"), sem(ctx, "f_root"), sem(ctx, "f_ready")
            vector_step = sem(ctx, "vector_step7")
            block = ctx.enter_context(nc.Block())

            @block.sync
            def _(sp):
                def load(i, r=FULL):
                    for s in range(2):
                        t, n = 2 * i + s, r[s]
                        after(sp, used, t - 1)
                        for k in range(SPLITS):
                            sp.dma_start(part[s][0:n, k, :], rows(sums[k], t, n))\
                                .then_inc(loaded[s], 16)
                        sp.dma_start(x1[s][0:n, :], rows(x1_rows, t, n)).then_inc(loaded[s], 16)

                rounds(sp, NT // 2, load, LAST)

            @block.scalar
            def _(act):
                def tile(i, r=FULL):
                    for s in range(2):
                        t, n = 2 * i + s, r[s]
                        act.wait_ge(dev, t + 1)
                        nc.scalar.activation(ydev[s][0:n, :], ydev[s][0:n, :], ACT.Sqrt)\
                            .then_inc(rooted, 1)

                rounds(act, NT // 2, tile, LAST)

            @block.vector
            def _(dve):
                STEPS = 9

                def tile(i, r=FULL):
                    chain = Chain(dve, vector_step, 2 * STEPS * i)
                    for s in range(2):
                        t, n = 2 * i + s, r[s]
                        dve.wait_ge(loaded[s], 16 * (SPLITS + 1) * (i + 1))
                        chain.link(nc.vector.tensor_reduce(
                            whole[s][0:n, :], part[s][0:n, :, :].rearrange("p k f -> p f k"),
                            axis=AX.X, op=ALU.add))
                        chain.link(nc.vector.tensor_scalar(low[s][0:n, :], whole[s][0:n, F:F + 1], 0.5,
                                                           None, ALU.is_lt))
                        chain.link(nc.vector.tensor_tensor(degree[s][0:n, :], whole[s][0:n, F:F + 1],
                                                           low[s][0:n, :], ALU.add))
                        chain.link(nc.vector.reciprocal(degree[s][0:n, :], degree[s][0:n, :]))
                        chain.link(nc.vector.scalar_tensor_tensor(
                            out=y[s][0:n, :], in0=whole[s][0:n, 0:F], scalar=degree[s][0:n, 0:1],
                            in1=x1[s][0:n, :], op0=ALU.mult, op1=ALU.add))
                        chain.link(nc.vector.bn_stats(ystat[s][0:n, :], y[s][0:n, :]))
                        dve.sem_inc(vector_passed, 1)
                        dve.nop().then_inc(used, 1)
                        chain.link(nc.vector.bn_aggr(ymom[s][0:n, :], ystat[s][0:n, :]))
                        nc.vector.tensor_scalar(ydev[s][0:n, :], ymom[s][0:n, 1:2], EPS, None,
                                                ALU.add).then_inc(dev, 1)
                    for s in range(2):
                        t, n = 2 * i + s, r[s]
                        dve.wait_ge(rooted, t + 1)
                        after(dve, stored[s], 16 * i)
                        chain.link(nc.vector.reciprocal(ydev[s][0:n, :], ydev[s][0:n, :]))
                        chain.link(nc.vector.tensor_scalar(
                            result[s][0:n, :], y[s][0:n, :], ymom[s][0:n, 0:1], ydev[s][0:n, 0:1],
                            ALU.subtract, ALU.mult))
                        dve.nop().then_inc(ready, 1)
                    assert chain.n == 2 * STEPS

                rounds(dve, NT // 2, tile, LAST)

            @block.gpsimd
            def _(pool):
                def store(i, r=FULL):
                    for s in range(2):
                        t, n = 2 * i + s, r[s]
                        gate(pool, ready, t + 1, pool_passed)
                        pool.dma_start(rows(out, t, n), result[s][0:n, :]).then_inc(stored[s], 16)

                rounds(pool, NT // 2, store, LAST)
                for s in range(2):
                    pool.wait_ge(stored[s], 16 * (NT // 2))


_INS = ["x", "src", "dst", "edge_weight", "L0_gnn_W_ft", "L0_gnn_b_ft", "L0_gnn_W_conv",
        "L0_gnn_b_conv", "L0_gnn_velocity_factor", "L0_gnn_velocity_params", "L0_gnn_attention",
        "L0_gnn_bn_scale", "L0_gnn_bn_bias", "L0_gnn_W1", "L0_gnn_b1", "L0_gnn_ln_scale",
        "L0_gnn_ln_bias", "L0_gnn_W2", "L0_gnn_b2", "L1_gnn_W", "L1_gnn_b"]


def kernel(**inputs):
    import numpy as _np
    import concourse.bacc as _bacc
    from concourse import mybir as _mybir
    from concourse.bass_utils import run_bass_kernel_spmd as _run

    nc = _bacc.Bacc("TRN2", target_bir_lowering=False, num_devices=1)
    arrays, args = {}, []
    for name in _INS:
        a = _np.ascontiguousarray(inputs[name])
        if a.ndim == 0:
            a = a.reshape(1)
        arrays[f"in_{name}"] = a
        args.append(nc.dram_tensor(f"in_{name}", a.shape, _mybir.dt.from_np(a.dtype),
                                   kind="ExternalInput").ap())
    shape = arrays["in_x"].shape
    args.append(nc.dram_tensor("out_x", shape, _mybir.dt.float32, kind="ExternalOutput").ap())
    resnorm_gnn(nc, *args)
    r = _run(nc, [arrays], core_ids=[0])
    return r.results[0]["out_x"]
```

```python
import concourse.bass as bass
from concourse import mybir
from contextlib import ExitStack

P = 128
F = 128
VIEWS = 4
ROW = 132
TPU = 5
WIN = 64
SPAN = 128
LEAD = 6
CHUNK = 250
SPLITS = TPU
FP32 = mybir.dt.float32
BF16 = mybir.dt.bfloat16
I32 = mybir.dt.int32
ALU = mybir.AluOpType
ACT = mybir.ActivationFunctionType
AX = mybir.AxisListType
FULL = (P, P)


def after(eng, sem, value):
    if isinstance(value, int) and value <= 0:
        return
    eng.wait_ge(sem, value)


def rounds(eng, n, body, last=None, full=FULL, unroll=1):
    extra = () if last is None else (full,)
    if n > 1:
        body(0, *extra)
    steps = max(n - 2, 0) // unroll
    if steps:
        with eng.Fori(0, steps) as i:
            for j in range(unroll):
                body(unroll * i + (j + 1), *extra)
    for r in range(1 + steps * unroll, n - 1):
        body(r, *extra)
    body(n - 1, *(() if last is None else (last,)))


class Quad:

    def __init__(self, c, h):
        self.c, self.h = c, h

    def back(self, lag):
        return Quad(self.c - lag, (self.h - lag) % 2)


def gate(eng, sem, value, passed):
    if isinstance(value, int) and value <= 0:
        return
    eng.wait_ge(sem, value)
    eng.sem_inc(passed, 1)


class Chain:

    def __init__(self, eng, sem, base=0):
        self.eng, self.sem, self.base, self.n = eng, sem, base, 0

    def link(self, instruction):
        instruction.then_inc(self.sem, 1)
        self.n += 1
        self.eng.wait_ge(self.sem, self.base + self.n)


def resnorm_gnn(nc, x, src, dst, edge_weight, W_ft, b_ft, W_conv, b_conv, velocity_factor,
                velocity_params, attention, bn_scale, bn_bias, W1, b1, ln_scale, ln_bias, W2, b2,
                L1_W, L1_b, out):
    N, E = x.shape[0], src.shape[0]
    NT = -(-N // P)
    assert NT % 2 == 0
    LAST = (P, N - (NT - 1) * P)
    UE = TPU * P
    NU = 2 * -(-E // (2 * UE))
    NG = NU // 2
    FU = E // UE
    TAIL = (E - FU * UE) // TPU
    assert TAIL * TPU == E - FU * UE and TAIL % 32 == 0 and NU - FU <= 2
    assert N % CHUNK == 0 and N // CHUNK % 2 == 0 and N <= 2 ** 15 and NU <= 512
    NQ = -(-NT // 4)
    LAST_QUAD = tuple(min(P, N - t * P) for t in range(4 * (NQ - 1), NT))
    Z = W1.shape[1]
    ZB = Z // P
    EPS = 1e-5
    SUM_ROWS = NT * P + P

    node_table = nc.dram_tensor("node_table", [N, ROW], FP32).ap()
    pos_table = nc.dram_tensor("pos_table", [N, 4], FP32).ap()
    gathered = nc.dram_tensor("gathered", [NU, P, TPU * ROW], FP32).ap()
    agg = nc.dram_tensor("agg", [SUM_ROWS, VIEWS * F], FP32).ap()
    AT_PART = -(-VIEWS * N // NG)
    aggT_flat = nc.dram_tensor("aggT", [NG * F * AT_PART], FP32).ap()
    aggT = aggT_flat[0:F * VIEWS * N].rearrange("(f v n) -> f v n", f=F, v=VIEWS)
    SUM_PART = -(-SUM_ROWS // NG)
    assert SUM_PART <= P
    sums = [nc.dram_tensor(f"sums{k}", [NG * SUM_PART, F + 1], FP32).ap() for k in range(SPLITS)]
    h1_table = nc.dram_tensor("h1_table", [N, F], FP32).ap()
    x1_rows = nc.dram_tensor("x1_rows", [N, F], FP32).ap()

    top = ExitStack()
    with top:
        def tensor(ctx, name, shape, dt=FP32):
            return ctx.enter_context(nc.sbuf_tensor(name, shape, dt))

        def bank(ctx, name, shape):
            return ctx.enter_context(nc.psum_tensor(name, shape, FP32))

        of_stage = {}

        def end_stage(sems):
            nc.clear_and_free_semaphores(sems)
            nc.all_engine_barrier()

        def sem(ctx, name):
            if ctx not in of_stage:
                of_stage[ctx] = []
                ctx.callback(end_stage, of_stage[ctx])
            of_stage[ctx].append(nc.alloc_semaphore(name))
            return of_stage[ctx][-1]

        pool_passed = sem(top, "pool_passed")
        vector_passed = sem(top, "vector_passed")
        ident = tensor(top, "ident", [P, P])
        earlier = tensor(top, "earlier", [P, P])
        ones = tensor(top, "ones", [1, P])
        trash = tensor(top, "trash", [P, 1])
        trash_i = tensor(top, "trash_i", [P, 1], I32)
        bias_conv_all = tensor(top, "bias_conv_all", [P, ROW])
        b1_all = tensor(top, "b1_all", [P, Z])
        b2_all = tensor(top, "b2_all", [P, F])
        l1_b_all = tensor(top, "l1_b_all", [P, F])
        w_ft = tensor(top, "w_ft", [P, F])
        w_conv = tensor(top, "w_conv", [P, ROW])
        b_ft_c = tensor(top, "b_ft_c", [P, 1])
        w1 = tensor(top, "w1", [P, VIEWS, Z])
        w2 = tensor(top, "w2", [P, ZB, F])
        ln_s = tensor(top, "ln_s", [P, ZB])
        ln_b = tensor(top, "ln_b", [P, ZB])
        bn_s = tensor(top, "bn_s", [P, VIEWS])
        bn_b = tensor(top, "bn_b", [P, VIEWS])
        att = tensor(top, "att", [VIEWS, F])
        l1_w = tensor(top, "l1_w", [P, F])
        v_obs = tensor(top, "v_obs", [P, VIEWS])
        v_fac = tensor(top, "v_fac", [P, 1])
        src_i = tensor(top, "src_i", [P, NU * TPU], I32)
        dst_i = tensor(top, "dst_i", [P, NU * TPU], I32)
        ew = tensor(top, "ew", [P, NU * TPU])
        dist = tensor(top, "dist", [P, NU * TPU])
        dirs = tensor(top, "dirs", [P, NU * TPU])
        aberr = tensor(top, "aberr", [P, VIEWS, NU * TPU])

        slot = tensor(top, "slot", [P, NU * TPU])
        slot_b = tensor(top, "slot_b", [P, NU * TPU], BF16)
        src_lo = tensor(top, "src_lo", [P, NU * TPU], BF16)
        src_hi = tensor(top, "src_hi", [P, NU * TPU], BF16)
        ident_b = tensor(top, "ident_b", [P, P], BF16)
        count_p = tensor(top, "count_p", [P, 1])
        count_f = tensor(top, "count_f", [P, WIN])
        unit_base = tensor(top, "unit_base", [1, NU], I32)
        span_base = tensor(top, "span_base", [1, NG], I32)
        unit_off = tensor(top, "unit_off", [1, NU], I32)
        sorted_flag = tensor(top, "sorted_flag", [1, 1], I32)

        def rows(table, t, r):
            return table[bass.ds(t * P, r), :]

        def quads(eng, body):
            for c in range(LEAD):
                body(Quad(c, c % 2))
            end = max(LEAD, (NQ - 2) // 2 * 2)
            if end > LEAD:
                with eng.Fori(LEAD // 2, end // 2) as i:
                    for h in range(2):
                        body(Quad(2 * i + h, h))
            for c in range(end, max(NQ + 3, LEAD)):
                body(Quad(c, c % 2))

        def missing(q):
            return isinstance(q.c, int) and not 0 <= q.c < NQ

        def sizes(q):
            return LAST_QUAD if isinstance(q.c, int) and q.c == NQ - 1 else (P,) * 4

        def stretches(q):
            r = sizes(q)
            full = sum(n == P for n in r)
            return [(0, full, P)] * (full > 0) + [(t, 1, r[t]) for t in range(full, len(r))]

        def landed(q):
            return 16 * (q.c // 2 if isinstance(q.c, int) else (q.c - q.h) // 2) + 16 * len(stretches(q))

        def quad_rows(table, q, t, k, n):
            return table[bass.ds(q.c * (4 * P) + t * P, (k - 1) * P + n), :]\
                .rearrange("(t p) f -> p t f", t=k)

        def pads(dve, chain, held):
            if TAIL:
                chain.link(nc.vector.memset(held[TAIL:P, FU * TPU:(FU + 1) * TPU]
                                            if len(held.shape) == 2 else
                                            held[TAIL:P, :, FU * TPU:(FU + 1) * TPU], 0.0))
            if NU > FU + (TAIL > 0):
                at = (FU + (TAIL > 0)) * TPU
                chain.link(nc.vector.memset(held[:, at:NU * TPU] if len(held.shape) == 2 else
                                            held[:, :, at:NU * TPU], 0.0))

        ZEROS = 5000
        SR, SLAST = -(-NG // 2), 2 - NG % 2
        VECTOR_VIEWS, SCALAR_VIEWS, POOL_VIEWS = (0, 1), (2,), (3,)

        def is_sorted():
            return nc.values_load(sorted_flag[0:1, 0:1], min_val=0, max_val=1) == 1

        def by_partition(table):
            return table.rearrange("n f -> (n f)").rearrange("(p m) -> p m", p=P)

        def clears(tables, zeros):
            for table in tables:
                for at in range(0, table.shape[1], ZEROS):
                    m = min(table.shape[1] - at, ZEROS)
                    yield table[:, at:at + m], zeros[:, 0:m]

        with ExitStack() as ctx:
            x_in = [tensor(ctx, f"x_in{h}", [P, 4, F]) for h in range(2)]
            xT = [tensor(ctx, f"xT{h}", [P, 4 * P]) for h in range(2)]
            hT = [tensor(ctx, f"hT{h}", [P, 4 * P]) for h in range(2)]
            row_out = [tensor(ctx, f"row_out{h}", [P, 4, ROW]) for h in range(2)]
            pt = [bank(ctx, f"pt{h}", [P, 4 * P]) for h in range(2)]
            ph = [bank(ctx, f"ph{h}", [P, 4 * P]) for h in range(2)]
            pr = [[bank(ctx, f"pr{h}{b}", [P, 2, ROW]) for b in range(2)] for h in range(2)]
            conv_cleared = sem(ctx, "conv_cleared")
            bias_cleared = sem(ctx, "bias_cleared")
            masks_cleared = sem(ctx, "masks_cleared")
            pads_cleared = sem(ctx, "pads_cleared")
            ones_written = sem(ctx, "ones_written")
            trash_written = sem(ctx, "trash_written")
            constants = sem(ctx, "constants")
            weights_in = sem(ctx, "weights_in")
            bias_in = sem(ctx, "bias_in")
            later_in = sem(ctx, "later_in")
            edges_in = sem(ctx, "edges_in")
            x_loaded = [sem(ctx, f"x_loaded{h}") for h in range(2)]
            x_transposed = sem(ctx, "x_transposed")
            xT_ready = sem(ctx, "xT_ready")
            h_summed = sem(ctx, "h_summed")
            hT_ready = sem(ctx, "hT_ready")
            row_summed = sem(ctx, "row_summed")
            row_ready = sem(ctx, "row_ready")
            row_stored = [sem(ctx, f"row_stored{h}") for h in range(2)]
            block = ctx.enter_context(nc.Block())

            @block.sync
            def _(sp):
                sp.dma_start(w_ft[:, :], W_ft).then_inc(weights_in, 16)
                sp.dma_start(b_ft_c[:, :], b_ft.unsqueeze(1)).then_inc(weights_in, 16)
                sp.wait_ge(conv_cleared, 1)
                sp.dma_start(w_conv[:, 0:F], W_conv).then_inc(weights_in, 16)

                def load(q):
                    if missing(q):
                        return
                    after(sp, x_transposed, q.c - 1)
                    for t, k, n in stretches(q):
                        sp.dma_start(x_in[q.h][0:n, t:t + k, :], quad_rows(x, q, t, k, n))\
                            .then_inc(x_loaded[q.h], 16)

                quads(sp, load)

            @block.gpsimd
            def _(pool):
                nc.gpsimd.memset(w_conv[:, F:ROW], 0.0).then_inc(conv_cleared, 1)
                nc.gpsimd.memset(bias_conv_all[:, F:ROW], 0.0).then_inc(bias_cleared, 1)
                nc.gpsimd.memset(ident[:, :], 0.0).then_inc(masks_cleared, 1)
                nc.gpsimd.memset(earlier[:, :], 1.0).then_inc(masks_cleared, 1)
                pool.wait_ge(masks_cleared, 2)
                nc.gpsimd.affine_select(out=ident[:, :], in_=ident[:, :], compare_op=ALU.not_equal,
                                        fill=1.0, base=0, pattern=[[-1, P]],
                                        channel_multiplier=1).then_inc(constants, 1)
                pool.wait_ge(conv_cleared, 1)
                nc.gpsimd.affine_select(out=w_conv[:, F:F + 3], in_=w_conv[:, F:F + 3],
                                        compare_op=ALU.not_equal, fill=1.0, base=0,
                                        pattern=[[-1, 3]], channel_multiplier=1).then_inc(constants, 1)
                nc.gpsimd.affine_select(out=earlier[:, :], in_=earlier[:, :], compare_op=ALU.is_gt,
                                        fill=0.0, base=0, pattern=[[-1, P]],
                                        channel_multiplier=1).then_inc(constants, 1)
                nc.gpsimd.iota(trash_i[:, :], [[0, 1]], base=NT * P, channel_multiplier=1)\
                    .then_inc(trash_written, 1)
                pool.wait_ge(trash_written, 1)
                nc.gpsimd.tensor_copy(trash[:, :], trash_i[:, :]).then_inc(constants, 1)
                pool.dma_start(bias_conv_all[:, 0:F], b_conv.unsqueeze(0).broadcast_to([P, F]))\
                    .then_inc(bias_in, 16)

                def store(q):
                    if missing(q):
                        return
                    gate(pool, row_ready, q.c + 1, pool_passed)
                    for t, k, n in stretches(q):
                        pool.dma_start(quad_rows(node_table, q, t, k, n),
                                       row_out[q.h][0:n, t:t + k, :]).then_inc(row_stored[q.h], 16)

                quads(pool, store)
                for q in (Quad(NQ - 2, (NQ - 2) % 2), Quad(NQ - 1, (NQ - 1) % 2)):
                    pool.wait_ge(row_stored[q.h], landed(q))

                n = 0
                for to, of in (
                        [(w1[:, :, :], W1.rearrange("(v p) z -> p v z", p=P)),
                         (w2[:, :, :], W2.rearrange("(v p) z -> p v z", p=P)),
                         (b1_all[:, :], b1.unsqueeze(0).broadcast_to([P, Z])),
                         (b2_all[:, :], b2.unsqueeze(0).broadcast_to([P, F])),
                         (l1_b_all[:, :], L1_b.unsqueeze(0).broadcast_to([P, F])),
                         (l1_w[:, :], L1_W), (att[:, :], attention),
                         (v_obs[:, :], velocity_params.unsqueeze(0).broadcast_to([P, VIEWS])),
                         (v_fac[:, :], velocity_factor.unsqueeze(0).broadcast_to([P, 1]))]
                        + [(bn_s[:, v:v + 1], bn_scale[v].unsqueeze(1)) for v in range(VIEWS)]
                        + [(bn_b[:, v:v + 1], bn_bias[v].unsqueeze(1)) for v in range(VIEWS)]
                        + [(ln_s[:, b:b + 1], ln_scale[b * P:(b + 1) * P].unsqueeze(1))
                           for b in range(ZB)]
                        + [(ln_b[:, b:b + 1], ln_bias[b * P:(b + 1) * P].unsqueeze(1))
                           for b in range(ZB)]):
                    pool.dma_start(to, of).then_inc(later_in, 16)
                    n += 1
                pool.wait_ge(later_in, 16 * n)

            @block.tensor
            def _(pe):
                pe.wait_ge(constants, 4)
                pe.wait_ge(ones_written, 1)
                pe.wait_ge(weights_in, 48)

                def transpose_x(q):
                    if missing(q):
                        return
                    pe.wait_ge(x_loaded[q.h], landed(q))
                    after(pe, xT_ready, q.c - 1)
                    for t, n in enumerate(sizes(q)):
                        last = nc.tensor.transpose(pt[q.h][:, t * P:t * P + n], x_in[q.h][0:n, t, :],
                                                   ident[0:n, 0:n])
                    last.then_inc(x_transposed, 1)

                def sum_h(q):
                    if missing(q):
                        return
                    m = sum(sizes(q))
                    pe.wait_ge(xT_ready, q.c + 1)
                    after(pe, hT_ready, q.c - 1)
                    nc.tensor.matmul(ph[q.h][:, 0:m], w_ft[:, :], xT[q.h][:, 0:m], start=True,
                                     stop=True).then_inc(h_summed, 1)

                def sum_rows(q):
                    if missing(q):
                        return
                    pe.wait_ge(hT_ready, q.c + 1)
                    after(pe, row_ready, q.c - 1)
                    for t, n in enumerate(sizes(q)):
                        last = nc.tensor.matmul(pr[q.h][t // 2][0:n, t % 2, :],
                                                hT[q.h][:, t * P:t * P + n], w_conv[:, :],
                                                start=True, stop=True)
                    last.then_inc(row_summed, 1)

                def body(q):
                    transpose_x(q)
                    sum_rows(q.back(1))
                    sum_h(q)

                quads(pe, body)

            @block.scalar
            def _(act):
                act.wait_ge(pads_cleared, 3)
                for held, given in ((src_i, src), (dst_i, dst), (ew, edge_weight)):
                    act.dma_start(held[:, 0:FU * TPU].rearrange("p (u k) -> p u k", k=TPU),
                                  given[0:FU * UE].rearrange("(u p k) -> p u k", p=P, k=TPU))\
                        .then_inc(edges_in, 16)
                    if TAIL:
                        act.dma_start(held[0:TAIL, FU * TPU:(FU + 1) * TPU],
                                      given[FU * UE:E].rearrange("(p k) -> p k", k=TPU))\
                            .then_inc(edges_in, 16)
                act.wait_ge(weights_in, 48)

                def tile(q):
                    if missing(q):
                        return
                    m = sum(sizes(q))
                    act.wait_ge(x_transposed, q.c + 1)
                    after(act, h_summed, q.c - 1)
                    nc.scalar.copy(xT[q.h][:, 0:m], pt[q.h][:, 0:m]).then_inc(xT_ready, 1)
                    act.wait_ge(h_summed, q.c + 1)
                    after(act, row_summed, q.c - 1)
                    nc.scalar.activation(hT[q.h][:, 0:m], ph[q.h][:, 0:m], ACT.Relu,
                                         bias=b_ft_c[:, 0:1]).then_inc(hT_ready, 1)

                quads(act, tile)
                act.wait_ge(edges_in, 16 * 3 * (1 + (TAIL > 0)))

            @block.vector
            def _(dve):
                nc.vector.memset(ones[:, :], 1.0).then_inc(ones_written, 1)
                for held in (src_i, dst_i, ew):
                    nc.vector.memset(held[:, FU * TPU:NU * TPU], 0).then_inc(pads_cleared, 1)
                dve.wait_ge(bias_cleared, 1)
                dve.wait_ge(bias_in, 16)

                def add_bias(q):
                    if missing(q):
                        return
                    r = sizes(q)
                    dve.wait_ge(row_summed, q.c + 1)
                    if not (isinstance(q.c, int) and q.c < 2):
                        dve.wait_ge(row_stored[q.h], landed(q.back(2)))
                    for b in range(-(-len(r) // 2)):
                        of = r[2 * b:2 * b + 2]
                        for t, k, n in ([(0, 2, P)] if of == (P, P) else
                                        [(t, 1, n) for t, n in enumerate(of)]):
                            last = nc.vector.tensor_tensor(
                                row_out[q.h][0:n, 2 * b + t:2 * b + t + k, :],
                                pr[q.h][b][0:n, t:t + k, :],
                                bias_conv_all[0:n, :].unsqueeze(1).to_broadcast([n, k, ROW]), ALU.add)
                    last.then_inc(row_ready, 1)

                quads(dve, add_bias)

        with ExitStack() as ctx:
            first = tensor(ctx, "first", [1, NU])
            first2 = tensor(ctx, "first2", [1, NG])
            offset = tensor(ctx, "offset", [1, NU])
            half_i = tensor(ctx, "half_i", [P, NU * TPU], I32)
            count_i = tensor(ctx, "count_i", [P, 1 + WIN], I32)
            over = tensor(ctx, "over", [P, 4])
            worst = tensor(ctx, "worst", [P, 1])
            worst_all = tensor(ctx, "worst_all", [P, 1])
            pb = bank(ctx, "pb_base", [P, NU])
            vector_step = sem(ctx, "vector_step0")
            first_ready = sem(ctx, "first_ready")
            first_spread = sem(ctx, "first_spread")
            counts_ready = sem(ctx, "counts_ready")
            worst_ready = sem(ctx, "worst_ready")
            worst_shared = sem(ctx, "worst_shared")
            block = ctx.enter_context(nc.Block())

            @block.tensor
            def _(pe):
                pe.wait_ge(first_ready, 1)
                nc.tensor.matmul(pb[:, :], ones[:, :], first[:, :], start=True, stop=True)\
                    .then_inc(first_spread, 1)

            @block.gpsimd
            def _(pool):
                nc.gpsimd.iota(count_i[:, 0:1], [[0, 1]], base=0, channel_multiplier=1)\
                    .then_inc(counts_ready, 1)
                nc.gpsimd.iota(count_i[:, 1:1 + WIN], [[1, WIN]], base=0, channel_multiplier=0)\
                    .then_inc(counts_ready, 1)
                pool.wait_ge(worst_ready, 1)
                nc.gpsimd.partition_all_reduce(worst_all[:, :], worst[:, :], P,
                                               bass.bass_isa.ReduceOp.max).then_inc(worst_shared, 1)

            @block.vector
            def _(dve):
                chain = Chain(dve, vector_step)
                firsts = dst_i[0:1, :].rearrange("p (u k) -> p u k", k=TPU)[:, :, 0]
                chain.link(nc.vector.tensor_scalar(first[:, :], firsts, float(N - WIN), None, ALU.min))
                if NU > FU + (TAIL > 0):
                    chain.link(nc.vector.tensor_copy(first[:, NU - 1:NU], first[:, NU - 2:NU - 1]))
                dve.nop().then_inc(first_ready, 1)
                by_two = first[:, :].rearrange("p (g a) -> p g a", a=2)
                chain.link(nc.vector.tensor_scalar(first2[:, :], by_two[:, :, 0], float(N - SPAN),
                                                   None, ALU.min))
                chain.link(nc.vector.tensor_tensor(
                    offset[:, :].rearrange("p (g a) -> p g a", a=2), by_two,
                    first2[:, :].unsqueeze(2).to_broadcast([1, NG, 2]), ALU.subtract))
                nc.vector.tensor_copy(unit_base[:, :], first[:, :])
                nc.vector.tensor_copy(span_base[:, :], first2[:, :])
                nc.vector.tensor_copy(unit_off[:, :], offset[:, :])
                nc.vector.tensor_copy(ident_b[:, :], ident[:, :])
                for half, bits in ((src_lo, P - 1), (src_hi, 2 ** 15 - P)):
                    chain.link(nc.vector.tensor_scalar(half_i[:, :], src_i[:, :], bits, None,
                                                       ALU.bitwise_and))
                    chain.link(nc.vector.tensor_copy(half[:, :], half_i[:, :]))
                dve.wait_ge(counts_ready, 2)
                nc.vector.tensor_copy(count_p[:, :], count_i[:, 0:1])
                nc.vector.tensor_copy(count_f[:, :], count_i[:, 1:1 + WIN])
                dve.wait_ge(first_spread, 1)
                by_unit = slot[:, :].rearrange("p (u k) -> p u k", k=TPU)
                chain.link(nc.vector.tensor_tensor(
                    by_unit, dst_i[:, :].rearrange("p (u k) -> p u k", k=TPU),
                    pb[:, :].unsqueeze(2).to_broadcast([P, NU, TPU]), ALU.subtract))
                pads(dve, chain, slot[:, :])
                chain.link(nc.vector.tensor_copy(slot_b[:, :], slot[:, :]))
                chain.link(nc.vector.memset(over[:, :], -1.0))
                chain.link(nc.vector.tensor_reduce(over[:, 0:1], slot[:, :], axis=AX.X, op=ALU.max))
                chain.link(nc.vector.tensor_reduce(over[:, 1:2], slot[:, :], axis=AX.X, op=ALU.min))
                chain.link(nc.vector.tensor_reduce(over[0:1, 2:3], offset[:, :], axis=AX.X, op=ALU.max))
                chain.link(nc.vector.tensor_reduce(over[0:1, 3:4], offset[:, :], axis=AX.X, op=ALU.min))
                chain.link(nc.vector.tensor_scalar(over[:, 0:1], over[:, 0:1], -float(WIN - 1), None,
                                                   ALU.add))
                chain.link(nc.vector.tensor_scalar(over[:, 1:2], over[:, 1:2], -1.0, None, ALU.mult))
                chain.link(nc.vector.tensor_scalar(over[0:1, 2:3], over[0:1, 2:3],
                                                   -float(SPAN - WIN), None, ALU.add))
                chain.link(nc.vector.tensor_scalar(over[0:1, 3:4], over[0:1, 3:4], -1.0, None,
                                                   ALU.mult))
                chain.link(nc.vector.tensor_reduce(worst[:, :], over[:, :], axis=AX.X, op=ALU.max))
                dve.nop().then_inc(worst_ready, 1)
                dve.wait_ge(worst_shared, 1)
                chain.link(nc.vector.tensor_scalar(sorted_flag[:, :], worst_all[0:1, :], 0.0, None,
                                                   ALU.is_le))

        with nc.If(is_sorted()):
            with ExitStack() as ctx:
                zeros = tensor(ctx, "w_zeros", [P, max(AT_PART, F + 1)])
                at_src = [tensor(ctx, f"w_at_src{a}", [P, TPU], I32) for a in range(2)]
                slots = [tensor(ctx, f"w_slots{a}", [P, TPU], BF16) for a in range(2)]
                src_row = [tensor(ctx, f"w_src_row{a}", [P, TPU, ROW]) for a in range(2)]
                pos_win = [tensor(ctx, f"w_pos_win{a}", [WIN, 4]) for a in range(2)]
                pick = [tensor(ctx, f"w_pick{a}", [WIN, TPU * P]) for a in range(2)]
                dpos = [tensor(ctx, f"w_dpos{a}", [P, TPU, 3]) for a in range(2)]
                square = [tensor(ctx, f"w_square{a}", [P, TPU, 3]) for a in range(2)]
                pr = [bank(ctx, f"w_pr{a}", [P, 1024]) for a in range(2)]
                pd = [bank(ctx, f"w_pd{a}", [P, TPU, 4]) for a in range(2)]
                zeros_ready = sem(ctx, "w_zeros_ready")
                tables_zeroed = sem(ctx, "w_tables_zeroed")
                index_ready = sem(ctx, "w_index_ready")
                slots_ready = sem(ctx, "w_slots_ready")
                window_in = [sem(ctx, f"w_window_in{a}") for a in range(2)]
                slots_spread = sem(ctx, "w_slots_spread")
                pick_ready = sem(ctx, "w_pick_ready")
                picked = sem(ctx, "w_picked")
                rows_in = [sem(ctx, f"w_rows_in{a}") for a in range(2)]
                rows_out = [sem(ctx, f"w_rows_out{a}") for a in range(2)]
                measured = sem(ctx, "w_measured")
                vector_step = sem(ctx, "w_vector_step")
                block = ctx.enter_context(nc.Block())

                @block.sync
                def _(sp):
                    def unit(g):
                        for a in range(2):
                            u = 2 * g + a
                            after(sp, picked, u - 1)
                            base = sp.value_load(unit_base[0:1, bass.ds(u, 1)], min_val=0,
                                                 max_val=N - WIN)
                            sp.dma_start(pos_win[a][:, :], node_table[bass.ds(base, WIN), F:ROW])\
                                .then_inc(window_in[a], 16)
                        for a in range(2):
                            sp.wait_ge(rows_in[a], 16 * TPU * (g + 1))
                            sp.dma_start(gathered[bass.ds(2 * g + a, 1), :, :].rearrange("a p m -> (a p) m"),
                                         src_row[a][:, :, :].rearrange("p k f -> p (k f)"))\
                                .then_inc(rows_out[a], 16)

                    rounds(sp, NG, unit)
                    for a in range(2):
                        sp.wait_ge(rows_out[a], 16 * NG)
                    sp.wait_ge(tables_zeroed, 16 * (1 + SPLITS) * NG)

                @block.gpsimd
                def _(pool):
                    def gather(g):
                        for a in range(2):
                            u = 2 * g + a
                            gate(pool, index_ready, u + 1, pool_passed)
                            gate(pool, rows_out[a], 16 * g, pool_passed)
                            gate(pool, measured, u - 1, pool_passed)
                            for k in range(TPU):
                                pool.indirect_dma_start(
                                    src_row[a][:, k, :], None, node_table,
                                    bass.IndirectOffsetOnAxis(ap=at_src[a][:, k:k + 1], axis=0),
                                ).then_inc(rows_in[a], 16)

                    rounds(pool, NG, gather)

                @block.scalar
                def _(act):
                    def indices(g):
                        for a in range(2):
                            u = 2 * g + a
                            after(act, slots_spread, u - 1)
                            nc.scalar.copy(slots[a][:, :], slot_b[:, bass.ds(u * TPU, TPU)])\
                                .then_inc(slots_ready, 1)
                            after(act, rows_in[a], 16 * TPU * g)
                            nc.scalar.copy(at_src[a][:, :], src_i[:, bass.ds(u * TPU, TPU)])\
                                .then_inc(index_ready, 1)
                        act.dma_start(aggT_flat[bass.ds(g * (P * AT_PART), P * AT_PART)]
                                      .rearrange("(p m) -> p m", p=P), zeros[:, 0:AT_PART])\
                            .then_inc(tables_zeroed, 16)
                        for k in range(SPLITS):
                            act.dma_start(sums[k][bass.ds(g * SUM_PART, SUM_PART), :],
                                          zeros[0:SUM_PART, 0:F + 1]).then_inc(tables_zeroed, 16)

                    act.wait_ge(zeros_ready, 1)
                    rounds(act, NG, indices)

                @block.tensor
                def _(pe):
                    def unit(g):
                        for a in range(2):
                            u = 2 * g + a
                            pe.wait_ge(slots_ready, u + 1)
                            after(pe, pick_ready, u - 1)
                            for k in range(TPU):
                                last = nc.tensor.matmul(pr[a][0:WIN, k * P:(k + 1) * P],
                                                        slots[a][:, k:k + 1].to_broadcast([P, WIN]),
                                                        ident_b[:, :], start=True, stop=True)
                            last.then_inc(slots_spread, 1)
                            pe.wait_ge(pick_ready, u + 1)
                            pe.wait_ge(window_in[a], 16 * (g + 1))
                            after(pe, measured, u - 1)
                            for k in range(TPU):
                                last = nc.tensor.matmul(pd[a][:, k, 0:3], pick[a][:, k * P:(k + 1) * P],
                                                        pos_win[a][:, 0:3], start=True, stop=True)
                            last.then_inc(picked, 1)

                    rounds(pe, NG, unit)

                @block.vector
                def _(dve):
                    nc.vector.memset(zeros[:, :], 0.0).then_inc(zeros_ready, 1)

                    def measure(g):
                        for a in range(2):
                            u = 2 * g + a
                            dve.wait_ge(slots_spread, u + 1)
                            after(dve, picked, u - 1)
                            nc.vector.tensor_scalar(pick[a][:, :], pr[a][0:WIN, 0:TPU * P],
                                                    count_p[0:WIN, 0:1], None, ALU.is_equal)\
                                .then_inc(pick_ready, 1)
                        for a in range(2):
                            u = 2 * g + a
                            chain = Chain(dve, vector_step, 3 * u)
                            dve.wait_ge(picked, u + 1)
                            dve.wait_ge(rows_in[a], 16 * TPU * (g + 1))
                            chain.link(nc.vector.tensor_tensor(dpos[a][:, :, :], src_row[a][:, :, F:F + 3],
                                                               pd[a][:, :, 0:3], ALU.subtract))
                            chain.link(nc.vector.tensor_tensor(square[a][:, :, :], dpos[a][:, :, :],
                                                               dpos[a][:, :, :], ALU.mult))
                            nc.vector.tensor_reduce(dist[:, bass.ds(u * TPU, TPU)], square[a][:, :, :],
                                                    axis=AX.X, op=ALU.add)
                            chain.link(nc.vector.tensor_reduce(dirs[:, bass.ds(u * TPU, TPU)],
                                                               dpos[a][:, :, :], axis=AX.X, op=ALU.add))
                            dve.nop().then_inc(measured, 1)

                    rounds(dve, NG, measure)

        with nc.Else():
            with ExitStack() as ctx:
                zeros = tensor(ctx, "zeros", [P, ZEROS])
                at_src = [tensor(ctx, f"at_src{a}", [P, TPU], I32) for a in range(2)]
                at_dst = [tensor(ctx, f"at_dst{a}", [P, TPU], I32) for a in range(2)]
                src_row = [tensor(ctx, f"src_row{a}", [P, TPU, ROW]) for a in range(2)]
                dst_pos = [tensor(ctx, f"dst_pos{a}", [P, TPU, 4]) for a in range(2)]
                dpos = tensor(ctx, "dpos", [P, TPU, 3])
                square = tensor(ctx, "square", [P, TPU, 3])
                zeros_ready = sem(ctx, "zeros_ready")
                pos_split = sem(ctx, "pos_split")
                tables_zeroed = sem(ctx, "tables_zeroed")
                index_ready = sem(ctx, "index_ready")
                rows_in = [sem(ctx, f"rows_in{a}") for a in range(2)]
                rows_out = [sem(ctx, f"rows_out{a}") for a in range(2)]
                measured = sem(ctx, "measured")
                vector_step = sem(ctx, "vector_step")
                block = ctx.enter_context(nc.Block())
                @block.sync
                def _(sp):
                    sp.dma_start(pos_table, node_table[:, F:ROW]).then_inc(pos_split, 16)
                    sp.wait_ge(zeros_ready, 1)
                    n = 0
                    for to, of in clears([by_partition(t[0:SUM_ROWS, :]) for t in (agg, *sums)], zeros):
                        sp.dma_start(to, of).then_inc(tables_zeroed, 16)
                        n += 1

                    def store(g):
                        for a in range(2):
                            sp.wait_ge(rows_in[a], 16 * 2 * TPU * (g + 1))
                            sp.dma_start(gathered[2 * g + a, :, :].squeeze() if isinstance(g, int) else
                                         gathered[bass.ds(2 * g + a, 1), :, :].rearrange("a p m -> (a p) m"),
                                         src_row[a][:, :, :].rearrange("p k f -> p (k f)"))\
                                .then_inc(rows_out[a], 16)

                    rounds(sp, NG, store)
                    for a in range(2):
                        sp.wait_ge(rows_out[a], 16 * NG)
                    sp.wait_ge(tables_zeroed, 16 * n)

                @block.gpsimd
                def _(pool):
                    pool.wait_ge(pos_split, 16)

                    def gather(g):
                        for a in range(2):
                            u = 2 * g + a
                            gate(pool, index_ready, 2 * (u + 1), pool_passed)
                            gate(pool, rows_out[a], 16 * g, pool_passed)
                            gate(pool, measured, u - 1, pool_passed)
                            for k in range(TPU):
                                pool.indirect_dma_start(
                                    src_row[a][:, k, :], None, node_table,
                                    bass.IndirectOffsetOnAxis(ap=at_src[a][:, k:k + 1], axis=0),
                                ).then_inc(rows_in[a], 16)
                                pool.indirect_dma_start(
                                    dst_pos[a][:, k, :], None, pos_table,
                                    bass.IndirectOffsetOnAxis(ap=at_dst[a][:, k:k + 1], axis=0),
                                ).then_inc(rows_in[a], 16)

                    rounds(pool, NG, gather)

                @block.scalar
                def _(act):
                    def indices(g):
                        for a in range(2):
                            u = 2 * g + a
                            after(act, rows_in[a], 16 * 2 * TPU * g)
                            nc.scalar.copy(at_src[a][:, :], src_i[:, bass.ds(u * TPU, TPU)])\
                                .then_inc(index_ready, 1)
                            nc.scalar.copy(at_dst[a][:, :], dst_i[:, bass.ds(u * TPU, TPU)])\
                                .then_inc(index_ready, 1)

                    rounds(act, NG, indices)

                @block.vector
                def _(dve):
                    nc.vector.memset(zeros[:, :], 0.0).then_inc(zeros_ready, 1)

                    def measure(g):
                        for a in range(2):
                            u = 2 * g + a
                            chain = Chain(dve, vector_step, 3 * u)
                            dve.wait_ge(rows_in[a], 16 * 2 * TPU * (g + 1))
                            chain.link(nc.vector.tensor_tensor(dpos[:, :, :], src_row[a][:, :, F:F + 3],
                                                               dst_pos[a][:, :, 0:3], ALU.subtract))
                            chain.link(nc.vector.tensor_tensor(square[:, :, :], dpos[:, :, :],
                                                               dpos[:, :, :], ALU.mult))
                            nc.vector.tensor_reduce(dist[:, bass.ds(u * TPU, TPU)], square[:, :, :],
                                                    axis=AX.X, op=ALU.add)
                            chain.link(nc.vector.tensor_reduce(dirs[:, bass.ds(u * TPU, TPU)],
                                                               dpos[:, :, :], axis=AX.X, op=ALU.add))
                            dve.nop().then_inc(measured, 1)

                    rounds(dve, NG, measure)

        with ExitStack() as ctx:
            far = tensor(ctx, "far", [P, 1])
            far_all = tensor(ctx, "far_all", [P, 1])
            near = tensor(ctx, "near", [P, 1])
            work = tensor(ctx, "work", [P, NU * TPU])
            speed = [tensor(ctx, f"speed{j}", [P, NU * TPU]) for j in range(2)]
            root = [tensor(ctx, f"root{j}", [P, NU * TPU]) for j in range(2)]
            one_c = tensor(ctx, "one_c", [P, 1])
            vector_step = sem(ctx, "vector_step2")
            squares_ready = sem(ctx, "squares_ready")
            dist_ready = sem(ctx, "dist_ready")
            far_ready = sem(ctx, "far_ready")
            far_shared = sem(ctx, "far_shared")
            speed_ready = sem(ctx, "speed_ready")
            square_ready = sem(ctx, "square_ready")
            root_ready = sem(ctx, "root_ready")
            block = ctx.enter_context(nc.Block())

            @block.scalar
            def _(act):
                act.wait_ge(squares_ready, 1)
                nc.scalar.activation(dist[:, :], dist[:, :], ACT.Sqrt).then_inc(dist_ready, 1)
                for v in range(VIEWS):
                    act.wait_ge(speed_ready, v + 1)
                    nc.scalar.activation(root[v % 2][:, :], speed[v % 2][:, :], ACT.Square)\
                        .then_inc(square_ready, 1)
                    act.wait_ge(square_ready, v + 1)
                    nc.scalar.activation(root[v % 2][:, :], root[v % 2][:, :], ACT.Sqrt, bias=one_c[:, 0:1],
                                         scale=-1.0).then_inc(root_ready, 1)

            @block.gpsimd
            def _(pool):
                pool.wait_ge(far_ready, 1)
                nc.gpsimd.partition_all_reduce(far_all[:, :], far[:, :], P,
                                               bass.bass_isa.ReduceOp.max).then_inc(far_shared, 1)

            @block.vector
            def _(dve):
                chain = Chain(dve, vector_step)
                pads(dve, chain, dist[:, :])
                chain.link(nc.vector.memset(one_c[:, :], 1.0))
                chain.link(nc.vector.tensor_scalar(dist[:, :], dist[:, :], 1e-32, None, ALU.max))
                dve.nop().then_inc(squares_ready, 1)
                dve.wait_ge(dist_ready, 1)
                nc.vector.tensor_reduce(far[:, :], dist[:, :], axis=AX.X, op=ALU.max)\
                    .then_inc(far_ready, 1)
                chain.link(nc.vector.tensor_scalar(work[:, :], dist[:, :], 1e-8, None, ALU.add))
                chain.link(nc.vector.reciprocal(work[:, :], work[:, :]))
                chain.link(nc.vector.tensor_tensor(dirs[:, :], dirs[:, :], work[:, :], ALU.mult))
                dve.wait_ge(far_shared, 1)
                chain.link(nc.vector.reciprocal(near[:, :], far_all[:, :]))
                chain.link(nc.vector.tensor_scalar(dist[:, :], dist[:, :], near[:, 0:1], None, ALU.mult))
                for v in range(VIEWS + 1):
                    if v < VIEWS:
                        chain.link(nc.vector.tensor_scalar(speed[v % 2][:, :], dist[:, :],
                                                           v_obs[:, v:v + 1], v_fac[:, 0:1], ALU.min,
                                                           ALU.mult))
                        dve.nop().then_inc(speed_ready, 1)
                    if v > 0:
                        j = (v - 1) % 2
                        chain.link(nc.vector.tensor_tensor(work[:, :], speed[j][:, :], dirs[:, :],
                                                           ALU.mult))
                        chain.link(nc.vector.tensor_scalar(work[:, :], work[:, :], 1.0, None, ALU.add))
                        chain.link(nc.vector.reciprocal(work[:, :], work[:, :]))
                        dve.wait_ge(root_ready, v)
                        chain.link(nc.vector.tensor_tensor(aberr[:, v - 1, :], root[j][:, :],
                                                           work[:, :], ALU.mult))
                pads(dve, chain, aberr[:, :, :])

        with nc.If(is_sorted()):
            with ExitStack() as ctx:
                row_in = [tensor(ctx, f"w_row_in{b}", [P, TPU, ROW]) for b in range(4)]
                put = [tensor(ctx, f"w_put{b}", [P, TPU, WIN]) for b in range(4)]
                weighed = [tensor(ctx, f"w_weighed{b}", [P, TPU, VIEWS, WIN]) for b in range(4)]
                total = [tensor(ctx, f"w_total{h}", [P, VIEWS, SPAN]) for h in range(2)]
                nothing = tensor(ctx, "w_nothing", [P, VIEWS * SPAN], BF16)
                pw = [bank(ctx, f"w_pw{h}", [P, VIEWS, SPAN]) for h in range(2)]
                nothing_ready = sem(ctx, "w_nothing_ready")
                rows_in = [sem(ctx, f"w_rows_in_b{b}") for b in range(4)]
                put_ready = sem(ctx, "w_put_ready")
                by_vector, by_scalar, by_pool = (sem(ctx, f"w_by_{n}") for n in ("vector", "scalar", "pool"))
                unit_summed = sem(ctx, "w_unit_summed")
                total_ready = sem(ctx, "w_total_ready")
                added = sem(ctx, "w_added")
                block = ctx.enter_context(nc.Block())
                BOTH, ONE = 2, 1

                @block.sync
                def _(sp):
                    def load(i, spans):
                        for h in range(spans):
                            for a in range(2):
                                g = 2 * i + h
                                u = 2 * g + a
                                b = 2 * h + a
                                after(sp, unit_summed, u - 3)
                                sp.dma_start(row_in[b][:, :, :].rearrange("p k f -> p (k f)"),
                                             gathered[bass.ds(u, 1), :, :].rearrange("a p m -> (a p) m"))\
                                    .then_inc(rows_in[b], 16)

                    rounds(sp, SR, load, SLAST, BOTH)

                @block.vector
                def _(dve):
                    nc.vector.memset(nothing[:, :], 0.0).then_inc(nothing_ready, 1)

                    def weigh(i, spans):
                        for h in range(spans):
                            for a in range(2):
                                u = 2 * (2 * i + h) + a
                                here = bass.ds(u * TPU, TPU)
                                b = 2 * h + a
                                after(dve, unit_summed, u - 3)
                                nc.vector.tensor_tensor(
                                    put[2 * h + a][:, :, :],
                                    count_f[:, :].unsqueeze(1).to_broadcast([P, TPU, WIN]),
                                    slot[:, here].unsqueeze(2).to_broadcast([P, TPU, WIN]),
                                    ALU.is_equal).then_inc(put_ready, 1)
                                dve.wait_ge(put_ready, u + 1)
                                for v in VECTOR_VIEWS:
                                    last = nc.vector.tensor_tensor(
                                        weighed[2 * h + a][:, :, v, :], put[2 * h + a][:, :, :],
                                        aberr[:, v, here].unsqueeze(2).to_broadcast([P, TPU, WIN]),
                                        ALU.mult)
                                last.then_inc(by_vector, 1)

                    rounds(dve, SR, weigh, SLAST, BOTH)

                @block.scalar
                def _(act):
                    def copy_total(g, h):
                        act.wait_ge(unit_summed, 2 * (g + 1))
                        after(act, added, 16 * (g - 1))
                        nc.scalar.copy(total[h][:, :, :], pw[h][:, :, :]).then_inc(total_ready, 1)

                    def weigh(i, spans):
                        for h in range(spans):
                            for a in range(2):
                                u = 2 * (2 * i + h) + a
                                act.wait_ge(put_ready, u + 1)
                                for v in SCALAR_VIEWS:
                                    for k in range(TPU):
                                        last = nc.scalar.activation(
                                            weighed[2 * h + a][:, k, v, :], put[2 * h + a][:, k, :], ACT.Copy,
                                            scale=aberr[:, v, bass.ds(u * TPU + k, 1)])
                                last.then_inc(by_scalar, 1)
                            if not (isinstance(i, int) and 2 * i + h == 0):
                                copy_total(2 * i + h - 1, 1 - h)

                    rounds(act, SR, weigh, SLAST, BOTH)
                    copy_total(NG - 1, (NG - 1) % 2)

                @block.tensor
                def _(pe):
                    pe.wait_ge(nothing_ready, 1)

                    def unit(i, spans):
                        for h in range(spans):
                            g = 2 * i + h
                            after(pe, total_ready, g - 1)
                            nc.tensor.matmul(pw[h][:, :, :].rearrange("p v n -> p (v n)"),
                                             nothing[:, 0:P], nothing[:, :], start=True, stop=True)
                            for a in range(2):
                                u = 2 * g + a
                                off = pe.value_load(unit_off[0:1, bass.ds(u, 1)], min_val=0,
                                                    max_val=SPAN - WIN)
                                pe.wait_ge(rows_in[2 * h + a], 16 * (i + 1))
                                pe.wait_ge(by_vector, u + 1)
                                pe.wait_ge(by_scalar, u + 1)
                                if POOL_VIEWS:
                                    pe.wait_ge(by_pool, u + 1)
                                for k in range(TPU):
                                    last = nc.tensor.matmul(
                                        pw[h][:, :, bass.ds(off, WIN)], row_in[2 * h + a][:, k, 0:F],
                                        weighed[2 * h + a][:, k, :, :], start=False, stop=True,
                                        skip_group_check=True)
                                last.then_inc(unit_summed, 1)

                    rounds(pe, SR, unit, SLAST, BOTH)

                @block.gpsimd
                def _(pool):
                    def weigh(i, spans):
                        for h in range(spans):
                            g = 2 * i + h
                            if POOL_VIEWS:
                                for a in range(2):
                                    u = 2 * g + a
                                    gate(pool, put_ready, u + 1, pool_passed)
                                    for v in POOL_VIEWS:
                                        last = nc.gpsimd.tensor_tensor(
                                            weighed[2 * h + a][:, :, v, :], put[2 * h + a][:, :, :],
                                            aberr[:, v, bass.ds(u * TPU, TPU)].unsqueeze(2)
                                            .to_broadcast([P, TPU, WIN]), ALU.mult)
                                    last.then_inc(by_pool, 1)
                            if h == 0:
                                if not (isinstance(i, int) and i == 0):
                                    add(2 * i - 1, 1)
                            else:
                                add(2 * i, 0)

                    def add(g, h):
                        base = pool.value_load(span_base[0:1, bass.ds(g, 1)], min_val=0, max_val=N - SPAN)
                        gate(pool, total_ready, g + 1, pool_passed)
                        gate(pool, added, 16 * g, pool_passed)
                        pool.dma_start(aggT[:, :, bass.ds(base, SPAN)], total[h][:, :, :],
                                       accum_op=ALU.add).then_inc(added, 16)

                    rounds(pool, SR, weigh, SLAST, BOTH)
                    add(NG - 1, (NG - 1) % 2)
                    pool.wait_ge(added, 16 * NG)

        with nc.Else():
            with ExitStack() as ctx:
                row_in = [tensor(ctx, f"row_in{a}", [P, TPU, ROW]) for a in range(2)]
                node = [tensor(ctx, f"node{a}", [P, TPU]) for a in range(2)]
                share = [tensor(ctx, f"share{a}", [P, VIEWS, TPU]) for a in range(2)]
                same = [tensor(ctx, f"same{j}", [P, VIEWS, P]) for j in range(2)]
                scrap = [tensor(ctx, f"scrap{j}", [P, P]) for j in range(2)]
                before = [tensor(ctx, f"before{a}", [P, TPU]) for a in range(2)]
                to_trash = tensor(ctx, "to_trash", [P, TPU])
                moved = tensor(ctx, "moved", [P, TPU])
                at_node = [tensor(ctx, f"at_node{a}", [P, TPU], I32) for a in range(2)]
                total = [tensor(ctx, f"total{j}", [P, VIEWS * F]) for j in range(2)]
                pn = [bank(ctx, f"pn{j}", [P, P]) for j in range(2)]
                ps = [bank(ctx, f"ps{j}", [P, VIEWS * F]) for j in range(2)]
                rows_in = [sem(ctx, f"rows_in_b{a}") for a in range(2)]
                staged = sem(ctx, "staged")
                nodes_spread = sem(ctx, "nodes_spread")
                same_ready = sem(ctx, "same_ready")
                summed = sem(ctx, "summed")
                total_ready = sem(ctx, "total_ready")
                at_ready = sem(ctx, "at_ready")
                added = sem(ctx, "added")
                vector_step = sem(ctx, "vector_step3")
                block = ctx.enter_context(nc.Block())

                @block.sync
                def _(sp):
                    def load(g):
                        for a in range(2):
                            u = 2 * g + a
                            after(sp, summed, TPU * (u - 1))
                            sp.dma_start(row_in[a][:, :, :].rearrange("p k f -> p (k f)"),
                                         gathered[bass.ds(u, 1), :, :].rearrange("a p m -> (a p) m"))\
                                .then_inc(rows_in[a], 16)

                    rounds(sp, NG, load)

                @block.scalar
                def _(act):
                    def stage(g):
                        for a in range(2):
                            u = 2 * g + a
                            after(act, at_ready, u - 1)
                            after(act, same_ready, TPU * (u - 1))
                            nc.scalar.copy(node[a][:, :], dst_i[:, bass.ds(u * TPU, TPU)])
                            nc.scalar.copy(share[a][:, :, :], aberr[:, :, bass.ds(u * TPU, TPU)])\
                                .then_inc(staged, 1)
                        for a in range(2):
                            u = 2 * g + a
                            for k in range(TPU):
                                q = TPU * u + k
                                act.wait_ge(summed, q + 1)
                                after(act, added, 16 * (q - 1))
                                j = (TPU * a + k) % 2
                                nc.scalar.copy(total[j][:, :], ps[j][:, :]).then_inc(total_ready, 1)

                    rounds(act, NG, stage)

                @block.tensor
                def _(pe):
                    def unit(g):
                        for a in range(2):
                            u = 2 * g + a
                            pe.wait_ge(staged, u + 1)
                            pe.wait_ge(rows_in[a], 16 * (g + 1))
                            for k in range(TPU):
                                q, j = TPU * u + k, (TPU * a + k) % 2
                                after(pe, same_ready, q - 1)
                                nc.tensor.matmul(pn[j][:, :], node[a][:, k:k + 1].to_broadcast([P, P]),
                                                 ident[:, :], start=True, stop=True)\
                                    .then_inc(nodes_spread, 1)
                                pe.wait_ge(same_ready, q + 1)
                                after(pe, total_ready, q - 1)
                                for v in range(VIEWS):
                                    last = nc.tensor.matmul(ps[j][:, v * F:(v + 1) * F], same[j][:, v, :],
                                                            row_in[a][:, k, 0:F], start=True, stop=True)
                                last.then_inc(summed, 1)

                    rounds(pe, NG, unit)

                @block.vector
                def _(dve):
                    def unit(g):
                        for a in range(2):
                            u = 2 * g + a
                            chain = Chain(dve, vector_step, 3 * u)
                            dve.wait_ge(staged, u + 1)
                            for k in range(TPU):
                                q, j = TPU * u + k, (TPU * a + k) % 2
                                dve.wait_ge(nodes_spread, q + 1)
                                after(dve, summed, q - 1)
                                nc.vector.scalar_tensor_tensor(
                                    out=scrap[j][:, :], in0=pn[j][:, :], scalar=node[a][:, k:k + 1],
                                    in1=earlier[:, :], op0=ALU.is_equal, op1=ALU.mult,
                                    accum_out=before[a][:, k:k + 1])
                                for v in range(VIEWS):
                                    last = nc.vector.tensor_scalar(
                                        same[j][:, v, :], pn[j][:, :], node[a][:, k:k + 1],
                                        share[a][:, v, k:k + 1], ALU.is_equal, ALU.mult)
                                last.then_inc(same_ready, 1)
                            dve.wait_ge(same_ready, TPU * (u + 1))
                            after(dve, added, 16 * TPU * (u - 1))
                            chain.link(nc.vector.tensor_scalar(to_trash[:, :], node[a][:, :], -1.0,
                                                               trash[:, 0:1], ALU.mult, ALU.add))
                            chain.link(nc.vector.scalar_tensor_tensor(
                                out=moved[:, :], in0=before[a][:, :], scalar=0.5, in1=to_trash[:, :],
                                op0=ALU.is_gt, op1=ALU.mult))
                            chain.link(nc.vector.tensor_tensor(at_node[a][:, :], moved[:, :],
                                                               node[a][:, :], ALU.add))
                            dve.nop().then_inc(at_ready, 1)

                    rounds(dve, NG, unit)

                @block.gpsimd
                def _(pool):
                    def scatter(g):
                        for a in range(2):
                            u = 2 * g + a
                            gate(pool, at_ready, u + 1, pool_passed)
                            for k in range(TPU):
                                q, j = TPU * u + k, (TPU * a + k) % 2
                                pool.wait_ge(total_ready, q + 1)
                                gate(pool, added, 16 * q, pool_passed)
                                pool.indirect_dma_start(
                                    agg, bass.IndirectOffsetOnAxis(ap=at_node[a][:, k:k + 1], axis=0),
                                    total[j][:, :], None, compute_op=ALU.add).then_inc(added, 16)

                    rounds(pool, NG, scatter)
                    pool.wait_ge(added, 16 * TPU * NU)

            with ExitStack() as ctx:
                a_in = [tensor(ctx, f"t_in{s}", [P, VIEWS * F]) for s in range(2)]
                a_out = [tensor(ctx, f"t_out{s}", [P, VIEWS, P]) for s in range(2)]
                pa = [bank(ctx, f"t_pa{s}", [P, VIEWS, P]) for s in range(2)]
                a_loaded = [sem(ctx, f"t_loaded{s}") for s in range(2)]
                a_stored = [sem(ctx, f"t_stored{s}") for s in range(2)]
                a_transposed = sem(ctx, "t_transposed")
                a_copied = sem(ctx, "t_copied")
                block = ctx.enter_context(nc.Block())

                @block.sync
                def _(sp):
                    def load(i, r=FULL):
                        for s in range(2):
                            t = 2 * i + s
                            after(sp, a_transposed, t - 1)
                            sp.dma_start(a_in[s][0:r[s], :], rows(agg, t, r[s])).then_inc(a_loaded[s], 16)

                    rounds(sp, NT // 2, load, LAST)

                @block.tensor
                def _(pe):
                    def tile(i, r=FULL):
                        for s in range(2):
                            t = 2 * i + s
                            pe.wait_ge(a_loaded[s], 16 * (i + 1))
                            after(pe, a_copied, t - 1)
                            for v in range(VIEWS):
                                last = nc.tensor.transpose(pa[s][:, v, 0:r[s]],
                                                           a_in[s][0:r[s], v * F:(v + 1) * F],
                                                           ident[0:r[s], 0:r[s]])
                            last.then_inc(a_transposed, 1)

                    rounds(pe, NT // 2, tile, LAST)

                @block.scalar
                def _(act):
                    def tile(i, r=FULL):
                        for s in range(2):
                            t = 2 * i + s
                            act.wait_ge(a_transposed, t + 1)
                            after(act, a_stored[s], 16 * i)
                            nc.scalar.copy(a_out[s][:, :, 0:r[s]], pa[s][:, :, 0:r[s]])\
                                .then_inc(a_copied, 1)

                    rounds(act, NT // 2, tile, LAST)

                @block.gpsimd
                def _(pool):
                    def store(i, r=FULL):
                        for s in range(2):
                            t = 2 * i + s
                            gate(pool, a_copied, t + 1, pool_passed)
                            pool.dma_start(aggT[:, :, bass.ds(t * P, r[s])], a_out[s][:, :, 0:r[s]])\
                                .then_inc(a_stored[s], 16)

                    rounds(pool, NT // 2, store, LAST)
                    for s in range(2):
                        pool.wait_ge(a_stored[s], 16 * (NT // 2))

        with ExitStack() as both:
            bn_scale_c = tensor(both, "bn_scale_c", [P, VIEWS])
            bn_bias_c = tensor(both, "bn_bias_c", [P, VIEWS])
            l1_wT = tensor(both, "l1_wT", [P, F])
            with ExitStack() as ctx:
                NC = N // CHUNK
                BS = 5 if NC % 5 == 0 else 2
                a_in = [tensor(ctx, f"a_in{s}", [P, VIEWS, CHUNK]) for s in range(BS)]
                stats = tensor(ctx, "stats", [P, VIEWS, NC * 6])
                moments = tensor(ctx, "moments", [P, VIEWS, 2])
                small = tensor(ctx, "small", [P, VIEWS])
                soft = tensor(ctx, "soft", [VIEWS, F])
                peak = tensor(ctx, "peak", [VIEWS, 1])
                mass = tensor(ctx, "mass", [VIEWS, 1])
                softT = tensor(ctx, "softT", [P, VIEWS])
                pw = bank(ctx, "pw", [P, P])
                px = bank(ctx, "px", [P, P])
                a_loaded = [sem(ctx, f"a_loaded{s}") for s in range(BS)]
                a_measured = sem(ctx, "a_measured")
                peak_ready = sem(ctx, "peak_ready")
                soft_ready = sem(ctx, "soft_ready")
                soft_scaled = sem(ctx, "soft_scaled")
                turned = sem(ctx, "turned")
                variance_ready = sem(ctx, "variance_ready")
                deviation_ready = sem(ctx, "deviation_ready")
                vector_step = sem(ctx, "vector_step4")
                block = ctx.enter_context(nc.Block())

                @block.sync
                def _(sp):
                    def load(i):
                        for s in range(BS):
                            c = BS * i + s
                            after(sp, a_measured, c - BS + 1)
                            sp.dma_start(a_in[s][:, :, :], aggT[:, :, bass.ds(c * CHUNK, CHUNK)])\
                                .then_inc(a_loaded[s], 16)

                    rounds(sp, NC // BS, load)

                @block.tensor
                def _(pe):
                    nc.tensor.transpose(pw[:, :], l1_w[:, :], ident[:, :]).then_inc(turned, 1)
                    pe.wait_ge(soft_scaled, 1)
                    nc.tensor.transpose(px[:, 0:VIEWS], soft[:, :], ident[0:VIEWS, 0:VIEWS])\
                        .then_inc(turned, 1)

                @block.scalar
                def _(act):
                    act.wait_ge(peak_ready, 1)
                    nc.scalar.activation(soft[:, :], att[:, :], ACT.Exp, bias=peak[:, 0:1],
                                         accum_out=mass[:, 0:1]).then_inc(soft_ready, 1)
                    act.wait_ge(variance_ready, 1)
                    nc.scalar.activation(small[:, :], small[:, :], ACT.Sqrt)\
                        .then_inc(deviation_ready, 1)

                @block.vector
                def _(dve):
                    def chunk(i):
                        for s in range(BS):
                            c = BS * i + s
                            dve.wait_ge(a_loaded[s], 16 * (i + 1))
                            for v in range(VIEWS):
                                last = nc.vector.bn_stats(stats[:, v, bass.ds(c * 6, 6)],
                                                          a_in[s][:, v, :])
                            last.then_inc(a_measured, 1)

                    rounds(dve, NC // BS, chunk)
                    chain = Chain(dve, vector_step)
                    chain.link(nc.vector.tensor_reduce(peak[:, :], att[:, :], axis=AX.X, op=ALU.max))
                    chain.link(nc.vector.tensor_scalar(peak[:, :], peak[:, :], -1.0, None, ALU.mult))
                    dve.nop().then_inc(peak_ready, 1)
                    dve.wait_ge(a_measured, NC)
                    for v in range(VIEWS):
                        chain.link(nc.vector.bn_aggr(moments[:, v, :], stats[:, v, :]))
                    chain.link(nc.vector.tensor_scalar(small[:, :], moments[:, :, 1], EPS, None,
                                                       ALU.add))
                    dve.nop().then_inc(variance_ready, 1)
                    dve.wait_ge(soft_ready, 1)
                    chain.link(nc.vector.reciprocal(mass[:, :], mass[:, :]))
                    chain.link(nc.vector.tensor_scalar(soft[:, :], soft[:, :], mass[:, 0:1], None,
                                                       ALU.mult))
                    dve.nop().then_inc(soft_scaled, 1)
                    dve.wait_ge(deviation_ready, 1)
                    chain.link(nc.vector.reciprocal(small[:, :], small[:, :]))
                    chain.link(nc.vector.tensor_tensor(bn_scale_c[:, :], small[:, :], bn_s[:, :],
                                                       ALU.mult))
                    chain.link(nc.vector.tensor_tensor(small[:, :], bn_scale_c[:, :],
                                                       moments[:, :, 0], ALU.mult))
                    chain.link(nc.vector.tensor_tensor(bn_bias_c[:, :], bn_b[:, :], small[:, :],
                                                       ALU.subtract))
                    dve.wait_ge(turned, 2)
                    chain.link(nc.vector.tensor_copy(l1_wT[:, :], pw[:, :]))
                    chain.link(nc.vector.tensor_copy(softT[:, :], px[:, 0:VIEWS]))
                    chain.link(nc.vector.tensor_tensor(bn_scale_c[:, :], bn_scale_c[:, :],
                                                       softT[:, :], ALU.mult))
                    chain.link(nc.vector.tensor_tensor(bn_bias_c[:, :], bn_bias_c[:, :],
                                                       softT[:, :], ALU.mult))

            with ExitStack() as ctx:
                a_in = [tensor(ctx, f"a_again{h}", [P, VIEWS, 4 * P]) for h in range(2)]
                view = [tensor(ctx, f"view{h}", [P, VIEWS, 4 * P]) for h in range(2)]
                x_in = [tensor(ctx, f"x_again{h}", [P, 4, F]) for h in range(2)]
                z_n = [tensor(ctx, f"z_n{h}", [P, 4, Z]) for h in range(2)]
                z_r = tensor(ctx, "z_r", [P, ZB, 4 * P])
                y = tensor(ctx, "y", [P, 4, F])
                x1 = [tensor(ctx, f"x1{h}", [P, 4, F]) for h in range(2)]
                x1T = tensor(ctx, "x1T", [P, 4 * P])
                h1 = [tensor(ctx, f"h1{h}", [P, 4, F]) for h in range(2)]
                zstat, zmom = tensor(ctx, "zstat", [P, 4, 6]), tensor(ctx, "zmom", [P, 4, 2])
                ystat, ymom = tensor(ctx, "ystat", [P, 4, 6]), tensor(ctx, "ymom", [P, 4, 2])
                zdev, ydev = tensor(ctx, "zdev", [P, 4]), tensor(ctx, "ydev", [P, 4])
                pz = [bank(ctx, f"pz{h}", [P, 4, Z]) for h in range(2)]
                pt = bank(ctx, "pt_z", [P, ZB, 4 * P])
                py = bank(ctx, "py", [P, 4, F])
                px = bank(ctx, "px1", [P, 4 * P])
                names = ("view_ready", "z_summed", "z_dev", "z_root", "z_ready", "z_turned", "z_relu",
                         "y_summed", "y_dev", "y_root", "x1_ready", "x1_turned", "x1T_ready",
                         "h1_summed", "h1_added", "h1_ready", "x_biased")
                (view_ready, z_summed, z_dev, z_root, z_ready, z_turned, z_relu, y_summed, y_dev,
                 y_root, x1_ready, x1_turned, x1T_ready, h1_summed, h1_added, h1_ready, x_biased) = (
                    sem(ctx, n) for n in names)
                loaded = [sem(ctx, f"loaded{h}") for h in range(2)]
                x_loaded = [sem(ctx, f"x_again_loaded{h}") for h in range(2)]
                x1_stored = [sem(ctx, f"x1_stored{h}") for h in range(2)]
                h1_stored = [sem(ctx, f"h1_stored{h}") for h in range(2)]
                z_step, y_step = sem(ctx, "z_step"), sem(ctx, "y_step")
                block = ctx.enter_context(nc.Block())


                @block.sync
                def _(sp):
                    def load(q):
                        if missing(q):
                            return
                        m = sum(sizes(q))
                        after(sp, view_ready, q.c - 1)
                        sp.dma_start(a_in[q.h][:, :, 0:m], aggT[:, :, bass.ds(q.c * (4 * P), m)])\
                            .then_inc(loaded[q.h], 16)
                        after(sp, y_dev, q.c - 1)
                        for t, k, n in stretches(q):
                            sp.dma_start(x_in[q.h][0:n, t:t + k, :], quad_rows(x, q, t, k, n))\
                                .then_inc(x_loaded[q.h], 16)

                    def store(table, held, ready, stored, q):
                        if missing(q):
                            return
                        sp.wait_ge(ready, q.c + 1)
                        for t, k, n in stretches(q):
                            sp.dma_start(quad_rows(table, q, t, k, n), held[q.h][0:n, t:t + k, :])\
                                .then_inc(stored[q.h], 16)

                    def body(q):
                        load(q)
                        store(x1_rows, x1, x1_ready, x1_stored, q.back(3))
                        store(h1_table, h1, h1_ready, h1_stored, q.back(3))

                    quads(sp, body)
                    for q in (Quad(NQ - 2, (NQ - 2) % 2), Quad(NQ - 1, (NQ - 1) % 2)):
                        sp.wait_ge(x1_stored[q.h], landed(q))
                        sp.wait_ge(h1_stored[q.h], landed(q))

                @block.gpsimd
                def _(pool):
                    def add_bias(q):
                        if missing(q):
                            return
                        pool.wait_ge(x_loaded[q.h], landed(q))
                        for t, k, n in stretches(q):
                            last = nc.gpsimd.tensor_tensor(
                                x_in[q.h][0:n, t:t + k, :], x_in[q.h][0:n, t:t + k, :],
                                b2_all[0:n, :].unsqueeze(1).to_broadcast([n, k, F]), ALU.add)
                        last.then_inc(x_biased, 1)

                    quads(pool, add_bias)

                @block.tensor
                def _(pe):
                    def sum_z(q):
                        if missing(q):
                            return
                        pe.wait_ge(view_ready, q.c + 1)
                        after(pe, z_dev, q.c - 1)
                        for t, n in enumerate(sizes(q)):
                            for v in range(VIEWS):
                                last = nc.tensor.matmul(pz[q.h][0:n, t, :],
                                                        view[q.h][:, v, t * P:t * P + n], w1[:, v, :],
                                                        start=(v == 0), stop=(v == VIEWS - 1))
                        last.then_inc(z_summed, 1)

                    def turn_z(q):
                        if missing(q):
                            return
                        pe.wait_ge(z_ready, q.c + 1)
                        after(pe, z_relu, q.c)
                        for t, n in enumerate(sizes(q)):
                            for b in range(ZB):
                                last = nc.tensor.transpose(pt[:, b, t * P:t * P + n],
                                                           z_n[q.h][0:n, t, b * P:(b + 1) * P],
                                                           ident[0:n, 0:n])
                        last.then_inc(z_turned, 1)

                    def sum_y(q):
                        if missing(q):
                            return
                        pe.wait_ge(z_relu, q.c + 1)
                        after(pe, y_dev, q.c)
                        for t, n in enumerate(sizes(q)):
                            for b in range(ZB):
                                last = nc.tensor.matmul(py[0:n, t, :], z_r[:, b, t * P:t * P + n],
                                                        w2[:, b, :], start=(b == 0),
                                                        stop=(b == ZB - 1))
                        last.then_inc(y_summed, 1)

                    def turn_x1(q):
                        if missing(q):
                            return
                        pe.wait_ge(x1_ready, q.c + 1)
                        after(pe, h1_added, q.c)
                        for t, n in enumerate(sizes(q)):
                            last = nc.tensor.transpose(px[:, t * P:t * P + n], x1[q.h][0:n, t, :],
                                                       ident[0:n, 0:n])
                        last.then_inc(x1_turned, 1)

                    def sum_h1(q):
                        if missing(q):
                            return
                        pe.wait_ge(x1T_ready, q.c + 1)
                        for t, n in enumerate(sizes(q)):
                            last = nc.tensor.matmul(px[0:n, t * P:(t + 1) * P],
                                                    x1T[:, t * P:t * P + n], l1_wT[:, :],
                                                    start=True, stop=True)
                        last.then_inc(h1_summed, 1)

                    def body(q):
                        sum_z(q)
                        turn_x1(q.back(2))
                        turn_z(q.back(1))
                        sum_h1(q.back(2))
                        sum_y(q.back(1))

                    quads(pe, body)

                @block.scalar
                def _(act):
                    def make_view(q):
                        if missing(q):
                            return
                        m = sum(sizes(q))
                        act.wait_ge(loaded[q.h], 16 * (q.c // 2 + 1) if isinstance(q.c, int) else
                                    16 * ((q.c - q.h) // 2) + 16)
                        after(act, z_summed, q.c - 1)
                        for v in range(VIEWS):
                            last = nc.scalar.activation(view[q.h][:, v, 0:m], a_in[q.h][:, v, 0:m],
                                                        ACT.Relu, bias=bn_bias_c[:, v:v + 1],
                                                        scale=bn_scale_c[:, v:v + 1])
                        last.then_inc(view_ready, 1)

                    def root(q, dev, dev_ready, rooted):
                        if missing(q):
                            return
                        act.wait_ge(dev_ready, q.c + 1)
                        for t, k, n in stretches(q):
                            last = nc.scalar.activation(dev[0:n, t:t + k], dev[0:n, t:t + k], ACT.Sqrt)
                        last.then_inc(rooted, 1)

                    def relu_z(q):
                        if missing(q):
                            return
                        m = sum(sizes(q))
                        act.wait_ge(z_turned, q.c + 1)
                        after(act, y_summed, q.c)
                        for b in range(ZB):
                            last = nc.scalar.activation(z_r[:, b, 0:m], pt[:, b, 0:m], ACT.Relu,
                                                        bias=ln_b[:, b:b + 1], scale=ln_s[:, b:b + 1])
                        last.then_inc(z_relu, 1)

                    def copy_x1T(q):
                        if missing(q):
                            return
                        m = sum(sizes(q))
                        act.wait_ge(x1_turned, q.c + 1)
                        after(act, h1_summed, q.c)
                        nc.scalar.copy(x1T[:, 0:m], px[:, 0:m]).then_inc(x1T_ready, 1)

                    def relu_h1(q):
                        if missing(q):
                            return
                        act.wait_ge(h1_added, q.c + 1)
                        for t, k, n in stretches(q):
                            last = nc.scalar.activation(h1[q.h][0:n, t:t + k, :],
                                                        h1[q.h][0:n, t:t + k, :], ACT.Relu)
                        last.then_inc(h1_ready, 1)

                    def body(q):
                        copy_x1T(q.back(2))
                        root(q, zdev, z_dev, z_root)
                        relu_z(q.back(1))
                        make_view(q.back(-1))
                        relu_h1(q.back(2))
                        root(q.back(1), ydev, y_dev, y_root)

                    make_view(Quad(0, 0))
                    quads(act, body)

                @block.vector
                def _(dve):
                    STEPS = 4

                    def moments(chain, q, held, stat, mom, dev, dev_ready):
                        for t, n in enumerate(sizes(q)):
                            last = nc.vector.bn_stats(stat[0:n, t, :], held[0:n, t, :])
                        chain.link(last)
                        dve.sem_inc(vector_passed, 1)
                        for t, n in enumerate(sizes(q)):
                            last = nc.vector.bn_aggr(mom[0:n, t, :], stat[0:n, t, :])
                        chain.link(last)
                        for t, k, n in stretches(q):
                            last = nc.vector.tensor_scalar(dev[0:n, t:t + k], mom[0:n, t:t + k, 1],
                                                           EPS, None, ALU.add)
                        last.then_inc(dev_ready, 1)

                    def normed(chain, q, to, held, mom, dev, rooted, ready):
                        dve.wait_ge(rooted, q.c + 1)
                        for t, k, n in stretches(q):
                            last = nc.vector.reciprocal(dev[0:n, t:t + k], dev[0:n, t:t + k])
                        chain.link(last)
                        for t, n in enumerate(sizes(q)):
                            last = nc.vector.tensor_scalar(to[0:n, t, :], held[0:n, t, :],
                                                           mom[0:n, t, 0:1], dev[0:n, t:t + 1],
                                                           ALU.subtract, ALU.mult)
                        last.then_inc(ready, 1)

                    def norm_z(q):
                        if missing(q):
                            return
                        chain = Chain(dve, z_step, STEPS * q.c)
                        dve.wait_ge(z_summed, q.c + 1)
                        after(dve, z_turned, q.c - 1)
                        for t, k, n in stretches(q):
                            last = nc.vector.tensor_tensor(
                                z_n[q.h][0:n, t:t + k, :], pz[q.h][0:n, t:t + k, :],
                                b1_all[0:n, :].unsqueeze(1).to_broadcast([n, k, Z]), ALU.add)
                        chain.link(last)
                        moments(chain, q, z_n[q.h], zstat, zmom, zdev, z_dev)
                        normed(chain, q, z_n[q.h], z_n[q.h], zmom, zdev, z_root, z_ready)
                        assert chain.n == STEPS

                    def norm_y(q):
                        if missing(q):
                            return
                        chain = Chain(dve, y_step, STEPS * q.c)
                        dve.wait_ge(y_summed, q.c + 1)
                        dve.wait_ge(x_biased, q.c + 1)
                        for t, k, n in stretches(q):
                            last = nc.vector.tensor_tensor(y[0:n, t:t + k, :], py[0:n, t:t + k, :],
                                                           x_in[q.h][0:n, t:t + k, :], ALU.add)
                        chain.link(last)
                        moments(chain, q, y, ystat, ymom, ydev, y_dev)
                        after(dve, x1_turned, q.c - 1)
                        if not (isinstance(q.c, int) and q.c < 2):
                            dve.wait_ge(x1_stored[q.h], landed(q.back(2)))
                        normed(chain, q, x1[q.h], y, ymom, ydev, y_root, x1_ready)
                        assert chain.n == STEPS

                    def add_h1(q):
                        if missing(q):
                            return
                        dve.wait_ge(h1_summed, q.c + 1)
                        if not (isinstance(q.c, int) and q.c < 2):
                            dve.wait_ge(h1_stored[q.h], landed(q.back(2)))
                        for t, k, n in stretches(q):
                            last = nc.vector.tensor_tensor(
                                h1[q.h][0:n, t:t + k, :],
                                px[0:n, t * P:(t + k) * P].rearrange("p (t f) -> p t f", t=k),
                                l1_b_all[0:n, :].unsqueeze(1).to_broadcast([n, k, F]), ALU.add)
                        last.then_inc(h1_added, 1)

                    def body(q):
                        norm_z(q)
                        add_h1(q.back(2))
                        norm_y(q.back(1))

                    quads(dve, body)

        with nc.If(is_sorted()):
            with ExitStack() as ctx:
                slots = [tensor(ctx, f"m_slots{a}", [P, TPU], BF16) for a in range(2)]
                lo = [tensor(ctx, f"m_lo{a}", [P, TPU], BF16) for a in range(2)]
                hi = [tensor(ctx, f"m_hi{a}", [P, TPU], BF16) for a in range(2)]
                at_src = [tensor(ctx, f"m_at_src{a}", [P, TPU], I32) for a in range(2)]
                node = [tensor(ctx, f"m_node{a}", [P, TPU]) for a in range(2)]
                share = [tensor(ctx, f"m_share{a}", [P, TPU]) for a in range(2)]
                h_win = [tensor(ctx, f"m_h_win{a}", [P, F]) for a in range(2)]
                win_parts = [tensor(ctx, f"m_win_parts{a}", [P, 2, F + 1], BF16) for a in range(2)]
                win_high = tensor(ctx, "m_win_high", [P, F], BF16)
                win_rest = tensor(ctx, "m_win_rest", [P, F])
                win_middle = tensor(ctx, "m_win_middle", [WIN, F], BF16)
                at_win = tensor(ctx, "m_at_win", [P, 1])
                pick = [tensor(ctx, f"m_pick{a}", [P, TPU * P], BF16) for a in range(2)]
                h_row = [tensor(ctx, f"m_h_row{k}", [P, F + 1]) for k in range(TPU)]
                same = [tensor(ctx, f"m_same{k}", [P, P]) for k in range(TPU)]
                scrap = [tensor(ctx, f"m_scrap{j}", [P, P]) for j in range(2)]
                before = [tensor(ctx, f"m_before{a}", [P, TPU]) for a in range(2)]
                to_trash = tensor(ctx, "m_to_trash", [P, TPU])
                moved = tensor(ctx, "m_moved", [P, TPU])
                total = [[tensor(ctx, f"m_total{a}{k}", [P, F + 1]) for k in range(TPU)]
                         for a in range(2)]
                pr = bank(ctx, "m_pr", [P, 1024])
                pn = [bank(ctx, f"m_pn{j}", [P, P]) for j in range(2)]
                ph = [bank(ctx, f"m_ph{j}", [P, F + 1]) for j in range(2)]
                ps = [bank(ctx, f"m_ps{j}", [P, F + 1]) for j in range(2)]
                (ones_ready, slots_ready, staged, slots_spread, pick_ready, nodes_spread, h_picked,
                 h_ready, same_ready, summed, total_ready, at_ready) = (
                    sem(ctx, f"m_{n}") for n in (
                        "ones_ready", "slots_ready", "staged", "slots_spread", "pick_ready",
                        "nodes_spread", "h_picked", "h_ready", "same_ready", "summed", "total_ready",
                        "at_ready"))
                high_ready = sem(ctx, "m_high_ready")
                rest_ready = sem(ctx, "m_rest_ready")
                middle_ready = sem(ctx, "m_middle_ready")
                low_ready = sem(ctx, "m_low_ready")
                halves_ready = sem(ctx, "m_halves_ready")
                trash_found = sem(ctx, "m_trash_found")
                moved_found = sem(ctx, "m_moved_found")
                window_in = [sem(ctx, f"m_window_in{a}") for a in range(2)]
                added = [sem(ctx, f"m_added{k}") for k in range(TPU)]
                block = ctx.enter_context(nc.Block())

                LAG = 2

                def lagging(u, a, k):
                    if k >= LAG:
                        return u, a, k - LAG
                    if isinstance(u, int) and u == 0:
                        return None
                    return u - 1, 1 - a, k - LAG + TPU

                def is_last(g, a):
                    return isinstance(g, int) and g == NG - 1 and a == 1

                @block.sync
                def _(sp):
                    def load(g):
                        for a in range(2):
                            u = 2 * g + a
                            base = sp.value_load(unit_base[0:1, bass.ds(u, 1)], min_val=0,
                                                 max_val=N - WIN)
                            after(sp, middle_ready, u - 1)
                            for half in range(2):
                                sp.dma_start(h_win[a][half * WIN:(half + 1) * WIN, :],
                                             h1_table[bass.ds(base, WIN), :])\
                                    .then_inc(window_in[a], 16)

                    rounds(sp, NG, load, unroll=2)

                @block.scalar
                def _(act):
                    def stage_slots(u, a):
                        here = bass.ds(u * TPU, TPU)
                        after(act, slots_spread, u - 1)
                        nc.scalar.copy(slots[a][:, :], slot_b[:, here]).then_inc(slots_ready, 1)

                    def stage(u, a):
                        here = bass.ds(u * TPU, TPU)
                        after(act, at_ready, u - 1)
                        nc.scalar.copy(lo[a][:, :], src_lo[:, here])
                        nc.scalar.copy(hi[a][:, :], src_hi[:, here])
                        nc.scalar.copy(node[a][:, :], src_i[:, here])
                        nc.scalar.copy(share[a][:, :], ew[:, here]).then_inc(staged, 1)

                    def cast_high(g, u, a):
                        act.wait_ge(window_in[a], 32 * (g + 1))
                        after(act, rest_ready, u)
                        nc.scalar.copy(win_high[:, :], h_win[a][:, :]).then_inc(high_ready, 1)
                        after(act, h_picked, TPU * (u - 1))
                        nc.scalar.copy(win_parts[a][0:WIN, 0, 0:F], h_win[a][0:WIN, :])

                    def cast_middle(u, a):
                        act.wait_ge(rest_ready, u + 1)
                        after(act, low_ready, u)
                        nc.scalar.copy(win_middle[:, :], win_rest[0:WIN, :])
                        nc.scalar.copy(win_parts[a][WIN:P, 0, 0:F], win_rest[WIN:P, :])\
                            .then_inc(middle_ready, 1)

                    def copy_total(u, a, k):
                        q, j = TPU * u + k, (TPU * a + k) % 2
                        act.wait_ge(summed, q + 1)
                        after(act, added[k], 16 * (u - 1))
                        nc.scalar.copy(total[a][k][:, :], ps[j][:, :]).then_inc(total_ready, 1)

                    def unit(g):
                        for a in range(2):
                            u = 2 * g + a
                            for k in range(TPU):
                                q, j = TPU * u + k, (TPU * a + k) % 2
                                act.wait_ge(h_picked, q + 1)
                                nc.scalar.copy(h_row[k][:, :], ph[j][:, :]).then_inc(h_ready, 1)
                                if lagging(u, a, k):
                                    copy_total(*lagging(u, a, k))
                                if k == 0 and not is_last(g, a):
                                    cast_high(g + a, u + 1, 1 - a)
                                if k == 1 and not is_last(g, a):
                                    stage_slots(u + 1, 1 - a)
                                if k == 2 and not is_last(g, a):
                                    cast_middle(u + 1, 1 - a)
                                    stage(u + 1, 1 - a)

                    stage_slots(0, 0)
                    stage(0, 0)
                    cast_high(0, 0, 0)
                    cast_middle(0, 0)
                    rounds(act, NG, unit, unroll=2)
                    for k in range(TPU - LAG, TPU):
                        copy_total(NU - 1, 1, k)

                @block.tensor
                def _(pe):
                    def spread_slots(u, a):
                        pe.wait_ge(slots_ready, u + 1)
                        after(pe, pick_ready, u)
                        for k in range(TPU):
                            last = nc.tensor.matmul(pr[:, k * P:(k + 1) * P],
                                                    slots[a][:, k:k + 1].to_broadcast([P, P]),
                                                    ident_b[:, :], start=True, stop=True)
                        last.then_inc(slots_spread, 1)

                    def sum_tile(u, a, k, drained=False):
                        q, j = TPU * u + k, (TPU * a + k) % 2
                        if drained:
                            pe.wait_ge(same_ready, q + 1)
                            pe.wait_ge(h_ready, q + 1)
                        after(pe, total_ready, q - 1)
                        nc.tensor.matmul(ps[j][:, :], same[k][:, :], h_row[k][:, :],
                                         start=True, stop=True).then_inc(summed, 1)

                    def unit(g):
                        for a in range(2):
                            u = 2 * g + a
                            pe.wait_ge(staged, u + 1)
                            for k in range(TPU):
                                q, j = TPU * u + k, (TPU * a + k) % 2
                                after(pe, same_ready, q - 1)
                                nc.tensor.matmul(pn[j][:, :], lo[a][:, k:k + 1].to_broadcast([P, P]),
                                                 ident_b[:, :], start=True, stop=False)
                                nc.tensor.matmul(pn[j][:, :], hi[a][:, k:k + 1].to_broadcast([P, P]),
                                                 ident_b[:, :], start=False, stop=True)\
                                    .then_inc(nodes_spread, 1)
                                if k == 0:
                                    pe.wait_ge(pick_ready, u + 1)
                                    pe.wait_ge(middle_ready, u + 1)
                                    pe.wait_ge(low_ready, u + 1)
                                after(pe, h_ready, q - 1)
                                nc.tensor.matmul(ph[j][:, :], pick[a][:, k * P:(k + 1) * P],
                                                 win_parts[a][:, 0, :], start=True, stop=False)
                                nc.tensor.matmul(ph[j][:, :], pick[a][0:WIN, k * P:(k + 1) * P],
                                                 win_parts[a][0:WIN, 1, :], start=False, stop=True)\
                                    .then_inc(h_picked, 1)
                                if lagging(u, a, k):
                                    sum_tile(*lagging(u, a, k))
                                if k == 2 and not is_last(g, a):
                                    spread_slots(u + 1, 1 - a)

                    pe.wait_ge(ones_ready, 6)
                    spread_slots(0, 0)
                    rounds(pe, NG, unit, unroll=2)
                    for k in range(TPU - LAG, TPU):
                        sum_tile(NU - 1, 1, k, drained=True)

                @block.vector
                def _(dve):
                    for a in range(2):
                        for held, value in ((win_parts[a][0:WIN, 0, F:F + 1], 1.0),
                                            (win_parts[a][WIN:P, 0, F:F + 1], 0.0),
                                            (win_parts[a][0:WIN, 1, F:F + 1], 0.0)):
                            nc.vector.memset(held, value).then_inc(ones_ready, 1)
                    nc.vector.tensor_scalar(at_win[:, :], count_p[:, :], WIN - 0.5, -float(WIN),
                                            ALU.is_gt, ALU.mult).then_inc(halves_ready, 1)
                    dve.wait_ge(halves_ready, 1)
                    nc.vector.tensor_tensor(at_win[:, :], at_win[:, :], count_p[:, :], ALU.add)\
                        .then_inc(halves_ready, 1)
                    dve.wait_ge(halves_ready, 2)

                    def take_rest(u, a):
                        dve.wait_ge(high_ready, u + 1)
                        after(dve, middle_ready, u)
                        nc.vector.tensor_tensor(win_rest[:, :], h_win[a][:, :], win_high[:, :],
                                                ALU.subtract).then_inc(rest_ready, 1)

                    def take_low(u, a):
                        dve.wait_ge(middle_ready, u + 1)
                        after(dve, h_picked, TPU * (u - 1))
                        nc.vector.tensor_tensor(win_parts[a][0:WIN, 1, 0:F], win_rest[0:WIN, :],
                                                win_middle[:, :], ALU.subtract).then_inc(low_ready, 1)

                    def make_pick(u, a):
                        dve.wait_ge(slots_spread, u + 1)
                        after(dve, h_picked, TPU * (u - 1))
                        nc.vector.tensor_scalar(pick[a][:, :], pr[:, 0:TPU * P], at_win[:, 0:1], None, ALU.is_equal)\
                            .then_inc(pick_ready, 1)

                    def find_moved(u, a):
                        dve.wait_ge(same_ready, TPU * (u + 1))
                        dve.wait_ge(trash_found, u + 1)
                        nc.vector.scalar_tensor_tensor(
                            out=moved[:, :], in0=before[a][:, :], scalar=0.5, in1=to_trash[:, :],
                            op0=ALU.is_gt, op1=ALU.mult).then_inc(moved_found, 1)

                    def find_rows(u, a):
                        dve.wait_ge(moved_found, u + 1)
                        nc.vector.tensor_tensor(at_src[a][:, :], moved[:, :], node[a][:, :],
                                                ALU.add).then_inc(at_ready, 1)

                    def unit(g):
                        for a in range(2):
                            u = 2 * g + a
                            dve.wait_ge(staged, u + 1)
                            for k in range(TPU):
                                q, j = TPU * u + k, (TPU * a + k) % 2
                                dve.wait_ge(nodes_spread, q + 1)
                                nc.vector.scalar_tensor_tensor(
                                    out=scrap[j][:, :], in0=pn[j][:, :], scalar=node[a][:, k:k + 1],
                                    in1=earlier[:, :], op0=ALU.is_equal, op1=ALU.mult,
                                    accum_out=before[a][:, k:k + 1])
                                after(dve, added[k], 16 * (u - 1))
                                nc.vector.tensor_scalar(
                                    same[k][:, :], pn[j][:, :], node[a][:, k:k + 1],
                                    share[a][:, k:k + 1], ALU.is_equal, ALU.mult)\
                                    .then_inc(same_ready, 1)
                                if k == 0 and not (isinstance(u, int) and u == 0):
                                    find_moved(u - 1, 1 - a)
                                if k == 1:
                                    if not (isinstance(u, int) and u == 0):
                                        find_rows(u - 1, 1 - a)
                                    nc.vector.tensor_scalar(to_trash[:, :], node[a][:, :], -1.0,
                                                            trash[:, 0:1], ALU.mult, ALU.add)\
                                        .then_inc(trash_found, 1)
                                if k == 1 and not is_last(g, a):
                                    take_rest(u + 1, 1 - a)
                                if k == 3 and not is_last(g, a):
                                    make_pick(u + 1, 1 - a)
                                    take_low(u + 1, 1 - a)

                    take_rest(0, 0)
                    take_low(0, 0)
                    make_pick(0, 0)
                    rounds(dve, NG, unit, unroll=2)
                    find_moved(NU - 1, 1)
                    find_rows(NU - 1, 1)

                @block.gpsimd
                def _(pool):
                    def scatter(g):
                        for a in range(2):
                            u = 2 * g + a
                            gate(pool, at_ready, u + 1, pool_passed)
                            for k in range(TPU):
                                gate(pool, total_ready, TPU * u + k + 1, pool_passed)
                                gate(pool, added[k], 16 * u, pool_passed)
                                pool.indirect_dma_start(
                                    sums[k], bass.IndirectOffsetOnAxis(ap=at_src[a][:, k:k + 1], axis=0),
                                    total[a][k][:, :], None, compute_op=ALU.add).then_inc(added[k], 16)

                    rounds(pool, NG, scatter, unroll=2)
                    for k in range(TPU):
                        pool.wait_ge(added[k], 16 * NU)

        with nc.Else():
            with ExitStack() as ctx:
                at_dst = [tensor(ctx, f"l1_at_dst{a}", [P, TPU], I32) for a in range(2)]
                at_src = [tensor(ctx, f"l1_at_src{a}", [P, TPU], I32) for a in range(2)]
                node = [tensor(ctx, f"l1_node{a}", [P, TPU]) for a in range(2)]
                share = [tensor(ctx, f"l1_share{a}", [P, TPU]) for a in range(2)]
                h_row = [tensor(ctx, f"h_row{a}", [P, TPU, F + 1]) for a in range(2)]
                same = [tensor(ctx, f"l1_same{j}", [P, P]) for j in range(2)]
                scrap = [tensor(ctx, f"l1_scrap{j}", [P, P]) for j in range(2)]
                before = [tensor(ctx, f"l1_before{a}", [P, TPU]) for a in range(2)]
                to_trash = tensor(ctx, "l1_to_trash", [P, TPU])
                moved = tensor(ctx, "l1_moved", [P, TPU])
                total = [tensor(ctx, f"l1_total{k}", [P, F + 1]) for k in range(TPU)]
                pn = [bank(ctx, f"l1_pn{j}", [P, P]) for j in range(2)]
                ps = [bank(ctx, f"l1_ps{j}", [P, F + 1]) for j in range(2)]
                ones_ready = sem(ctx, "ones_ready")
                staged = sem(ctx, "l1_staged")
                index_ready = sem(ctx, "l1_index_ready")
                rows_in = [sem(ctx, f"l1_rows_in{a}") for a in range(2)]
                nodes_spread = sem(ctx, "l1_nodes_spread")
                same_ready = sem(ctx, "l1_same_ready")
                summed = sem(ctx, "l1_summed")
                total_ready = sem(ctx, "l1_total_ready")
                at_ready = sem(ctx, "l1_at_ready")
                added = [sem(ctx, f"l1_added{k}") for k in range(TPU)]
                vector_step = sem(ctx, "vector_step6")
                block = ctx.enter_context(nc.Block())

                @block.scalar
                def _(act):
                    def stage(g):
                        for a in range(2):
                            u = 2 * g + a
                            after(act, rows_in[a], 16 * TPU * g)
                            nc.scalar.copy(at_dst[a][:, :], dst_i[:, bass.ds(u * TPU, TPU)])\
                                .then_inc(index_ready, 1)
                            after(act, at_ready, u - 1)
                            nc.scalar.copy(node[a][:, :], src_i[:, bass.ds(u * TPU, TPU)])
                            nc.scalar.copy(share[a][:, :], ew[:, bass.ds(u * TPU, TPU)])\
                                .then_inc(staged, 1)
                        for a in range(2):
                            u = 2 * g + a
                            for k in range(TPU):
                                q, j = TPU * u + k, (TPU * a + k) % 2
                                act.wait_ge(summed, q + 1)
                                after(act, added[k], 16 * u)
                                nc.scalar.copy(total[k][:, :], ps[j][:, :]).then_inc(total_ready, 1)

                    rounds(act, NG, stage)

                @block.tensor
                def _(pe):
                    def unit(g):
                        for a in range(2):
                            u = 2 * g + a
                            pe.wait_ge(staged, u + 1)
                            for k in range(TPU):
                                q, j = TPU * u + k, (TPU * a + k) % 2
                                after(pe, same_ready, q - 1)
                                nc.tensor.matmul(pn[j][:, :], node[a][:, k:k + 1].to_broadcast([P, P]),
                                                 ident[:, :], start=True, stop=True)\
                                    .then_inc(nodes_spread, 1)
                                if k == 0:
                                    pe.wait_ge(rows_in[a], 16 * TPU * (g + 1))
                                pe.wait_ge(same_ready, q + 1)
                                after(pe, total_ready, q - 1)
                                nc.tensor.matmul(ps[j][:, :], same[j][:, :], h_row[a][:, k, :],
                                                 start=True, stop=True).then_inc(summed, 1)

                    rounds(pe, NG, unit)

                @block.vector
                def _(dve):
                    for a in range(2):
                        nc.vector.memset(h_row[a][:, :, F:F + 1], 1.0).then_inc(ones_ready, 1)

                    def unit(g):
                        for a in range(2):
                            u = 2 * g + a
                            chain = Chain(dve, vector_step, 3 * u)
                            dve.wait_ge(staged, u + 1)
                            for k in range(TPU):
                                q, j = TPU * u + k, (TPU * a + k) % 2
                                dve.wait_ge(nodes_spread, q + 1)
                                after(dve, summed, q - 1)
                                nc.vector.scalar_tensor_tensor(
                                    out=scrap[j][:, :], in0=pn[j][:, :], scalar=node[a][:, k:k + 1],
                                    in1=earlier[:, :], op0=ALU.is_equal, op1=ALU.mult,
                                    accum_out=before[a][:, k:k + 1])
                                nc.vector.tensor_scalar(
                                    same[j][:, :], pn[j][:, :], node[a][:, k:k + 1],
                                    share[a][:, k:k + 1], ALU.is_equal, ALU.mult)\
                                    .then_inc(same_ready, 1)
                            dve.wait_ge(same_ready, TPU * (u + 1))
                            chain.link(nc.vector.tensor_scalar(to_trash[:, :], node[a][:, :], -1.0,
                                                               trash[:, 0:1], ALU.mult, ALU.add))
                            chain.link(nc.vector.scalar_tensor_tensor(
                                out=moved[:, :], in0=before[a][:, :], scalar=0.5, in1=to_trash[:, :],
                                op0=ALU.is_gt, op1=ALU.mult))
                            for k in range(TPU):
                                after(dve, added[k], 16 * (u - 1))
                            chain.link(nc.vector.tensor_tensor(at_src[a][:, :], moved[:, :],
                                                               node[a][:, :], ALU.add))
                            dve.nop().then_inc(at_ready, 1)

                    rounds(dve, NG, unit)

                @block.gpsimd
                def _(pool):
                    pool.wait_ge(ones_ready, 2)

                    def gather(g, a):
                        u = 2 * g + a
                        gate(pool, index_ready, u + 1, pool_passed)
                        gate(pool, summed, TPU * (u - 1), pool_passed)
                        for k in range(TPU):
                            pool.indirect_dma_start(
                                h_row[a][:, k, 0:F], None, h1_table,
                                bass.IndirectOffsetOnAxis(ap=at_dst[a][:, k:k + 1], axis=0),
                            ).then_inc(rows_in[a], 16)

                    def scatter(g):
                        for a in range(2):
                            gather(g, a)
                        for a in range(2):
                            u = 2 * g + a
                            gate(pool, at_ready, u + 1, pool_passed)
                            for k in range(TPU):
                                gate(pool, total_ready, TPU * u + k + 1, pool_passed)
                                gate(pool, added[k], 16 * u, pool_passed)
                                pool.indirect_dma_start(
                                    sums[k], bass.IndirectOffsetOnAxis(ap=at_src[a][:, k:k + 1], axis=0),
                                    total[k][:, :], None, compute_op=ALU.add).then_inc(added[k], 16)

                    rounds(pool, NG, scatter)
                    for k in range(TPU):
                        pool.wait_ge(added[k], 16 * NU)

        with ExitStack() as ctx:
            part = [tensor(ctx, f"part{h}", [P, SPLITS, 4, F + 1]) for h in range(2)]
            x1 = [tensor(ctx, f"x1_in{h}", [P, 4, F]) for h in range(2)]
            low = tensor(ctx, "low", [P, 4])
            degree = tensor(ctx, "degree", [P, 4])
            y = [tensor(ctx, f"y_out{h}", [P, 4, F]) for h in range(2)]
            ystat = tensor(ctx, "ystat_out", [P, 4, 6])
            ymom = [tensor(ctx, f"ymom_out{h}", [P, 4, 2]) for h in range(2)]
            ydev = [tensor(ctx, f"ydev_out{h}", [P, 4]) for h in range(2)]
            result = [tensor(ctx, f"result{h}", [P, 4, F]) for h in range(2)]
            loaded = [sem(ctx, f"f_loaded{h}") for h in range(2)]
            stored = [sem(ctx, f"f_stored{h}") for h in range(2)]
            paired, used = sem(ctx, "f_paired"), sem(ctx, "f_used")
            dev, rooted, ready = sem(ctx, "f_dev"), sem(ctx, "f_root"), sem(ctx, "f_ready")
            sum_step, norm_step = sem(ctx, "f_sum_step"), sem(ctx, "f_norm_step")
            block = ctx.enter_context(nc.Block())

            @block.sync
            def _(sp):
                def load(q):
                    if missing(q):
                        return
                    after(sp, used, q.c - 1)
                    for t, k, n in stretches(q):
                        for j in range(SPLITS):
                            sp.dma_start(part[q.h][0:n, j, t:t + k, :], quad_rows(sums[j], q, t, k, n))\
                                .then_inc(loaded[q.h], 16)
                        sp.dma_start(x1[q.h][0:n, t:t + k, :], quad_rows(x1_rows, q, t, k, n))\
                            .then_inc(loaded[q.h], 16)

                quads(sp, load)

            @block.gpsimd
            def _(pool):
                def add_pair(q):
                    if missing(q):
                        return
                    pool.wait_ge(loaded[q.h], (SPLITS + 1) * landed(q))
                    for t, k, n in stretches(q):
                        last = nc.gpsimd.tensor_tensor(
                            part[q.h][0:n, SPLITS - 2, t:t + k, :], part[q.h][0:n, SPLITS - 2, t:t + k, :],
                            part[q.h][0:n, SPLITS - 1, t:t + k, :], ALU.add)
                    last.then_inc(paired, 1)

                quads(pool, add_pair)

            @block.scalar
            def _(act):
                def root(q):
                    if missing(q):
                        return
                    act.wait_ge(dev, q.c + 1)
                    for t, k, n in stretches(q):
                        last = nc.scalar.activation(ydev[q.h][0:n, t:t + k], ydev[q.h][0:n, t:t + k],
                                                    ACT.Sqrt)
                    last.then_inc(rooted, 1)

                def store(q):
                    if missing(q):
                        return
                    act.wait_ge(ready, q.c + 1)
                    for t, k, n in stretches(q):
                        act.dma_start(quad_rows(out, q, t, k, n), result[q.h][0:n, t:t + k, :])\
                            .then_inc(stored[q.h], 16)

                def body(q):
                    root(q)
                    store(q.back(1))

                quads(act, body)
                for q in (Quad(NQ - 2, (NQ - 2) % 2), Quad(NQ - 1, (NQ - 1) % 2)):
                    act.wait_ge(stored[q.h], landed(q))

            @block.vector
            def _(dve):
                STEPS = SPLITS - 2 + 6

                def sum_up(q):
                    if missing(q):
                        return
                    chain = Chain(dve, sum_step, STEPS * q.c)
                    whole = part[q.h][:, 0, :, :]
                    dve.wait_ge(loaded[q.h], (SPLITS + 1) * landed(q))
                    for j in range(1, SPLITS - 1):
                        if j == SPLITS - 2:
                            dve.wait_ge(paired, q.c + 1)
                        for t, k, n in stretches(q):
                            last = nc.vector.tensor_tensor(whole[0:n, t:t + k, :], whole[0:n, t:t + k, :],
                                                           part[q.h][0:n, j, t:t + k, :], ALU.add)
                        chain.link(last)
                    for t, k, n in stretches(q):
                        last = nc.vector.tensor_scalar(low[0:n, t:t + k], whole[0:n, t:t + k, F], 0.5,
                                                       None, ALU.is_lt)
                    chain.link(last)
                    for t, k, n in stretches(q):
                        last = nc.vector.tensor_tensor(degree[0:n, t:t + k], whole[0:n, t:t + k, F],
                                                       low[0:n, t:t + k], ALU.add)
                    chain.link(last)
                    for t, k, n in stretches(q):
                        last = nc.vector.reciprocal(degree[0:n, t:t + k], degree[0:n, t:t + k])
                    chain.link(last)
                    for t, n in enumerate(sizes(q)):
                        last = nc.vector.scalar_tensor_tensor(
                            out=y[q.h][0:n, t, :], in0=whole[0:n, t, 0:F], scalar=degree[0:n, t:t + 1],
                            in1=x1[q.h][0:n, t, :], op0=ALU.mult, op1=ALU.add)
                    chain.link(last)
                    dve.nop().then_inc(used, 1)
                    for t, n in enumerate(sizes(q)):
                        last = nc.vector.bn_stats(ystat[0:n, t, :], y[q.h][0:n, t, :])
                    chain.link(last)
                    dve.sem_inc(vector_passed, 1)
                    for t, n in enumerate(sizes(q)):
                        last = nc.vector.bn_aggr(ymom[q.h][0:n, t, :], ystat[0:n, t, :])
                    chain.link(last)
                    for t, k, n in stretches(q):
                        last = nc.vector.tensor_scalar(ydev[q.h][0:n, t:t + k], ymom[q.h][0:n, t:t + k, 1],
                                                       EPS, None, ALU.add)
                    last.then_inc(dev, 1)
                    assert chain.n == STEPS

                def norm(q):
                    if missing(q):
                        return
                    chain = Chain(dve, norm_step, q.c)
                    dve.wait_ge(rooted, q.c + 1)
                    for t, k, n in stretches(q):
                        last = nc.vector.reciprocal(ydev[q.h][0:n, t:t + k], ydev[q.h][0:n, t:t + k])
                    chain.link(last)
                    if not (isinstance(q.c, int) and q.c < 2):
                        dve.wait_ge(stored[q.h], landed(q.back(2)))
                    for t, n in enumerate(sizes(q)):
                        last = nc.vector.tensor_scalar(result[q.h][0:n, t, :], y[q.h][0:n, t, :],
                                                       ymom[q.h][0:n, t, 0:1], ydev[q.h][0:n, t:t + 1],
                                                       ALU.subtract, ALU.mult)
                    last.then_inc(ready, 1)

                def body(q):
                    sum_up(q)
                    norm(q.back(1))

                quads(dve, body)


_INS = ["x", "src", "dst", "edge_weight", "L0_gnn_W_ft", "L0_gnn_b_ft", "L0_gnn_W_conv",
        "L0_gnn_b_conv", "L0_gnn_velocity_factor", "L0_gnn_velocity_params", "L0_gnn_attention",
        "L0_gnn_bn_scale", "L0_gnn_bn_bias", "L0_gnn_W1", "L0_gnn_b1", "L0_gnn_ln_scale",
        "L0_gnn_ln_bias", "L0_gnn_W2", "L0_gnn_b2", "L1_gnn_W", "L1_gnn_b"]


def kernel(**inputs):
    import numpy as _np
    import concourse.bacc as _bacc
    from concourse import mybir as _mybir
    from concourse.bass_utils import run_bass_kernel_spmd as _run

    nc = _bacc.Bacc("TRN2", target_bir_lowering=False, num_devices=1)
    arrays, args = {}, []
    for name in _INS:
        a = _np.ascontiguousarray(inputs[name])
        if a.ndim == 0:
            a = a.reshape(1)
        arrays[f"in_{name}"] = a
        args.append(nc.dram_tensor(f"in_{name}", a.shape, _mybir.dt.from_np(a.dtype),
                                   kind="ExternalInput").ap())
    shape = arrays["in_x"].shape
    args.append(nc.dram_tensor("out_x", shape, _mybir.dt.float32, kind="ExternalOutput").ap())
    resnorm_gnn(nc, *args)
    r = _run(nc, [arrays], core_ids=[0])
    return r.results[0]["out_x"]
```
